# Optimizing a Trainium2 kernel written in Bass

```python
import numpy as np
import jax
import jax.numpy as jnp

def _softmax(x, axis=-1):
    return jax.nn.softmax(x, axis=axis)

def _gelu(x):
    return jax.nn.gelu(x, approximate=True)

def _silu(x):
    return jax.nn.silu(x)

def _sigmoid(x):
    return jax.nn.sigmoid(x)

def _layernorm(x, axis=-1, eps=1e-05):
    m = jnp.mean(x, axis=axis, keepdims=True)
    v = jnp.var(x, axis=axis, keepdims=True)
    return (x - m) / jnp.sqrt(v + eps)

def _scatter_add(tgt, idx, src, axis=0):
    return tgt.at[idx].add(src)

def _segment_sum(src, seg, n):
    return jax.ops.segment_sum(src, seg, n)
kernel_name = 'mk_gnn_ffn_d2_gnn_r8_97b356'

def setup_inputs(seed: int=0):
    np.random.seed(seed)
    _w = jnp.asarray

    def _rec_inputs():
        import jax
        import jax.numpy as jnp
        _gk = jax.random.key(seed)
        x = -0.0003713 + 1 * jax.random.normal(jax.random.fold_in(_gk, 1), (12500, 256), jnp.float32)
        _s = jax.random.randint(jax.random.fold_in(_gk, 2), (100000,), 0, 12500, jnp.int32)
        _d = jax.random.randint(jax.random.fold_in(_gk, 3), (100000,), 0, 12500, jnp.int32)
        _loop = jnp.arange(12500, dtype=jnp.int32)
        src = jnp.concatenate([_s, _d, _loop])
        dst = jnp.concatenate([_d, _s, _loop])
        _o = jnp.argsort(dst, stable=True)
        src = src[_o]
        dst = dst[_o]
        edge_weight = jax.random.uniform(jax.random.fold_in(_gk, 13), (212500,), jnp.float32, 0.0, 1)
        return (x, src, dst, edge_weight)
    x, src, dst, edge_weight = _rec_inputs()

    def _L0_gnn_setup():
        import jax, jax.numpy as jnp
        import numpy as np
        N_NODES = 6250
        N_EDGES = 100000
        DIM = 256
        key = jax.random.key(seed)
        k1, k2, k3, k4, k5 = jax.random.split(key, 5)
        x = jax.random.normal(k1, (N_NODES, DIM), dtype=jnp.float32)
        edge_index = jax.random.randint(k2, (2, N_EDGES), 0, N_NODES, dtype=jnp.int64)
        W1 = jax.random.normal(k3, (DIM, DIM), dtype=jnp.float32) / np.sqrt(DIM)
        W2 = jax.random.normal(k4, (DIM, DIM), dtype=jnp.float32) / np.sqrt(DIM)
        return {'x': x, 'edge_index': edge_index, 'W1': W1, 'W2': W2}
    _L0_gnn_all = _L0_gnn_setup()
    _L0_gnn_in = {k: v for k, v in _L0_gnn_all.items() if k in ('W1', 'W2')}
    del _L0_gnn_all

    def _L0_ffn_setup():
        import jax, jax.numpy as jnp
        import numpy as np
        E = 8
        K = 2
        D = 256
        H = 512
        DOUT = 256
        EPS = 1e-05
        key = jax.random.key(seed)
        ks = jax.random.split(key, 9)
        s = 0.02
        return {'x': jax.random.normal(ks[0], (4, 1024, D), jnp.float32), 'gamma': 1.0 + 0.05 * jax.random.normal(ks[1], (D,), jnp.float32), 'beta': 0.05 * jax.random.normal(ks[2], (D,), jnp.float32), 'Wr': 0.01 * jax.random.normal(ks[3], (D, E), jnp.float32), 'br': jnp.zeros((E,), jnp.float32), 'W1': s * jax.random.normal(ks[4], (E, D, H), jnp.float32), 'b1': s * jax.random.normal(ks[5], (E, H), jnp.float32), 'W2': s * jax.random.normal(ks[6], (E, H, DOUT), jnp.float32), 'b2': s * jax.random.normal(ks[7], (E, DOUT), jnp.float32)}
    _L0_ffn_all = _L0_ffn_setup()
    _L0_ffn_in = {k: v for k, v in _L0_ffn_all.items() if k in ('gamma', 'beta', 'Wr', 'br', 'W1', 'b1', 'W2', 'b2')}
    del _L0_ffn_all

    def _L1_gnn_setup():
        import jax, jax.numpy as jnp
        import numpy as np
        MU = 2.0
        key = jax.random.key(seed)
        ks = jax.random.split(key, 8)
        N, E, IN, P, OUT = (12500, 200000, 256, 128, 256)
        x = jax.random.normal(ks[0], (N, IN), dtype=jnp.float32)
        edge_vals = jnp.ones((E,), dtype=jnp.float32)
        Wp = jax.random.normal(ks[1], (P, IN), dtype=jnp.float32) * (1.0 / np.sqrt(IN))
        bp = jnp.zeros((P,), dtype=jnp.float32)
        W1 = jax.random.normal(ks[2], (OUT, P), dtype=jnp.float32) * (1.0 / np.sqrt(P))
        b1 = jnp.zeros((OUT,), dtype=jnp.float32)
        W2 = jax.random.normal(ks[3], (OUT, P), dtype=jnp.float32) * (1.0 / np.sqrt(P))
        b2 = jnp.zeros((OUT,), dtype=jnp.float32)
        src = jax.random.randint(ks[4], (E,), 0, N, dtype=jnp.int32)
        dst = jax.random.randint(ks[5], (E,), 0, N, dtype=jnp.int32)
        return {'x': x, 'edge_vals': edge_vals, 'Wp': Wp, 'bp': bp, 'W1': W1, 'b1': b1, 'W2': W2, 'b2': b2, 'src': src, 'dst': dst}
    _L1_gnn_all = _L1_gnn_setup()
    _L1_gnn_in = {k: v for k, v in _L1_gnn_all.items() if k in ('Wp', 'bp', 'W1', 'b1', 'W2', 'b2')}
    del _L1_gnn_all

    def _L1_ffn_setup():
        import jax, jax.numpy as jnp
        import numpy as np
        B, S, D = (8, 512, 256)
        H = 4 * D
        CAPACITY = 0.5
        key = jax.random.key(seed)
        ks = jax.random.split(key, 6)
        x = jax.random.normal(ks[0], (B, S, D), dtype=jnp.float32)
        attention_mask = jnp.zeros((B, 1, 1, S), dtype=jnp.float32)
        wr = jax.random.normal(ks[1], (D, 1), dtype=jnp.float32) * 0.02
        br = jnp.zeros((1,), dtype=jnp.float32)
        w1 = jax.random.normal(ks[2], (D, H), dtype=jnp.float32) * 0.02
        b1 = jnp.zeros((H,), dtype=jnp.float32)
        w2 = jax.random.normal(ks[3], (H, D), dtype=jnp.float32) * 0.02
        b2 = jnp.zeros((D,), dtype=jnp.float32)
        return {'x': x, 'attention_mask': attention_mask, 'wr': wr, 'br': br, 'w1': w1, 'b1': b1, 'w2': w2, 'b2': b2}
    _L1_ffn_all = _L1_ffn_setup()
    _L1_ffn_in = {k: v for k, v in _L1_ffn_all.items() if k in ('attention_mask', 'wr', 'br', 'w1', 'b1', 'w2', 'b2')}
    del _L1_ffn_all
    return {'x': x, 'src': src, 'dst': dst, 'edge_weight': edge_weight, 'L0_gnn_W1': _L0_gnn_in['W1'], 'L0_gnn_W2': _L0_gnn_in['W2'], 'L0_ffn_gamma': _L0_ffn_in['gamma'], 'L0_ffn_beta': _L0_ffn_in['beta'], 'L0_ffn_Wr': _L0_ffn_in['Wr'], 'L0_ffn_br': _L0_ffn_in['br'], 'L0_ffn_W1': _L0_ffn_in['W1'], 'L0_ffn_b1': _L0_ffn_in['b1'], 'L0_ffn_W2': _L0_ffn_in['W2'], 'L0_ffn_b2': _L0_ffn_in['b2'], 'L1_gnn_Wp': _L1_gnn_in['Wp'], 'L1_gnn_bp': _L1_gnn_in['bp'], 'L1_gnn_W1': _L1_gnn_in['W1'], 'L1_gnn_b1': _L1_gnn_in['b1'], 'L1_gnn_W2': _L1_gnn_in['W2'], 'L1_gnn_b2': _L1_gnn_in['b2'], 'L1_ffn_attention_mask': _L1_ffn_in['attention_mask'], 'L1_ffn_wr': _L1_ffn_in['wr'], 'L1_ffn_br': _L1_ffn_in['br'], 'L1_ffn_w1': _L1_ffn_in['w1'], 'L1_ffn_b1': _L1_ffn_in['b1'], 'L1_ffn_w2': _L1_ffn_in['w2'], 'L1_ffn_b2': _L1_ffn_in['b2']}

def reference(x, src, dst, edge_weight, L0_gnn_W1, L0_gnn_W2, L0_ffn_gamma, L0_ffn_beta, L0_ffn_Wr, L0_ffn_br, L0_ffn_W1, L0_ffn_b1, L0_ffn_W2, L0_ffn_b2, L1_gnn_Wp, L1_gnn_bp, L1_gnn_W1, L1_gnn_b1, L1_gnn_W2, L1_gnn_b2, L1_ffn_attention_mask, L1_ffn_wr, L1_ffn_br, L1_ffn_w1, L1_ffn_b1, L1_ffn_w2, L1_ffn_b2):
    import jax
    import jax.numpy as jnp

    def _L0_gnn_ref(x, edge_index, W1, W2):
        import jax, jax.numpy as jnp
        import numpy as np
        N_NODES = 6250
        N_EDGES = 100000
        DIM = 256
        self_part = x @ W1.T
        proj = x @ W2.T
        src, dst = (edge_index[0], edge_index[1])
        source_feats = proj[src]
        neighbor_part = jax.ops.segment_sum(source_feats, dst, num_segments=x.shape[0])
        return jax.nn.relu(self_part + neighbor_part)

    def _L0_ffn_ref(x, gamma, beta, Wr, br, W1, b1, W2, b2):
        import jax, jax.numpy as jnp
        import numpy as np
        E = 8
        K = 2
        D = 256
        H = 512
        DOUT = 256
        EPS = 1e-05
        mu = jnp.mean(x, axis=-1, keepdims=True)
        var = jnp.mean(jnp.square(x - mu), axis=-1, keepdims=True)
        xn = (x - mu) * jax.lax.rsqrt(var + EPS) * gamma + beta
        logits = jnp.einsum('bsd,de->bse', xn, Wr) + br
        top_vals, top_idx = jax.lax.top_k(logits, K)
        w = jax.nn.softmax(top_vals, axis=-1)
        w_full = jnp.einsum('bsk,bske->bse', w, jax.nn.one_hot(top_idx, E, dtype=w.dtype))
        y = jnp.zeros(x.shape[:-1] + (DOUT,), x.dtype)
        for e in range(E):
            h = jax.nn.gelu(jnp.einsum('bsd,dh->bsh', xn, W1[e]) + b1[e], approximate=False)
            y_e = jnp.einsum('bsh,hd->bsd', h, W2[e]) + b2[e]
            y = y + y_e * w_full[..., e, None]
        return y

    def _L1_gnn_ref(x, edge_vals, Wp, bp, W1, b1, W2, b2, src, dst):
        import jax, jax.numpy as jnp
        import numpy as np
        MU = 2.0
        N = x.shape[0]
        h = jax.nn.relu(x @ Wp.T + bp)
        hp = h ** MU
        msgs = edge_vals[:, None] * hp[src]
        agg = jax.ops.segment_sum(msgs, dst, num_segments=N)
        agg = agg ** (1.0 / MU)
        return h @ W1.T + b1 + agg @ W2.T + b2

    def _L1_ffn_ref(x, attention_mask, wr, br, w1, b1, w2, b2):
        import jax, jax.numpy as jnp
        import numpy as np
        B, S, D = (8, 512, 256)
        H = 4 * D
        CAPACITY = 0.5
        b, s, d = x.shape
        weights = (jnp.einsum('bsd,do->bso', x, wr) + br)[..., 0]
        k = max(1, int(CAPACITY * s))
        kk = k - 1 if k > 1 else 1
        _, idx = jax.lax.top_k(weights, k)
        sel_idx = idx[:, :kk]
        sel = jnp.take_along_axis(x, sel_idx[:, :, None], axis=1)
        h = jax.nn.gelu(jnp.einsum('bkd,dh->bkh', sel, w1) + b1)
        y = jnp.einsum('bkh,hd->bkd', h, w2) + b2
        w_sel = jnp.take_along_axis(weights, sel_idx, axis=1)
        y = y * w_sel[..., None]
        batch_idx = jnp.arange(b)[:, None]
        processed = jnp.zeros_like(x).at[batch_idx, sel_idx].set(y)
        return processed + x
    edge_index = jnp.stack([src, dst])
    x = x + _L0_gnn_ref(_layernorm(x, axis=-1), edge_index, L0_gnn_W1, L0_gnn_W2)
    x = x + _L0_ffn_ref(_layernorm(x, axis=-1)[None], L0_ffn_gamma, L0_ffn_beta, L0_ffn_Wr, L0_ffn_br, L0_ffn_W1, L0_ffn_b1, L0_ffn_W2, L0_ffn_b2)[0]
    x = x + _L1_gnn_ref(_layernorm(x, axis=-1), edge_weight, L1_gnn_Wp, L1_gnn_bp, L1_gnn_W1, L1_gnn_b1, L1_gnn_W2, L1_gnn_b2, src, dst)
    x = x + _L1_ffn_ref(_layernorm(x, axis=-1)[None], L1_ffn_attention_mask, L1_ffn_wr, L1_ffn_br, L1_ffn_w1, L1_ffn_b1, L1_ffn_w2, L1_ffn_b2)[0]
    return x

_drawn_inputs = setup_inputs


def setup_inputs(seed=0):
    import zlib

    import numpy as np

    out = dict(_drawn_inputs(seed))
    spreads = {'L0_ffn_br': (0.0, 0.485),
     'L1_gnn_bp': (0.0, 0.1),
     'L1_gnn_b1': (0.0, 0.298),
     'L1_gnn_b2': (0.0, 0.268),
     'L1_ffn_b1': (0.0, 0.8),
     'L1_ffn_b2': (0.0, 0.8)}
    factors = {'L0_ffn_gamma': 8.0,
     'L0_ffn_beta': 8.0,
     'L0_ffn_Wr': 4.814,
     'L0_ffn_W1': 3.499,
     'L0_ffn_b1': 8.0,
     'L0_ffn_W2': 3.376,
     'L0_ffn_b2': 8.0,
     'L1_ffn_wr': 8.0,
     'L1_ffn_w1': 8.0,
     'L1_ffn_w2': 8.0}
    for name, (base, spread) in spreads.items():
        noise = np.random.default_rng([zlib.crc32(name.encode()), seed]).standard_normal(out[name].shape)
        drawn = base * np.exp(spread * noise) if base else spread * noise
        out[name] = jnp.asarray(drawn.astype(out[name].dtype))
    for name, factor in factors.items():
        out[name] = (out[name] * factor).astype(out[name].dtype)
    return out
```

```python
import numpy as np
import concourse.bass as bass
from concourse import mybir
from contextlib import ExitStack

f32 = mybir.dt.float32
i32 = mybir.dt.int32
bf16 = mybir.dt.bfloat16
ALU = mybir.AluOpType
ACT = mybir.ActivationFunctionType
AX = mybir.AxisListType

P = 128
N = 12500
E = 212500
D = 256
NB = -(-N // P)
TAIL = N - (NB - 1) * P
CC = 13
ER = P * CC
WROWS = 20
KD = D // P
NE, H0 = 8, 512
HT0 = H0 // P
PJ = 128
H1 = 1024
HT1 = H1 // P
KEEP = int(0.5 * N) - 1
EPS = 1e-5
GRP = 2
GW = WROWS // GRP
GT = 5
CH = 7
NCH = NB // CH

C_B1 = 0
C_GAMMA = C_B1 + NE * HT0
C_BETA = C_GAMMA + KD
C_BP = C_BETA + KD
C_FB1 = C_BP + 1
C_WR0 = C_FB1 + HT1
C_WR1 = C_WR0 + KD * NE
NCOL = C_WR1 + KD
R_BR0 = 0
R_BR1 = R_BR0 + NE
R_GB1 = R_BR1 + 1
R_GB2 = R_GB1 + D
R_FB2 = R_GB2 + D
NROW = R_FB2 + D


class At:

    def __init__(self, i, c):
        self.i, self.c = i, c

    def __sub__(self, d):
        return At(self.i, self.c - d)

    def __add__(self, d):
        return At(self.i, self.c + d)

    @property
    def par(self):
        return self.c % 2

    def times(self, m, add=0):
        if self.i is None:
            return self.c * m + add
        return self.i * (2 * m) + (self.c * m + add)

    def uses(self, m, add=0):
        if self.i is None:
            return (self.c // 2 + 1) * m + add
        return self.i * m + ((self.c // 2 + 1) * m + add)


def after(eng, sem, at, m=1, add=0):
    if at.i is not None:
        assert at.c * m + m + add > 0
    if at.c * m + m + add > 0:
        eng.wait_ge(sem, at.times(m, m + add))


def landed(eng, sems, at, m=16):
    assert at.i is None or at.c >= 0
    if at.c >= 0:
        eng.wait_ge(sems[at.par], at.uses(m))


def gnn_kernel(nc, xpad, edges, firsts, dstrun, wmoe1, wmoe2, gw0, wp, gw1, wf1, wf2, b2e, cols, rows, out):
    ctx = ExitStack()
    with ctx:
        def sb(name, shape, dt=f32):
            return ctx.enter_context(nc.sbuf_tensor(name, shape, dt))

        def sem(name):
            return ctx.enter_context(nc.semaphore(name))

        def pair(name):
            return [sem(name + "0"), sem(name + "1")]

        t_xn = nc.dram_tensor("t_xn", [NB * P, D], f32).ap()
        t_x1 = nc.dram_tensor("t_x1", [NB * P, D], f32).ap()
        t_ht = nc.dram_tensor("t_ht", [NB * P, PJ], f32).ap()
        t_hp = nc.dram_tensor("t_hp", [NB * P, PJ], f32).ap()
        t_base = nc.dram_tensor("t_base", [NB * P, D], f32).ap()

        ARENA = NB * D
        arena = sb("arena", [P, ARENA])
        w1e = arena[:, 0:NE * KD * H0].rearrange("p (e k h) -> p e k h", e=NE, k=KD)
        w2e = arena[:, NE * KD * H0:NE * (KD * H0 + HT0 * D)].rearrange("p (e t d) -> p e t d", e=NE, t=HT0)
        at0 = NE * (KD * H0 + HT0 * D)
        win = arena[0:NB, at0:at0 + WROWS * 3 * P].bitcast(i32).rearrange("p (j k) -> p j k", j=WROWS)
        spot = [at0]

        def l0(*shape):
            size = int(np.prod(shape))
            spot[0] += size
            flat = arena[:, spot[0] - size:spot[0]]
            if len(shape) == 1:
                return flat
            return flat.rearrange("p (a b) -> p a b", a=shape[0])

        gw0_s = l0(KD, 2 * D)
        xnb = [l0(D), l0(D)]
        xnd = l0(D)
        xndT = l0(KD, P)
        hq = l0(P)
        yw = arena

        src_t = sb("src_t", [P, NB + 1, WROWS], i32)
        dst_t = sb("dst_t", [P, NB + 1, WROWS], bf16)
        wgt_t = sb("wgt_t", [P, NB + 1, WROWS])
        gbuf = sb("gbuf", [P, WROWS, D])
        oh = [sb(f"oh{q}", [P, WROWS, P]) for q in range(2)]
        gflat = gbuf[:, :, :].rearrange("p j d -> p (j d)")
        xin = [gflat[:, q * CH * D:(q + 1) * CH * D].rearrange("p (t d) -> p t d", t=CH) for q in range(2)]
        xno = [oh[q][:, 0:CH * D // P, :].rearrange("p j n -> p (j n)").rearrange("p (t d) -> p t d", t=CH)
               for q in range(2)]
        winf = gflat[0:NB, 0:WROWS * P].rearrange("p (j k) -> p j k", j=WROWS)
        idx = sb("idx", [P, 2, WROWS], i32)
        iota_f = sb("iota_f", [P, P])
        iota_i = sb("iota_i", [P, P], i32)
        part_i = sb("part_i", [P, 1], i32)
        part_f = sb("part_f", [P, 1])
        ident = sb("ident", [P, P])
        ones = sb("ones", [P, P])
        tri_i = sb("tri_i", [P, NE, NE], i32)
        tri = sb("tri", [P, NE, NE])
        wp_s = sb("wp_s", [P, KD, PJ])
        gw1_s = sb("gw1_s", [P, 2, D])
        wf1_s = sb("wf1_s", [P, KD, H1])
        wf2_s = sb("wf2_s", [P, HT1, D])
        b2e_s = sb("b2e_s", [NE, D])
        col = sb("col", [P, NCOL])
        row = sb("row", [P, NROW])
        xb = [sb(f"xb{q}", [P, D]) for q in range(2)]
        agg_s = sb("agg_s", [P, D])
        xaT = sb("xaT", [P, 2 * KD, P])
        x0 = [sb(f"x0_{q}", [P, D]) for q in range(2)]
        xn = sb("xn", [P, D])
        xnT = [sb(f"xnT{q}", [P, KD, P]) for q in range(2)]
        hs = [sb(f"hs{q}", [P, HT0, P]) for q in range(2)]
        acc = [sb(f"acc{q}", [P, D]) for q in range(2)]
        hT = [sb(f"hT{q}", [P, P]) for q in range(2)]
        hp_s = [sb(f"hp{q}", [P, PJ]) for q in range(2)]
        st = sb("st", [P, CH, 6])
        mv = sb("mv", [P, CH, 2])
        rs = sb("rs", [P, 2, CH])
        inv = sb("inv", [P, 2, CH])
        mvc = [sb(f"mvc{q}", [P, CH, 2]) for q in range(2)]
        sm = sb("sm", [P, 8])
        rb = sb("rb", [P, 1])
        rd = sb("rd", [P, 1])
        smd = sb("smd", [P, 2])
        std = sb("std", [P, 6])
        mvd = sb("mvd", [P, 2])
        lg = sb("lg", [P, NE])
        gt = sb("gt", [P, NE, NE])
        eq = sb("eq", [P, NE, NE])
        rank = sb("rank", [P, NE])
        ex = sb("ex", [P, NE])
        exs = sb("exs", [P, NE])
        wf = [sb(f"wf{q}", [P, NE]) for q in range(2)]
        wfT = sb("wfT", [NE, P])
        wts = sb("wts", [P, NB + 1])
        ps = [ctx.enter_context(nc.psum_tensor(f"ps{b}", [P, 512], f32)) for b in range(8)]

        wc = sb("wc", [P, 2])
        brow = sb("brow", [1, D])
        fb2row = row[0:1, R_FB2:R_FB2 + D]
        ki, kj, hi, lo, node, valid, cmpf, msk = (oh[0][:, k, 0:NB] for k in range(8))
        ki, kj = ki.bitcast(i32), kj.bitcast(i32)
        fc = sb("fc", [P, 8])
        bad = sb("bad", [P, 3])
        flag_i = sb("flag_i", [P, 1], i32)
        away = sb("away", [P, 1])
        zero = sb("zero", [P, D])
        dsts = arena[:, 0:ER + 1].bitcast(i32)
        order = arena[:, ER + 1:2 * ER + 1]
        k_cols = sb("k_cols", [P, 3], i32)
        k_f = sb("k_f", [P, 8])
        k_ix = sb("k_ix", [P, 1], i32)
        k_row, k_same, k_low, k_wgt = (oh[0][:, k, :] for k in range(4))
        k_row = k_row.bitcast(i32)
        k_got, k_out = gbuf[:, 0, :], gbuf[:, 1, :]
        t_rest = [nc.dram_tensor("t_rest0", [(NB + 1) * P, D], f32).ap(), nc.dram_tensor("t_rest1", [(NB + 1) * P, PJ], f32).ap()]
        rest = [[l0(D), l0(D)], [gbuf[:, q, PJ:2 * PJ] for q in range(2)]]
        first_i = sb("first_i", [P, CC], i32)
        first_f = sb("first_f", [P, CC])
        thr_i = sb("thr_i", [P, NB + 1], i32)
        thr_f = sb("thr_f", [P, NB + 1])
        cnt = sb("cnt", [P, NB + 1])
        r0 = sb("r0", [NB, 1])
        r1 = sb("r1", [NB, 1])
        rowi = sb("rowi", [NB, WROWS], i32)

        g_in = [sem(f"gathered{j}") for j in range(WROWS)]
        go_sp, go_gp, go_v, go_t = sem("go_sp"), sem("go_gp"), sem("go_v"), sem("go_t")
        s_dst, s_flag, s_flagp, s_zero = sem("dsts_in"), sem("flag_steps"), sem("flag_sum"), sem("zeros")
        k_zeroed, k_in, k_gather, k_v, k_sum, k_scatter = (sem("general_" + n) for n in ("zeroed", "edges_in", "gathered", "vector", "summed", "scattered"))
        k_low_ready = sem("general_low")
        s_rest = [pair("rest_in_l0_"), pair("rest_in_l1_")]
        s_par, s_first, s_w2 = sem("params"), sem("first_edges"), sem("moe_weights")
        s_iota, s_const, s_cnt, s_cntp, s_row = (sem(n) for n in ("iotas", "consts", "counted", "count_sum", "rows_of_windows"))
        s_win, s_winf, s_tp, s_tab = (sem(n) for n in ("windows", "windows_f", "window_T", "tables"))
        p_ld, p_st, p_bn, p_mv, p_rs, p_ve, p_xn = pair("p_load"), pair("p_store"), sem("p_bn"), sem("p_mv"), sem("p_rs"), sem("p_var_eps"), sem("p_xn")
        p_iv = sem("p_inverse")
        s_idx, s_oh, s_sum = sem("idx_ready"), sem("onehot_ready"), sem("window_summed")
        s_xb = pair("block_in")
        s_agg, s_T, s_aggT, s_gnn = sem("agg_ready"), sem("aggxn_T"), sem("aggT_ready"), sem("gnn_done")
        s_x0, s_bst, s_r, s_xn = (sem(n) for n in ("x0_ready", "b_stat_steps", "b_scale", "xn_ready"))
        s_iv, s_di = sem("b_inverse"), sem("d_inverse")
        s_xnTp, s_xnT, s_lgp, s_lg, s_rt, s_dl, s_ex, s_exs, s_wf = (
            sem(n) for n in ("xn_T", "xnT_ready", "logits", "lg_ready", "route_steps", "lg_less_max",
                             "exp_done", "exp_sel", "wf_ready"))
        s_wfTp, s_wfT = sem("wf_T"), sem("wfT_ready")
        s_hps, s_h, s_y, s_acc = sem("hidden_sum"), sem("hidden_ready"), sem("y_sum"), sem("acc_ready")
        s_x1st = pair("x1_stored")
        s_dst3, s_dr, s_dn, s_dTp, s_dT, s_hj, s_hT, s_hq, s_hpT, s_hp = (
            sem(n) for n in ("d_stat_steps", "d_scale", "xnd_ready", "xnd_T", "xndT_ready", "proj", "hT_ready", "hsq", "hp_T", "hp_ready"))
        s_htst, s_hpst = pair("ht_stored"), pair("hp_stored")

        u_in, u_bst = pair("l1_in"), pair("base_stored")
        u_idx, u_eq, u_oh, u_sum, u_sq, u_sqTp, u_sqT, u_gnn, u_x2, u_bst3, u_r, u_xn, u_base, u_xnTp, u_xnT, u_wp, u_wc, u_wts, u_hps, u_h, u_y, u_yw = (
            sem("l1_" + n) for n in ("idx", "eq", "onehot", "summed", "sqrt", "sqrt_T", "sqrtT_ready", "gnn", "x2_ready", "stat_steps", "scale",
                                     "xn_ready", "base_ready", "xn_T", "xnT_ready", "w_sum", "w_col", "w_kept", "hidden_sum", "hidden_ready", "y_sum", "yw_ready"))
        u_agg = sem("l1_agg_ready")
        u_iv = sem("l1_inverse")
        f_ld, f_st = pair("base_in"), pair("out_stored")
        f_key, f_cnt, f_tot, f_g, f_step, f_c, f_set, f_mask, f_out, s_brow = (
            sem("f_" + n) for n in ("keys", "count", "total", "grow", "halve", "cand", "set_up", "mask", "out_ready", "bias_row"))

        S0 = NB + 3
        S1 = NB + 2
        FRONT0 = 6
        LOOP0 = (NB - FRONT0) // 2

        def drive(eng, body, nsteps):
            for s in range(FRONT0):
                body(At(None, s))
            with eng.Fori(0, LOOP0) as i:
                for u in range(2):
                    body(At(i, FRONT0 + u))
            for s in range(FRONT0 + 2 * LOOP0, nsteps):
                body(At(None, s))

        def has(at, d):
            if at.i is not None:
                return True
            return 0 <= at.c - d < NB

        KV = 11

        def flagged(eng):
            eng.wait_ge(s_flag, 7)
            return eng.value_load(flag_i[0:1, 0:1], min_val=0, max_val=1)

        def load_rest(sp, flag, layer, b):
            with sp.If(flag == 1):
                sp.dma_start(rest[layer][b.par], t_rest[layer][bass.ds(b.times(P), P), :]).then_inc(s_rest[layer][b.par], 16)
            with sp.Else():
                sp.sem_inc(s_rest[layer][b.par], 16)
            sp.sem_inc(go_sp)

        block = ctx.enter_context(nc.Block())

        @block.sync
        def _(sp):
            sp.dma_start(first_i[:, :], firsts).then_inc(s_first, 16)
            sp.dma_start(dsts, dstrun).then_inc(s_dst, 16)

            def load_x(n):
                sp.sem_inc(go_sp)
                sp.dma_start(xin[n.par], xpad[bass.ds(n.times(CH * P), CH * P), :].rearrange("(t p) d -> p t d", p=P)).then_inc(p_ld[n.par], 16)

            def store_xn(n):
                sp.sem_inc(go_sp)
                sp.dma_start(t_xn[bass.ds(n.times(CH * P), CH * P), :].rearrange("(t p) d -> p t d", p=P), xno[n.par]).then_inc(p_st[n.par], 16)

            load_x(At(None, 0))
            load_x(At(None, 1))
            for dst, src in ((col[:, :], cols), (row[:, :], rows[0:1, :].broadcast_to([P, NROW])),
                             (wp_s[:, :, :], wp.rearrange("(k p) n -> p k n", p=P)),
                             (gw1_s[:, :, :], gw1.rearrange("(k p) n -> p k n", p=P)),
                             (wf1_s[:, :, :], wf1.rearrange("(k p) n -> p k n", p=P)),
                             (wf2_s[:, :, :], wf2.rearrange("(k p) n -> p k n", p=P)),
                             (b2e_s[:, :], b2e)):
                sp.dma_start(dst, src).then_inc(s_par, 16)
            with sp.Fori(0, NCH // 2 - 1) as i:
                for q in range(2):
                    n = At(i, 2 + q)
                    after(sp, p_xn, n - 2, CH)
                    load_x(n)
                    store_xn(n - 2)
            for n in (At(None, NCH - 2), At(None, NCH - 1)):
                after(sp, p_xn, n, CH)
                store_xn(n)
            sp.wait_ge(s_tab, 3 * WROWS // GT)
            sp.dma_start(gw0_s, gw0.rearrange("(k p) n -> p k n", p=P)).then_inc(s_par, 16)
            sp.dma_start(w1e, wmoe1.rearrange("e (k p) h -> p e k h", p=P)).then_inc(s_w2, 16)
            sp.dma_start(w2e, wmoe2.rearrange("e (t p) d -> p e t d", p=P)).then_inc(s_w2, 16)
            for q in range(2):
                sp.wait_ge(p_st[q], 16 * (NCH // 2))

            flag = flagged(sp)

            def general(layer):
                width = (D, PJ)[layer]
                with sp.If(flag == 1):
                    sp.wait_ge(s_zero, 1)
                    with sp.Fori(0, NB + 1) as i:
                        sp.dma_start(t_rest[layer][bass.ds(i * P, P), :], zero[:, 0:width]).then_inc(k_zeroed, 16)
                    with sp.Fori(0, ER) as r:
                        with sp.If(r > 0):
                            sp.wait_ge(k_scatter, r * 16 + 16 * ER * layer)
                            sp.sem_inc(go_sp)
                        with sp.Else():
                            sp.sem_inc(go_sp)
                        for k in range(3):
                            sp.dma_start(k_cols[:, k:k + 1], edges[bass.ds(r, 1), k * P:(k + 1) * P].rearrange("a k -> k a")).then_inc(k_in, 16)
                        sp.dma_start(k_row, edges[bass.ds(r, 1), P:2 * P].broadcast_to([P, P])).then_inc(k_in, 16)
                sp.sem_inc(go_sp)

            general(0)
            sp.wait_ge(s_zero, 3)

            def body(at):
                if has(at, 0):
                    b, q = at, at.par
                    after(sp, s_x0, b - 2)
                    sp.sem_inc(go_sp)
                    after(sp, s_T, b - 2)
                    after(sp, s_agg, b - 2)
                    sp.sem_inc(go_sp)
                    sp.dma_start(xb[q][:, :], xpad[bass.ds(b.times(P), P), :]).then_inc(s_xb[q], 16)
                    sp.sem_inc(go_sp)
                    sp.dma_start(xnb[q], t_xn[bass.ds(b.times(P), P), :]).then_inc(s_xb[q], 16)
                    load_rest(sp, flag, 0, b)
                if has(at, 3):
                    b, q = at - 3, (at - 3).par
                    after(sp, s_acc, b, NE + 1)
                    sp.sem_inc(go_sp)
                    sp.dma_start(t_x1[bass.ds(b.times(P), P), :], acc[q][:, :]).then_inc(s_x1st[q], 16)
                    after(sp, s_hT, b)
                    sp.sem_inc(go_sp)
                    sp.dma_start(t_ht[bass.ds(b.times(P), P), :], hT[q][:, :]).then_inc(s_htst[q], 16)
                    after(sp, s_hp, b)
                    sp.sem_inc(go_sp)
                    sp.dma_start(t_hp[bass.ds(b.times(P), P), :], hp_s[q][:, :]).then_inc(s_hpst[q], 16)
            drive(sp, body, S0)
            for q in range(2):
                for s in (s_x1st, s_htst, s_hpst):
                    sp.wait_ge(s[q], 16 * (NB // 2))

            sp.wait_ge(s_sum, NB * WROWS)
            general(1)
            sp.wait_ge(s_zero, 5)

            def body1(at):
                if has(at, 0):
                    b, q = at, at.par
                    after(sp, u_x2, b - 2)
                    sp.sem_inc(go_sp)
                    after(sp, u_gnn, b - 2)
                    after(sp, u_agg, b - 2)
                    sp.sem_inc(go_sp)
                    sp.dma_start(xb[q][:, :], t_x1[bass.ds(b.times(P), P), :]).then_inc(u_in[q], 16)
                    sp.sem_inc(go_sp)
                    sp.dma_start(hT[q][:, :], t_ht[bass.ds(b.times(P), P), :]).then_inc(u_in[q], 16)
                    load_rest(sp, flag, 1, b)
                if has(at, 1):
                    b, q = at - 1, (at - 1).par
                    after(sp, u_base, b)
                    sp.sem_inc(go_sp)
                    sp.dma_start(t_base[bass.ds(b.times(P), P), :], acc[q][:, :]).then_inc(u_bst[q], 16)
            drive(sp, body1, S1)

            def load_base(n):
                sp.sem_inc(go_sp)
                sp.dma_start(xin[n.par], t_base[bass.ds(n.times(CH * P), CH * P), :].rearrange("(t p) d -> p t d", p=P)).then_inc(f_ld[n.par], 16)

            def store_out(n):
                sp.sem_inc(go_sp)
                sp.dma_start(out[bass.ds(n.times(CH * P), CH * P), :].rearrange("(t p) d -> p t d", p=P), xin[n.par]).then_inc(f_st[n.par], 16)

            for q in range(2):
                sp.wait_ge(u_bst[q], 16 * (NB // 2))
            sp.wait_ge(u_sum, NB * WROWS)
            load_base(At(None, 0))
            load_base(At(None, 1))
            with sp.Fori(0, NCH // 2 - 1) as i:
                for q in range(2):
                    n = At(i, 2 + q)
                    after(sp, f_out, n - 2, CH)
                    store_out(n - 2)
                    landed(sp, f_st, n - 2)
                    load_base(n)
            for n in (At(None, NCH - 2), At(None, NCH - 1)):
                after(sp, f_out, n, CH)
                store_out(n)
            for q in range(2):
                sp.wait_ge(f_st[q], 16 * (NCH // 2))

        @block.gpsimd
        def _(gp):
            gp.iota(iota_i[:, :], [[1, P]], base=0, channel_multiplier=0).then_inc(s_iota, 1)
            gp.iota(part_i[:, :], [[0, 1]], base=0, channel_multiplier=1).then_inc(s_iota, 1)
            gp.iota(thr_i[:, :], [[P, NB + 1]], base=0, channel_multiplier=0).then_inc(s_iota, 1)
            gp.iota(tri_i[:, :, :], [[-1, NE], [1, NE]], base=0, channel_multiplier=0).then_inc(s_iota, 1)
            gp.wait_ge(s_row, 3)
            for j in range(WROWS):
                gp.indirect_dma_start(win[:, j, :], None, edges, bass.IndirectOffsetOnAxis(ap=rowi[:, j:j + 1], axis=0)).then_inc(s_win, 16)
            gp.wait_ge(s_tab, 3 * WROWS // GT)
            for q in range(2):
                gp.wait_ge(p_st[q], 16 * (NCH // 2))
            flag = flagged(gp)

            def general(layer):
                table = (t_xn, t_hp)[layer]
                width = (D, PJ)[layer]
                with gp.If(flag == 1):
                    gp.wait_ge(k_zeroed, 16 * (NB + 1) * (layer + 1))
                    with gp.Fori(0, ER) as r:
                        gp.wait_ge(k_in, r * 64 + 64 * (ER * layer + 1))
                        gp.sem_inc(go_gp)
                        gp.indirect_dma_start(k_got[:, 0:width], None, table, bass.IndirectOffsetOnAxis(ap=k_cols[:, 0:1], axis=0)).then_inc(k_gather, 16)
                        gp.wait_ge(k_v, r * KV + KV * (ER * layer + 1))
                        gp.sem_inc(go_gp)
                        gp.indirect_dma_start(t_rest[layer], bass.IndirectOffsetOnAxis(ap=k_ix[:, 0:1], axis=0), k_out[:, 0:width], None,
                                              compute_op=ALU.add).then_inc(k_scatter, 16)
                        gp.wait_ge(k_scatter, r * 16 + 16 * (ER * layer + 1))
                        gp.sem_inc(go_gp)
                gp.sem_inc(go_gp)

            general(0)
            gp.tensor_copy(idx[:, 0, :], src_t[:, 0, :]).then_inc(s_idx, 1)

            def body(at):
                if not has(at, 0):
                    return
                b, q = at, at.par
                after(gp, s_idx, b)
                for j in range(WROWS):
                    if j == WROWS - 1 and (at.i is not None or at.c + 1 < NB):
                        after(gp, s_sum, b - 1, WROWS)
                        gp.tensor_copy(idx[:, 1 - q, :], src_t[:, bass.ds((b + 1).times(1), 1), :].rearrange("p a j -> p (a j)")).then_inc(s_idx, 1)
                    after(gp, s_sum, b - 1, WROWS, j + 1 - WROWS)
                    gp.sem_inc(go_gp)
                    gp.indirect_dma_start(gbuf[:, j, :], None, t_xn, bass.IndirectOffsetOnAxis(ap=idx[:, q, j:j + 1], axis=0)).then_inc(g_in[j], 16)
            drive(gp, body, S0)

            gp.wait_ge(s_idx, NB + 1)
            for q in range(2):
                gp.wait_ge(s_hpst[q], 16 * (NB // 2))
            general(1)
            gp.tensor_copy(idx[:, 0, :], src_t[:, 0, :]).then_inc(u_idx, 1)

            def body1(at):
                if not has(at, 0):
                    return
                b, q = at, at.par
                after(gp, u_idx, b)
                for j in range(WROWS):
                    if j == WROWS - 1 and (at.i is not None or at.c + 1 < NB):
                        after(gp, u_sum, b - 1, WROWS)
                        gp.tensor_copy(idx[:, 1 - q, :], src_t[:, bass.ds((b + 1).times(1), 1), :].rearrange("p a j -> p (a j)")).then_inc(u_idx, 1)
                    after(gp, u_sum, b - 1, WROWS, j + 1 - WROWS)
                    gp.sem_inc(go_gp)
                    gp.indirect_dma_start(gbuf[:, j, 0:PJ], None, t_hp, bass.IndirectOffsetOnAxis(ap=idx[:, q, j:j + 1], axis=0)).then_inc(g_in[j], 16)
            drive(gp, body1, S1)

        @block.vector
        def _(v):
            v.wait_ge(s_iota, 4)
            v.memset(ones[:, :], 1.0).then_inc(s_const, 1)
            v.memset(src_t[:, NB, :], 0).then_inc(s_const, 1)
            v.memset(dst_t[:, NB, :], -1.0).then_inc(s_const, 1)
            v.memset(wgt_t[:, NB, :], 0.0).then_inc(s_const, 1)
            v.tensor_copy(iota_f[:, :], iota_i[:, :]).then_inc(s_const, 1)
            v.tensor_copy(part_f[:, :], part_i[:, :]).then_inc(s_const, 1)
            v.tensor_copy(thr_f[:, :], thr_i[:, :]).then_inc(s_const, 1)
            v.tensor_scalar(tri[:, :, :], tri_i[:, :, :], 0.0, None, ALU.is_lt).then_inc(s_const, 1)
            v.wait_ge(s_const, 8)
            v.tensor_scalar(ident[:, :], iota_f[:, :], part_f[:, 0:1], None, ALU.is_equal).then_inc(s_const, 1)
            v.wait_ge(s_first, 16)
            v.tensor_copy(first_f[:, :], first_i[:, :]).then_inc(s_cnt, 1)
            v.wait_ge(s_cnt, 1)
            cmp = oh[0][:, 0:11, :].rearrange("p j n -> p (j n)")[:, 0:(NB + 1) * CC].rearrange("p (b c) -> p b c", c=CC)
            v.tensor_tensor(cmp, first_f[:, :].unsqueeze(1).broadcast_to([P, NB + 1, CC]),
                            thr_f[:, :].unsqueeze(2).broadcast_to([P, NB + 1, CC]), ALU.is_lt).then_inc(s_cnt, 1)
            v.wait_ge(s_cnt, 2)
            v.tensor_reduce(cnt[:, :], cmp, AX.X, ALU.add).then_inc(s_cnt, 1)
            v.wait_ge(s_cntp, 1)
            v.tensor_scalar(r0[:, :], ps[0][0:NB, 0:1], -1.0, 0.0, ALU.add, ALU.max).then_inc(s_row, 1)
            v.wait_ge(s_row, 1)
            v.tensor_scalar(r1[:, :], r0[:, :], float(ER - WROWS), None, ALU.min).then_inc(s_row, 1)
            v.wait_ge(s_row, 2)
            v.tensor_scalar(rowi[:, :], iota_f[0:NB, 0:WROWS], r1[:, 0:1], None, ALU.add).then_inc(s_row, 1)

            v.memset(bad[:, :], 0.0).then_inc(s_flag, 1)
            v.wait_ge(s_flag, 1)
            v.tensor_scalar(bad[0:NB, 0:1], r1[:, :], float(WROWS), ps[0][0:NB, 1:2], ALU.add, ALU.is_lt).then_inc(s_flag, 1)
            v.wait_ge(s_dst, 16)
            v.tensor_tensor(order, dsts[:, 0:ER], dsts[:, 1:ER + 1], ALU.is_gt).then_inc(s_flag, 1)
            v.wait_ge(s_flag, 3)
            v.tensor_reduce(bad[:, 1:2], order, AX.X, ALU.add).then_inc(s_flag, 1)
            v.wait_ge(s_flag, 4)
            v.tensor_tensor(bad[:, 2:3], bad[:, 0:1], bad[:, 1:2], ALU.add).then_inc(s_flag, 1)
            v.wait_ge(s_flagp, 1)
            v.tensor_scalar(flag_i[:, :], ps[0][:, 2:3], 0.0, None, ALU.is_gt).then_inc(s_flag, 1)
            v.tensor_scalar(away[:, :], ps[0][:, 2:3], 0.0, float(1 << 20), ALU.is_gt, ALU.mult).then_inc(s_flag, 1)
            v.memset(zero[:, :], 0.0).then_inc(s_zero, 1)

            def chunk_stats(n):
                q = n.par
                landed(v, p_ld, n)
                for t in range(CH):
                    v.bn_stats(st[:, t, :], xin[q][:, t, :]).then_inc(p_bn, 1)
                after(v, p_bn, n, CH)
                v.sem_inc(go_v)
                for t in range(CH):
                    v.bn_aggr(mvc[q][:, t, :], st[:, t, :]).then_inc(p_mv, 1)
                after(v, p_mv, n, CH)
                v.tensor_scalar(rs[:, q, :], mvc[q][:, :, 1], EPS, None, ALU.add).then_inc(p_ve, 1)
                after(v, p_ve, n)
                after(v, p_rs, n - 2)
                v.reciprocal(inv[:, q, :], rs[:, q, :]).then_inc(p_iv, 1)

            def chunk_norm(n):
                q = n.par
                after(v, p_rs, n)
                landed(v, p_st, n - 2)
                for t in range(CH):
                    v.tensor_scalar(xno[q][:, t, :], xin[q][:, t, :], mvc[q][:, t, 0:1], rs[:, q, t:t + 1], ALU.subtract, ALU.mult).then_inc(p_xn, 1)

            chunk_stats(At(None, 0))
            chunk_stats(At(None, 1))
            chunk_norm(At(None, 0))
            chunk_norm(At(None, 1))
            chunk_stats(At(None, 2))
            with v.Fori(0, NCH // 2 - 2) as i:
                for q in range(2):
                    chunk_stats(At(i, 3 + q))
                    chunk_norm(At(i, 2 + q))
            chunk_stats(At(None, NCH - 1))
            chunk_norm(At(None, NCH - 2))
            chunk_norm(At(None, NCH - 1))

            v.wait_ge(s_win, 16 * WROWS)
            for q in range(2):
                v.wait_ge(p_st[q], 16 * (NCH // 2))
            blk0 = sm[0:NB, 0:1]
            v.tensor_scalar(blk0, part_f[0:NB, 0:1], float(P), None, ALU.mult).then_inc(s_winf, 1)
            v.wait_ge(s_winf, 1)
            v.tensor_scalar(oh[0][0:NB, :, :], win[:, :, P:2 * P], blk0, None, ALU.subtract).then_inc(s_winf, 1)
            v.tensor_copy(winf, win[:, :, 0:P]).then_inc(s_winf, 1)
            v.tensor_copy(oh[1][0:NB, :, :], win[:, :, 2 * P:3 * P].bitcast(f32)).then_inc(s_winf, 1)
            for g in range(3 * WROWS // GT):
                k, j0 = g // (WROWS // GT), g % (WROWS // GT) * GT
                v.wait_ge(s_tp, g + 1)
                dst = (dst_t, src_t, wgt_t)[k]
                to, of = dst[:, 0:NB, j0:j0 + GT].rearrange("p b j -> p j b"), ps[g % 8][:, 0:GT * NB].rearrange("p (j b) -> p j b", j=GT)
                if k == 0:
                    v.tensor_scalar(to, of, away[:, 0:1], None, ALU.subtract).then_inc(s_tab, 1)
                else:
                    v.tensor_copy(to, of).then_inc(s_tab, 1)

            v.wait_ge(s_par, 16 * 8)

            def onehot(b, g):
                q = b.par
                if g == 0:
                    after(v, s_sum, b - 2, WROWS)
                d = dst_t[:, bass.ds(b.times(1), 1), g * GW:(g + 1) * GW].rearrange("p a j -> p (a j)")
                v.tensor_tensor(oh[q][:, g * GW:(g + 1) * GW, :], iota_f[:, :].unsqueeze(1).broadcast_to([P, GW, P]),
                                d.unsqueeze(2).broadcast_to([P, GW, P]), ALU.is_equal).then_inc(s_oh, 1)

            v.wait_ge(s_tab, 3 * WROWS // GT)
            v.wait_ge(s_tp, 3 * WROWS // GT)
            for q in range(2):
                v.memset(rest[0][q], 0.0).then_inc(s_zero, 1)
            flag = flagged(v)

            def general(layer):
                width = (D, PJ)[layer]
                dst_f, before, ok, here, off, to, dump, wone = (k_f[:, k:k + 1] for k in range(8))
                with v.If(flag == 1):
                    v.tensor_scalar(k_low, iota_f[:, :], part_f[:, 0:1], None, ALU.is_lt).then_inc(k_low_ready, 1)
                    v.tensor_scalar(dump, part_f[:, 0:1], float(NB * P), None, ALU.add).then_inc(k_low_ready, 1)
                    v.wait_ge(k_low_ready, 2 * layer + 2)
                    with v.Fori(0, ER) as r:
                        v.wait_ge(k_in, r * 64 + 64 * (ER * layer + 1))
                        n = [0]

                        def link(ins):
                            n[0] += 1
                            ins.then_inc(k_v, 1)
                            v.wait_ge(k_v, r * KV + (KV * ER * layer + n[0]))

                        link(v.tensor_copy(dst_f, k_cols[:, 1:2]))
                        link(v.tensor_scalar(k_same, k_row, dst_f, None, ALU.is_equal))
                        link(v.tensor_tensor(k_wgt, k_same, k_low, ALU.mult))
                        link(v.tensor_reduce(before, k_wgt, AX.X, ALU.add))
                        link(v.tensor_scalar(ok, before, 0.0, None, ALU.is_equal))
                        link(v.tensor_scalar(here, dst_f, float(N), ok, ALU.is_lt, ALU.mult))
                        link(v.tensor_scalar(off, dst_f, dump, None, ALU.subtract))
                        link(v.tensor_scalar(to, off, here, dump, ALU.mult, ALU.add))
                        link(v.tensor_copy(k_ix[:, :], to))
                        if layer:
                            link(v.tensor_scalar(k_wgt, k_same, k_cols[:, 2:3].bitcast(f32), None, ALU.mult))
                        else:
                            link(v.tensor_copy(k_wgt, k_same))
                        v.wait_ge(k_sum, r + (ER * layer + 1))
                        link(v.tensor_copy(k_out[:, 0:width], ps[0][:, 0:width]))
                v.sem_inc(go_v)

            general(0)
            for g in range(GRP):
                onehot(At(None, 0), g)

            def body(at):
                A, B, C, Dd = has(at, 0), has(at, 1), has(at, 2), has(at, 3)
                nxt = at + 1
                N1 = at.i is not None or at.c + 1 < NB
                b, c, d = at - 1, at - 2, at - 3
                if B:
                    after(v, s_sum, b, WROWS)
                    after(v, s_T, b - 1)
                    landed(v, s_rest[0], b)
                    v.tensor_tensor(agg_s[:, :], ps[b.par][:, 0:D], rest[0][b.par], ALU.add).then_inc(s_agg, 1)
                if Dd:
                    after(v, s_acc, d, NE + 1)
                    v.bn_stats(std[:, :], acc[d.par][:, :]).then_inc(s_dst3, 1)
                    after(v, s_dst3, d, 3, -2)
                    v.sem_inc(go_v)
                    v.bn_aggr(mvd[:, :], std[:, :]).then_inc(s_dst3, 1)
                    after(v, s_dst3, d, 3, -1)
                    v.tensor_scalar(smd[:, 0:1], mvd[:, 1:2], EPS, None, ALU.add).then_inc(s_dst3, 1)
                    after(v, s_dst3, d, 3, 0)
                    v.reciprocal(smd[:, 1:2], smd[:, 0:1]).then_inc(s_di, 1)
                if B:
                    after(v, s_gnn, b)
                    landed(v, s_xb, b, 32)
                    after(v, s_acc, b - 2, NE + 1, -NE)
                    v.scalar_tensor_tensor(x0[b.par][:, :], ps[4][:, 0:D], 0.0, xb[b.par][:, :], ALU.max, ALU.add).then_inc(s_x0, 1)
                    after(v, s_x0, b)
                    v.bn_stats(st[:, 0, :], x0[b.par][:, :]).then_inc(s_bst, 1)
                    after(v, s_bst, b, 6, -5)
                    v.sem_inc(go_v)
                    v.bn_aggr(mv[:, 0, :], st[:, 0, :]).then_inc(s_bst, 1)
                    after(v, s_bst, b, 6, -4)
                    v.tensor_scalar(sm[:, 0:1], mv[:, 0, 1:2], EPS, None, ALU.add).then_inc(s_bst, 1)
                    after(v, s_bst, b, 6, -3)
                    v.reciprocal(sm[:, 1:2], sm[:, 0:1]).then_inc(s_bst, 1)
                    after(v, s_bst, b, 6, -2)
                    v.tensor_scalar(sm[:, 2:3], mv[:, 0, 1:2], sm[:, 1:2], EPS, ALU.mult, ALU.add).then_inc(s_bst, 1)
                    after(v, s_bst, b, 6, -1)
                    v.tensor_tensor(sm[:, 3:4], sm[:, 0:1], sm[:, 2:3], ALU.mult).then_inc(s_bst, 1)
                    after(v, s_bst, b, 6, 0)
                    v.reciprocal(sm[:, 7:8], sm[:, 3:4]).then_inc(s_iv, 1)
                if Dd:
                    after(v, s_dr, d)
                    after(v, s_dTp, d - 1)
                    v.tensor_scalar(xnd, acc[d.par][:, :], mvd[:, 0:1], rd[:, 0:1], ALU.subtract, ALU.mult).then_inc(s_dn, 1)
                if B:
                    after(v, s_r, b)
                    after(v, s_xnTp, b - 1)
                    v.tensor_scalar(xn[:, :], x0[b.par][:, :], mv[:, 0, 0:1], rb[:, 0:1], ALU.subtract, ALU.mult).then_inc(s_xn, 1)

                def accumulate(e):
                    yp = ps[(3, 7)[(e + 1) % 2]][:, 0:D]
                    after(v, s_y, c, NE + 1, e + 1 - NE)
                    if e < 0:
                        landed(v, s_x1st, c - 2)
                        v.tensor_tensor(acc[c.par][:, :], yp, x0[c.par][:, :], ALU.add).then_inc(s_acc, 1)
                    else:
                        after(v, s_acc, c, NE + 1, e - NE)
                        v.scalar_tensor_tensor(acc[c.par][:, :], yp, wf[c.par][:, e:e + 1], acc[c.par][:, :], ALU.mult, ALU.add).then_inc(s_acc, 1)

                if C:
                    accumulate(-1)
                    accumulate(0)
                    accumulate(1)
                if N1:
                    onehot(nxt, 0)
                if C:
                    accumulate(2)
                    accumulate(3)
                if B:
                    after(v, s_lgp, b)
                    v.tensor_tensor(lg[:, :], ps[4][:, D:D + NE], row[:, R_BR0:R_BR0 + NE], ALU.add).then_inc(s_lg, 1)
                    after(v, s_lg, b)
                    lj = lg[:, :].unsqueeze(1).broadcast_to([P, NE, NE])
                    le = lg[:, :].unsqueeze(2).broadcast_to([P, NE, NE])
                    v.tensor_reduce(sm[:, 4:5], lg[:, :], AX.X, ALU.max).then_inc(s_rt, 1)
                    after(v, s_rt, b, 8, -7)
                    after(v, s_ex, b - 1)
                    v.tensor_scalar(exs[:, :], lg[:, :], sm[:, 4:5], None, ALU.subtract).then_inc(s_dl, 1)
                    v.tensor_tensor(gt[:, :, :], lj, le, ALU.is_gt).then_inc(s_rt, 1)
                    v.tensor_tensor(eq[:, :, :], lj, le, ALU.is_equal).then_inc(s_rt, 1)
                    after(v, s_rt, b, 8, -5)
                    v.tensor_tensor(eq[:, :, :], eq[:, :, :], tri[:, :, :], ALU.mult).then_inc(s_rt, 1)
                    after(v, s_rt, b, 8, -4)
                    after(v, s_rt, b, 8, -6)
                    v.tensor_tensor(gt[:, :, :], gt[:, :, :], eq[:, :, :], ALU.add).then_inc(s_rt, 1)
                    after(v, s_rt, b, 8, -3)
                    v.tensor_reduce(rank[:, :], gt[:, :, :], AX.X, ALU.add).then_inc(s_rt, 1)
                if Dd:
                    after(v, s_hT, d)
                    after(v, s_hpT, d - 1)
                    v.tensor_tensor(hq, hT[d.par][:, :], hT[d.par][:, :], ALU.mult).then_inc(s_hq, 1)
                if B:
                    after(v, s_ex, b)
                    after(v, s_rt, b, 8, -2)
                    v.scalar_tensor_tensor(exs[:, :], rank[:, :], 2.0, ex[:, :], ALU.is_lt, ALU.mult).then_inc(s_exs, 1)
                    after(v, s_exs, b)
                    v.tensor_reduce(sm[:, 5:6], exs[:, :], AX.X, ALU.add).then_inc(s_rt, 1)
                    after(v, s_rt, b, 8, -1)
                    v.reciprocal(sm[:, 6:7], sm[:, 5:6]).then_inc(s_rt, 1)
                    after(v, s_rt, b, 8, 0)
                    after(v, s_acc, b - 2, NE + 1)
                    v.tensor_scalar(wf[b.par][:, :], exs[:, :], sm[:, 6:7], None, ALU.mult).then_inc(s_wf, 1)
                if C:
                    accumulate(4)
                    accumulate(5)
                if N1:
                    onehot(nxt, 1)
                if C:
                    accumulate(6)
                    accumulate(7)
            drive(v, body, S0)

            v.tensor_tensor(brow[:, :], row[0:1, R_GB1:R_GB1 + D], row[0:1, R_GB2:R_GB2 + D], ALU.add).then_inc(s_brow, 1)

            def onehot1(b, g):
                q = b.par
                if g == 0:
                    after(v, u_sum, b - 2, WROWS)
                d = dst_t[:, bass.ds(b.times(1), 1), g * GW:(g + 1) * GW].rearrange("p a j -> p (a j)")
                w = wgt_t[:, bass.ds(b.times(1), 1), g * GW:(g + 1) * GW].rearrange("p a j -> p (a j)")
                o = oh[q][:, g * GW:(g + 1) * GW, :]
                v.tensor_tensor(o, iota_f[:, :].unsqueeze(1).broadcast_to([P, GW, P]), d.unsqueeze(2).broadcast_to([P, GW, P]), ALU.is_equal).then_inc(u_eq, 1)
                after(v, u_eq, b, GRP, g + 1 - GRP)
                v.tensor_tensor(o, o, w.unsqueeze(2).broadcast_to([P, GW, P]), ALU.mult).then_inc(u_oh, 1)

            v.wait_ge(s_sum, NB * WROWS)
            v.wait_ge(s_oh, GRP * (NB + 1))
            v.wait_ge(s_hp, NB)
            general(1)
            for q in range(2):
                v.memset(rest[1][q], 0.0).then_inc(s_zero, 1)
            v.wait_ge(s_zero, 5)
            for g in range(GRP):
                onehot1(At(None, 0), g)

            def body1(at):
                B, C = has(at, 1), has(at, 2)
                N1 = at.i is not None or at.c + 1 < NB
                b, c = at - 1, at - 2
                if B:
                    after(v, u_sum, b, WROWS)
                    after(v, u_sqTp, b - 1)
                    landed(v, s_rest[1], b)
                    v.tensor_tensor(agg_s[:, 0:PJ], ps[b.par][:, 0:PJ], rest[1][b.par], ALU.add).then_inc(u_agg, 1)
                if N1:
                    onehot1(at + 1, 0)
                if B:
                    after(v, u_gnn, b)
                    landed(v, u_in, b, 32)
                    v.tensor_tensor(x0[b.par][:, :], ps[4][:, 0:D], xb[b.par][:, :], ALU.add).then_inc(u_x2, 1)
                    after(v, u_x2, b)
                    v.bn_stats(st[:, 0, :], x0[b.par][:, :]).then_inc(u_bst3, 1)
                    after(v, u_bst3, b, 3, -2)
                    v.sem_inc(go_v)
                    v.bn_aggr(mv[:, 0, :], st[:, 0, :]).then_inc(u_bst3, 1)
                    after(v, u_bst3, b, 3, -1)
                    v.tensor_scalar(sm[:, 0:1], mv[:, 0, 1:2], EPS, None, ALU.add).then_inc(u_bst3, 1)
                    after(v, u_bst3, b, 3, 0)
                    v.reciprocal(sm[:, 1:2], sm[:, 0:1]).then_inc(u_iv, 1)
                    after(v, u_r, b)
                    after(v, u_xnTp, b - 1)
                    v.tensor_scalar(xn[:, :], x0[b.par][:, :], mv[:, 0, 0:1], rb[:, 0:1], ALU.subtract, ALU.mult).then_inc(u_xn, 1)
                    after(v, u_xn, b)
                    landed(v, u_bst, b - 2)
                    v.tensor_tensor(acc[b.par][:, :], x0[b.par][:, :], xn[:, :], ALU.add).then_inc(u_base, 1)
                if N1:
                    onehot1(at + 1, 1)
                if C:
                    after(v, u_y, c)
                    after(v, u_wc, c)
                    v.tensor_scalar(yw[:, bass.ds(c.times(D), D)], ps[(3, 7)[c.par]][:, 0:D], wc[:, c.par:c.par + 1], None, ALU.mult).then_inc(u_yw, 1)
                if B:
                    after(v, u_wp, b)
                    after(v, u_yw, b - 2)
                    after(v, u_wts, b - 2)
                    v.tensor_tensor(wc[:, b.par:b.par + 1], ps[4][:, D:D + 1], row[:, R_BR1:R_BR1 + 1], ALU.add).then_inc(u_wc, 1)
                    after(v, u_wc, b)
                    v.tensor_copy(wts[:, bass.ds(b.times(1), 1)], wc[:, b.par:b.par + 1]).then_inc(u_wts, 1)
            drive(v, body1, S1)

            nf = [0]

            def link(ins):
                nf[0] += 1
                ins.then_inc(f_key, 1)
                v.wait_ge(f_key, nf[0])

            v.wait_ge(u_wts, NB)
            v.wait_ge(s_const, 9)
            link(v.tensor_scalar(node, thr_f[:, 0:NB], part_f[:, 0:1], None, ALU.add))
            link(v.tensor_scalar(valid, node, float(N), None, ALU.is_lt))
            link(v.tensor_scalar(cmpf, wts[:, 0:NB], 0.0, None, ALU.add))
            bits = cmpf.bitcast(i32)
            link(v.tensor_scalar(ki, bits, 31, 0x7fffffff, ALU.arith_shift_right, ALU.bitwise_and))
            link(v.tensor_tensor(kj, ki, bits, ALU.bitwise_xor))
            link(v.tensor_scalar(ki, kj, 16, None, ALU.arith_shift_right))
            link(v.tensor_copy(hi, ki))
            link(v.tensor_scalar(ki, kj, 0xffff, None, ALU.bitwise_and))
            link(v.tensor_copy(lo, ki))
            LOW = 65536.0
            link(v.scalar_tensor_tensor(hi, hi, LOW, valid, ALU.add, ALU.mult))
            link(v.tensor_scalar(hi, hi, LOW, None, ALU.subtract))
            cand, step, grow, count, want, hstar, lstar, nstar = (fc[:, k:k + 1] for k in range(8))
            link(v.memset(want, float(KEEP)))
            done = [0]

            def search(key, base, bits_, star):
                link(v.memset(cand, base + 2.0 ** (bits_ - 1)))
                link(v.memset(step, 2.0 ** (bits_ - 1)))
                n0 = done[0]
                with v.Fori(0, bits_) as i:
                    v.tensor_scalar(cmpf, key, cand, 0.0, ALU.is_ge, ALU.add, accum_out=count).then_inc(f_cnt, 1)
                    v.wait_ge(f_tot, i + (n0 + 1))
                    v.tensor_scalar(grow, ps[0][:, 0:1], want, step, ALU.is_ge, ALU.mult).then_inc(f_g, 1)
                    v.wait_ge(f_g, i + (n0 + 1 - extra[0]))
                    v.tensor_scalar(step, step, 0.5, None, ALU.mult).then_inc(f_step, 1)
                    v.wait_ge(f_step, i + (n0 + 1 - extra[0]))
                    v.tensor_scalar(cand, grow, cand, step, ALU.add, ALU.subtract).then_inc(f_c, 1)
                    v.wait_ge(f_c, i + (n0 + 1 - extra[0]))
                done[0] += bits_
                link(v.tensor_scalar(star, cand, -0.5, None, ALU.add))

            extra = [0]

            def wanted_less_above(key, star):
                v.tensor_scalar(cmpf, key, star, 0.0, ALU.is_gt, ALU.add, accum_out=count).then_inc(f_cnt, 1)
                done[0] += 1
                extra[0] += 1
                v.wait_ge(f_tot, done[0])
                link(v.tensor_tensor(want, want, ps[0][:, 0:1], ALU.subtract))

            search(hi, -32768.0, 16, hstar)
            wanted_less_above(hi, hstar)
            link(v.tensor_scalar(cmpf, hi, hstar, None, ALU.is_equal))
            link(v.scalar_tensor_tensor(lo, lo, 1.0, cmpf, ALU.add, ALU.mult))
            link(v.tensor_scalar(lo, lo, 1.0, None, ALU.subtract))
            search(lo, 0.0, 16, lstar)
            wanted_less_above(lo, lstar)
            link(v.tensor_scalar(cmpf, lo, lstar, None, ALU.is_equal))
            link(v.tensor_scalar(node, node, -1.0, float(NB * P), ALU.mult, ALU.add))
            link(v.tensor_tensor(node, node, cmpf, ALU.mult))
            link(v.tensor_scalar(node, node, 1.0, None, ALU.subtract))
            search(node, 0.0, 14, nstar)
            link(v.tensor_scalar(msk, hi, hstar, None, ALU.is_gt))
            link(v.scalar_tensor_tensor(msk, lo, lstar, msk, ALU.is_gt, ALU.add))
            link(v.scalar_tensor_tensor(msk, node, nstar, msk, ALU.is_ge, ALU.add))

            v.wait_ge(u_yw, NB)
            with v.Fori(0, NCH // 2) as i:
                for q in range(2):
                    n = At(i, q)
                    landed(v, f_ld, n)
                    for k in range(CH):
                        v.scalar_tensor_tensor(xin[q][:, k, :], yw[:, bass.ds(n.times(CH * D, k * D), D)], oh[0][:, 7, bass.ds(n.times(CH, k), 1)],
                                               xin[q][:, k, :], ALU.mult, ALU.add).then_inc(f_out, 1)

        @block.scalar
        def _(a):
            def chunk_scale(n):
                after(a, p_iv, n)
                after(a, p_xn, n - 2, CH)
                a.activation(rs[:, n.par, :], inv[:, n.par, :], ACT.Sqrt).then_inc(p_rs, 1)
            chunk_scale(At(None, 0))
            chunk_scale(At(None, 1))
            with a.Fori(0, NCH // 2 - 1) as i:
                for q in range(2):
                    chunk_scale(At(i, 2 + q))
            a.wait_ge(s_par, 16 * 8)

            def body(at):
                B, C, Dd = has(at, 1), has(at, 2), has(at, 3)
                b, c, d = at - 1, at - 2, at - 3

                def gelu(e):
                    k = e % 2
                    for t in range(HT0):
                        if t == 0:
                            after(a, s_hps, c, NE, e + 1 - NE)
                            after(a, s_y, c, NE + 1, e - NE - 1)
                        a.activation(hs[k][:, t, :], ps[5 + k][:, t * P:(t + 1) * P], ACT.Gelu,
                                     bias=col[:, C_B1 + e * HT0 + t:C_B1 + e * HT0 + t + 1]).then_inc(s_h, 1)

                if B:
                    after(a, s_T, b)
                    after(a, s_gnn, b - 1)
                    a.copy(xaT[:, :, :], ps[2][:, :].rearrange("p (k n) -> p k n", k=2 * KD)).then_inc(s_aggT, 1)
                if Dd:
                    after(a, s_di, d)
                    after(a, s_dn, d - 1)
                    a.activation(rd[:, :], smd[:, 1:2], ACT.Sqrt).then_inc(s_dr, 1)
                if B:
                    after(a, s_iv, b)
                    after(a, s_xn, b - 1)
                    a.activation(rb[:, :], sm[:, 7:8], ACT.Sqrt).then_inc(s_r, 1)
                if C:
                    gelu(0)
                    gelu(1)
                    gelu(2)
                    gelu(3)
                if B:
                    after(a, s_xnTp, b)
                    if Dd:
                        after(a, s_dTp, d)
                    after(a, s_hps, b - 2, NE)
                    for k in range(KD):
                        a.activation(xnT[b.par][:, k, :], ps[2][:, k * P:(k + 1) * P], ACT.Identity,
                                     bias=col[:, C_BETA + k:C_BETA + k + 1], scale=col[:, C_GAMMA + k:C_GAMMA + k + 1]).then_inc(s_xnT, 1)
                if Dd:
                    after(a, s_dTp, d)
                    after(a, s_hj, d - 1)
                    a.copy(xndT, ps[2][:, D:2 * D].rearrange("p (k n) -> p k n", k=KD)).then_inc(s_dT, 1)
                if C:
                    gelu(4)
                if Dd:
                    after(a, s_hj, d)
                    landed(a, s_htst, d - 2)
                    after(a, s_hq, d - 2)
                    a.activation(hT[d.par][:, :], ps[1 - at.par][:, D:D + P], ACT.Relu, bias=col[:, C_BP:C_BP + 1]).then_inc(s_hT, 1)
                if B:
                    after(a, s_dl, b)
                    after(a, s_exs, b - 1)
                    a.activation(ex[:, :], exs[:, :], ACT.Exp).then_inc(s_ex, 1)
                if C:
                    gelu(5)
                    gelu(6)
                if B:
                    after(a, s_wfTp, b)
                    after(a, s_y, b - 1, NE + 1, -NE)
                    a.copy(wfT[:, :], ps[4][0:NE, D + NE:D + NE + P]).then_inc(s_wfT, 1)
                if Dd:
                    after(a, s_hpT, d)
                    landed(a, s_hpst, d - 2)
                    a.copy(hp_s[d.par][:, :], ps[1 - at.par][:, D + P:D + 2 * P]).then_inc(s_hp, 1)
                if C:
                    gelu(7)
            drive(a, body, S0)

            def body1(at):
                B, C = has(at, 1), has(at, 2)
                b, c = at - 1, at - 2
                if B:
                    after(a, u_agg, b)
                    a.activation(agg_s[:, PJ:2 * PJ], agg_s[:, 0:PJ], ACT.Sqrt).then_inc(u_sq, 1)
                    after(a, u_sqTp, b)
                    after(a, u_gnn, b - 1)
                    a.copy(xaT[:, 0, :], ps[2][:, 0:P]).then_inc(u_sqT, 1)
                    after(a, u_iv, b)
                    after(a, u_xn, b - 1)
                    a.activation(rb[:, :], sm[:, 1:2], ACT.Sqrt).then_inc(u_r, 1)
                if C:
                    for t in range(HT1):
                        after(a, u_hps, c, 2, t // HT0 - 1)
                        after(a, u_y, c - 1)
                        a.activation(hs[t // HT0][:, t % HT0, :], ps[5 + t // HT0][:, t % HT0 * P:(t % HT0 + 1) * P], ACT.Gelu_apprx_tanh,
                                     bias=col[:, C_FB1 + t:C_FB1 + t + 1]).then_inc(u_h, 1)
                if B:
                    after(a, u_xnTp, b)
                    after(a, u_hps, b - 2, 2)
                    a.copy(xnT[b.par][:, :, :], ps[2][:, 0:D].rearrange("p (k n) -> p k n", k=KD)).then_inc(u_xnT, 1)
            drive(a, body1, S1)

        @block.tensor
        def _(t):
            t.wait_ge(s_const, 9)
            t.wait_ge(s_cnt, 3)
            t.matmul(ps[0][0:NB, 0:1], cnt[:, 0:NB], ones[:, 0:1], start=True, stop=True)
            t.matmul(ps[0][0:NB, 1:2], cnt[:, 1:NB + 1], ones[:, 0:1], start=True, stop=True).then_inc(s_cntp, 1)
            t.wait_ge(s_flag, 5)
            t.matmul(ps[0][:, 2:3], ones[:, :], bad[:, 2:3], start=True, stop=True).then_inc(s_flagp, 1)
            t.wait_ge(s_flag, 7)
            t.wait_ge(s_winf, 4)
            for g in range(3 * WROWS // GT):
                k, j0 = g // (WROWS // GT), g % (WROWS // GT) * GT
                if g >= 8:
                    t.wait_ge(s_tab, g - 7)
                w = (oh[0][0:NB, :, :], winf, oh[1][0:NB, :, :])[k]
                for j in range(GT):
                    last = t.transpose(ps[g % 8][:, j * NB:(j + 1) * NB], w[:, j0 + j, :], ident[0:NB, 0:NB])
                last.then_inc(s_tp, 1)
            t.wait_ge(s_tab, 3 * WROWS // GT)
            t.wait_ge(s_par, 16 * 8)
            flag = flagged(t)

            def general(layer):
                width = (D, PJ)[layer]
                with t.If(flag == 1):
                    with t.Fori(0, ER) as r:
                        t.wait_ge(k_v, r * KV + KV * (ER * layer + 1) - 1)
                        t.wait_ge(k_gather, r * 16 + 16 * (ER * layer + 1))
                        t.matmul(ps[0][:, 0:width], k_wgt, k_got[:, 0:width], start=True, stop=True).then_inc(k_sum, 1)
                t.sem_inc(go_t)

            general(0)
            t.wait_ge(s_w2, 32)

            def body(at):
                A, B, C, Dd = has(at, 0), has(at, 1), has(at, 2), has(at, 3)
                b, c, d = at - 1, at - 2, at - 3

                def sums(g):
                    if g == 0:
                        after(t, s_agg, at - 2)
                        after(t, s_hp, at - 4)
                    after(t, s_oh, at, GRP, g + 1 - GRP)
                    for j in range(g * GW, (g + 1) * GW):
                        t.wait_ge(g_in[j], at.times(16, 16))
                        t.matmul(ps[at.par][:, 0:D], oh[at.par][:, j, :], gbuf[:, j, :], start=(j == 0), stop=(j == WROWS - 1)).then_inc(s_sum, 1)

                def hidden(e):
                    k = e % 2
                    if True:
                        after(t, s_h, c, NE * HT0, (e - 1) * HT0 - NE * HT0)
                    if e == 0:
                        after(t, s_xnT, c, KD)
                    for h in range(HT0):
                        for kk in range(KD):
                            last = t.matmul(ps[5 + k][:, h * P:(h + 1) * P], w1e[:, e, kk, h * P:(h + 1) * P], xnT[c.par][:, kk, :],
                                            start=(kk == 0), stop=(kk == KD - 1))
                    last.then_inc(s_hps, 1)

                def y(e):
                    yp = ps[(3, 7)[(e + 1) % 2]][:, 0:D]
                    after(t, s_acc, c, NE + 1, max(e, 0) - 1 - NE if e else -1 - NE)
                    if e < 0:
                        after(t, s_wfT, c)
                        t.matmul(yp, wfT[:, :], b2e_s[:, :], start=True, stop=True).then_inc(s_y, 1)
                        return
                    for h in range(HT0):
                        after(t, s_h, c, NE * HT0, e * HT0 + h + 1 - NE * HT0)
                        last = t.matmul(yp, hs[e % 2][:, h, :], w2e[:, e, h, :], start=(h == 0), stop=(h == HT0 - 1))
                    last.then_inc(s_y, 1)

                if A:
                    sums(0)
                if B:
                    after(t, s_xnT, b - 1, KD)
                    after(t, s_dT, d - 1)
                    landed(t, s_xb, b, 32)
                    for k in range(KD):
                        last = t.transpose(ps[2][:, k * P:(k + 1) * P], xnb[b.par][:, k * P:(k + 1) * P], ident[:, :])
                    after(t, s_agg, b)
                    for k in range(KD):
                        last = t.transpose(ps[2][:, D + k * P:D + (k + 1) * P], agg_s[:, k * P:(k + 1) * P], ident[:, :])
                    last.then_inc(s_T, 1)
                if A:
                    sums(1)
                if B:
                    after(t, s_aggT, b)
                    after(t, s_wfT, b - 1)
                    for k in range(2 * KD):
                        last = t.matmul(ps[4][:, 0:D], xaT[:, k, :], gw0_s[:, k % KD, k // KD * D:k // KD * D + D],
                                        start=(k == 0), stop=(k == 2 * KD - 1))
                    last.then_inc(s_gnn, 1)
                if C:
                    y(-1)
                    hidden(0)
                    hidden(1)
                    y(0)
                    hidden(2)
                    y(1)
                    hidden(3)
                if B:
                    after(t, s_xn, b)
                    for k in range(KD):
                        last = t.transpose(ps[2][:, k * P:(k + 1) * P], xn[:, k * P:(k + 1) * P], ident[:, :])
                    last.then_inc(s_xnTp, 1)
                if Dd:
                    after(t, s_dn, d)
                    if not B:
                        after(t, s_dT, d - 1)
                    for k in range(KD):
                        last = t.transpose(ps[2][:, D + k * P:D + (k + 1) * P], xnd[:, k * P:(k + 1) * P], ident[:, :])
                    last.then_inc(s_dTp, 1)
                if C:
                    y(2)
                    hidden(4)
                    y(3)
                if B:
                    after(t, s_xnT, b, KD)
                    after(t, s_x0, b)
                    for k in range(KD):
                        last = t.matmul(ps[4][:, D:D + NE], xnT[b.par][:, k, :], col[:, C_WR0 + k * NE:C_WR0 + (k + 1) * NE],
                                        start=(k == 0), stop=(k == KD - 1))
                    last.then_inc(s_lgp, 1)
                if Dd:
                    after(t, s_dT, d)
                    if B:
                        after(t, s_agg, b)
                    after(t, s_hp, d - 1)
                    for k in range(KD):
                        last = t.matmul(ps[1 - at.par][:, D:D + P], wp_s[:, k, :], xndT[:, k, :], start=(k == 0), stop=(k == KD - 1))
                    last.then_inc(s_hj, 1)
                if C:
                    hidden(5)
                    y(4)
                    hidden(6)
                    y(5)
                if B:
                    after(t, s_wf, b)
                    t.transpose(ps[4][0:NE, D + NE:D + NE + P], wf[b.par][:, :], ident[:, :]).then_inc(s_wfTp, 1)
                if Dd:
                    after(t, s_hq, d)
                    t.transpose(ps[1 - at.par][:, D + P:D + 2 * P], hq, ident[:, :]).then_inc(s_hpT, 1)
                if C:
                    hidden(7)
                    y(6)
                    y(7)
            drive(t, body, S0)

            t.wait_ge(s_brow, 1)
            general(1)

            def body1(at):
                A, B, C = has(at, 0), has(at, 1), has(at, 2)
                b, c = at - 1, at - 2

                def sums(g):
                    if g == 0:
                        after(t, u_agg, at - 2)
                    after(t, u_oh, at, GRP, g + 1 - GRP)
                    for j in range(g * GW, (g + 1) * GW):
                        t.wait_ge(g_in[j], at.times(16, 16 * (NB + 1)))
                        t.matmul(ps[at.par][:, 0:PJ], oh[at.par][:, j, :], gbuf[:, j, 0:PJ], start=(j == 0), stop=(j == WROWS - 1)).then_inc(u_sum, 1)

                if A:
                    sums(0)
                if B:
                    after(t, u_sq, b)
                    after(t, u_xnT, b - 1)
                    t.transpose(ps[2][:, 0:P], agg_s[:, PJ:2 * PJ], ident[:, :]).then_inc(u_sqTp, 1)
                if A:
                    sums(1)
                if B:
                    after(t, u_sqT, b)
                    landed(t, u_in, b, 32)
                    after(t, u_wc, b - 1)
                    t.matmul(ps[4][:, 0:D], hT[b.par][:, :], gw1_s[:, 0, :], start=True, stop=False)
                    t.matmul(ps[4][:, 0:D], xaT[:, 0, :], gw1_s[:, 1, :], start=False, stop=False)
                    t.matmul(ps[4][:, 0:D], ones[0:1, :], brow[:, :], start=False, stop=True).then_inc(u_gnn, 1)
                if C:
                    for h in range(HT1):
                        if h % HT0 == 0:
                            after(t, u_h, c - 1, HT1, h + HT0 - HT1)
                        if h == 0:
                            after(t, u_xnT, c)
                        for k in range(KD):
                            last = t.matmul(ps[5 + h // HT0][:, h % HT0 * P:(h % HT0 + 1) * P], wf1_s[:, k, h * P:(h + 1) * P], xnT[c.par][:, k, :],
                                            start=(k == 0), stop=(k == KD - 1))
                        if h % HT0 == HT0 - 1:
                            last.then_inc(u_hps, 1)
                if B:
                    after(t, u_xn, b)
                    for k in range(KD):
                        last = t.transpose(ps[2][:, k * P:(k + 1) * P], xn[:, k * P:(k + 1) * P], ident[:, :])
                    last.then_inc(u_xnTp, 1)
                if C:
                    yp = ps[(3, 7)[c.par]][:, 0:D]
                    after(t, u_yw, c - 2)
                    t.matmul(yp, ones[0:1, :], fb2row, start=True, stop=False)
                    for h in range(HT1):
                        after(t, u_h, c, HT1, h + 1 - HT1)
                        last = t.matmul(yp, hs[h // HT0][:, h % HT0, :], wf2_s[:, h, :], start=False, stop=(h == HT1 - 1))
                    last.then_inc(u_y, 1)
                if B:
                    after(t, u_xnT, b)
                    after(t, u_x2, b)
                    for k in range(KD):
                        last = t.matmul(ps[4][:, D:D + 1], xnT[b.par][:, k, :], col[:, C_WR1 + k:C_WR1 + k + 1], start=(k == 0), stop=(k == KD - 1))
                    last.then_inc(u_wp, 1)
            drive(t, body1, S1)

            t.wait_ge(u_agg, NB)
            with t.Fori(0, 16 + 1 + 16 + 1 + 14) as i:
                t.wait_ge(f_cnt, i + 1)
                t.matmul(ps[0][:, 0:1], ones[:, :], fc[:, 3:4], start=True, stop=True).then_inc(f_tot, 1)




def kernel(x, src, dst, edge_weight, L0_gnn_W1, L0_gnn_W2, L0_ffn_gamma, L0_ffn_beta, L0_ffn_Wr, L0_ffn_br, L0_ffn_W1,
           L0_ffn_b1, L0_ffn_W2, L0_ffn_b2, L1_gnn_Wp, L1_gnn_bp, L1_gnn_W1, L1_gnn_b1, L1_gnn_W2, L1_gnn_b2,
           L1_ffn_attention_mask, L1_ffn_wr, L1_ffn_br, L1_ffn_w1, L1_ffn_b1, L1_ffn_w2, L1_ffn_b2):
    import concourse.bacc as bacc
    from concourse.bass_utils import run_bass_kernel_spmd

    a = np.asarray
    xpad = np.concatenate([a(x), np.zeros((NB * P - N, D), np.float32)])
    pad = ER * P - E

    def edge_rows(v, fill):
        return np.concatenate([a(v), np.full(pad, fill, a(v).dtype)]).reshape(ER, P)

    dst_r = edge_rows(dst, 1 << 20)
    flat = dst_r.reshape(P, ER)
    dstrun = np.concatenate([flat, np.append(flat[1:, 0], flat[-1, -1])[:, None].astype(flat.dtype)], 1)
    edges = np.concatenate([edge_rows(src, 0), dst_r, edge_rows(edge_weight, 0).view(np.int32)], 1)
    cols = np.concatenate([
        a(L0_ffn_b1).reshape(NE * HT0, P).T, a(L0_ffn_gamma).reshape(KD, P).T, a(L0_ffn_beta).reshape(KD, P).T,
        a(L1_gnn_bp).reshape(1, P).T, a(L1_ffn_b1).reshape(HT1, P).T,
        a(L0_ffn_Wr).reshape(KD, P, NE).transpose(1, 0, 2).reshape(P, KD * NE), a(L1_ffn_wr).reshape(KD, P).T], 1)
    rows = np.concatenate([a(L0_ffn_br), a(L1_ffn_br), a(L1_gnn_b1), a(L1_gnn_b2), a(L1_ffn_b2)])[None]
    ins = dict(
        xpad=xpad, edges=edges, firsts=dst_r[:, 0].reshape(P, CC), dstrun=dstrun, wmoe1=a(L0_ffn_W1), wmoe2=a(L0_ffn_W2),
        gw0=np.concatenate([a(L0_gnn_W1).T, a(L0_gnn_W2).T], 1), wp=a(L1_gnn_Wp).T,
        gw1=np.concatenate([a(L1_gnn_W1).T, a(L1_gnn_W2).T], 0), wf1=a(L1_ffn_w1), wf2=a(L1_ffn_w2), b2e=a(L0_ffn_b2),
        cols=cols, rows=rows)
    ins = {k: np.ascontiguousarray(v) for k, v in ins.items()}
    nc = bacc.Bacc("TRN2", target_bir_lowering=False, num_devices=1)
    aps = {k: nc.dram_tensor("in_" + k, v.shape, mybir.dt.from_np(v.dtype), kind="ExternalInput").ap() for k, v in ins.items()}
    out = nc.dram_tensor("out_0", (NB * P, D), f32, kind="ExternalOutput").ap()
    gnn_kernel(nc, **aps, out=out)
    r = run_bass_kernel_spmd(nc, [{"in_" + k: v for k, v in ins.items()}], core_ids=[0])
    return r.results[0]["out_0"][:N]
```

```python
import numpy as np
import concourse.bass as bass
from concourse import mybir
from contextlib import ExitStack

f32 = mybir.dt.float32
i32 = mybir.dt.int32
bf16 = mybir.dt.bfloat16
f16 = mybir.dt.float16
ALU = mybir.AluOpType
ACT = mybir.ActivationFunctionType
AX = mybir.AxisListType

P = 128
N = 12500
E = 212500
D = 256
NB = -(-N // P)
TAIL = N - (NB - 1) * P
CC = 13
ER = P * CC
WROWS = 19
KD = D // P
NE, H0 = 8, 512
HT0 = H0 // P
PJ = 128
H1 = 1024
HT1 = H1 // P
KEEP = int(0.5 * N) - 1
EPS = 1e-5
GRP = 2
GROUP = [range(0, WROWS // 2 + 1), range(WROWS // 2 + 1, WROWS)]
GT = 5
BANKS = [(k, range(j, min(j + GT, WROWS))) for k in range(3) for j in range(0, WROWS, GT)]
WCH = 8
WSZ = 2 * NE * 2 * P * H0 // P // WCH
CH = 7
NCH = NB // CH

C_B1 = 0
C_GAMMA = C_B1 + NE * HT0
C_BETA = C_GAMMA + KD
C_BP = C_BETA + KD
C_FB1 = C_BP + 1
C_WR0 = C_FB1 + HT1
C_WR1 = C_WR0 + KD * NE
NCOL = C_WR1 + KD
R_BR0 = 0
R_BR1 = R_BR0 + NE
R_GB1 = R_BR1 + 1
R_GB2 = R_GB1 + D
R_FB2 = R_GB2 + D
NROW = R_FB2 + D


class At:

    def __init__(self, i, c):
        self.i, self.c = i, c

    def __sub__(self, d):
        return At(self.i, self.c - d)

    def __add__(self, d):
        return At(self.i, self.c + d)

    @property
    def par(self):
        return self.c % 2

    def times(self, m, add=0):
        if self.i is None:
            return self.c * m + add
        return self.i * (2 * m) + (self.c * m + add)

    def uses(self, m, add=0):
        if self.i is None:
            return (self.c // 2 + 1) * m + add
        return self.i * m + ((self.c // 2 + 1) * m + add)


def after(eng, sem, at, m=1, add=0):
    if at.i is not None:
        assert at.c * m + m + add > 0
    if at.c * m + m + add > 0:
        eng.wait_ge(sem, at.times(m, m + add))


def landed(eng, sems, at, m=16):
    assert at.i is None or at.c >= 0
    if at.c >= 0:
        eng.wait_ge(sems[at.par], at.uses(m))


def gnn_kernel(nc, xpad, edges, firsts, dstrun, wmoe1, wmoe2, gw0, wp, gw1, wf1, wf2, b2e, cols, rows, out):
    ctx = ExitStack()
    with ctx:
        def sb(name, shape, dt=f32):
            return ctx.enter_context(nc.sbuf_tensor(name, shape, dt))

        def sem(name):
            return ctx.enter_context(nc.semaphore(name))

        def pair(name):
            return [sem(name + "0"), sem(name + "1")]

        t_xn = nc.dram_tensor("t_xn", [NB * P, 2 * D], f16).ap()
        t_x1 = nc.dram_tensor("t_x1", [NB * P, D], f32).ap()
        t_ht = nc.dram_tensor("t_ht", [NB * P, PJ], f32).ap()
        t_hp = nc.dram_tensor("t_hp", [NB * P, PJ], f32).ap()
        t_base = nc.dram_tensor("t_base", [NB * P, D], f32).ap()

        ARENA = NB * D
        arena = sb("arena", [P, ARENA])
        gap = 2 * WSZ

        def raw(c):
            return arena[:, c * WSZ:(c + 1) * WSZ]

        def part(c, low):
            return arena[:, gap + c * WSZ:gap + (c + 1) * WSZ].bitcast(f16)[:, low * WSZ:(low + 1) * WSZ]

        w1e = arena[:, 0:NE * KD * H0].rearrange("p (e k h) -> p e k h", e=NE, k=KD)
        w2e = arena[:, NE * KD * H0:NE * (KD * H0 + HT0 * D)].rearrange("p (e t d) -> p e t d", e=NE, t=HT0)
        w1s = [[part(e // 2, low)[:, e % 2 * KD * H0:(e % 2 + 1) * KD * H0].rearrange("p (k h) -> p k h", k=KD) for low in range(2)]
               for e in range(NE)]
        w2s = [[part(WCH // 2 + e // 2, low)[:, e % 2 * HT0 * D:(e % 2 + 1) * HT0 * D].rearrange("p (t d) -> p t d", t=HT0) for low in range(2)]
               for e in range(NE)]
        at_win = 2 * WSZ
        win = arena[0:NB, at_win:at_win + WROWS * 3 * P].bitcast(i32).rearrange("p (j k) -> p j k", j=WROWS)
        at_wf = at_win + WROWS * 3 * P
        winf = [arena[0:NB, at_wf + k * WROWS * P:at_wf + (k + 1) * WROWS * P].rearrange("p (j k) -> p j k", j=WROWS) for k in range(2)]
        at0 = gap + WCH * WSZ
        xs = [[arena[:, (2 * q + low) * P:(2 * q + low + 1) * P].bitcast(f16).rearrange("p (k n) -> p k n", k=KD) for low in range(2)]
              for q in range(2)]
        hp16 = [[arena[:, 4 * P + (2 * q + low) * D:4 * P + (2 * q + low + 1) * D].bitcast(f16).rearrange("p (t n) -> p t n", t=HT0)
                 for low in range(2)] for q in range(2)]
        spot = [at0]

        def l0(*shape):
            size = int(np.prod(shape))
            spot[0] += size
            assert spot[0] <= ARENA
            flat = arena[:, spot[0] - size:spot[0]]
            if len(shape) == 1:
                return flat
            return flat.rearrange("p (a b) -> p a b", a=shape[0])

        gw0_s = l0(KD, 2 * D)
        xnb = [l0(D).bitcast(f16), l0(D).bitcast(f16)]
        xnd = l0(D)
        xndT = l0(KD, P)
        hq = l0(P)
        fch = [l0(CH * D), arena[:, at0 - CH * D:at0]]
        yw = arena

        src_t = sb("src_t", [P, NB + 1, WROWS], i32)
        dst_t = sb("dst_t", [P, NB + 1, WROWS], bf16)
        wgt_t = sb("wgt_t", [P, NB + 1, WROWS])
        gbuf = sb("gbuf", [P, WROWS, D])
        oh = [sb(f"oh{q}", [P, WROWS, P]) for q in range(2)]
        gflat = gbuf[:, :, :].rearrange("p j d -> p (j d)")
        gb16 = gflat.bitcast(f16).rearrange("p (j d) -> p j d", j=WROWS)
        oh16 = [oh[0][:, :, :].rearrange("p j n -> p (j n)").bitcast(f16)[:, q * WROWS * P:(q + 1) * WROWS * P].rearrange("p (j n) -> p j n", j=WROWS)
                for q in range(2)]
        xin = [gflat[:, q * CH * D:(q + 1) * CH * D].rearrange("p (t d) -> p t d", t=CH) for q in range(2)]
        xno = [oh[q][:, 0:CH * D // P, :].rearrange("p j n -> p (j n)").bitcast(f16).rearrange("p (t d) -> p t d", t=CH)
               for q in range(2)]
        fch = [f.rearrange("p (t d) -> p t d", t=CH) for f in fch]
        idx = sb("idx", [P, 2, WROWS], i32)
        iota_f = sb("iota_f", [P, P])
        iota_i = sb("iota_i", [P, P], i32)
        part_i = sb("part_i", [P, 1], i32)
        part_f = sb("part_f", [P, 1])
        ident = sb("ident", [P, P])
        ident16 = sb("ident16", [P, P], f16)
        iota_b = sb("iota_b", [P, P], bf16)
        ones = sb("ones", [P, P])
        tri_i = sb("tri_i", [P, NE, NE], i32)
        tri = sb("tri", [P, NE, NE])
        wp_s = sb("wp_s", [P, KD, PJ])
        gw1_s = sb("gw1_s", [P, 2, D])
        wf1_s = sb("wf1_s", [P, KD, H1])
        wf2_s = sb("wf2_s", [P, HT1, D])
        b2e_s = sb("b2e_s", [NE, D])
        col = sb("col", [P, NCOL])
        row = sb("row", [P, NROW])
        xb = [sb(f"xb{q}", [P, D]) for q in range(2)]
        agg_s = sb("agg_s", [P, D])
        xaT = sb("xaT", [P, 2 * KD, P])
        x0 = [sb(f"x0_{q}", [P, D]) for q in range(2)]
        xn = sb("xn", [P, D])
        xnT = [sb(f"xnT{q}", [P, KD, P]) for q in range(2)]
        hs = [sb(f"hs{q}", [P, HT0, P]) for q in range(2)]
        acc = [sb(f"acc{q}", [P, D]) for q in range(2)]
        hT = [sb(f"hT{q}", [P, P]) for q in range(2)]
        hp_s = [sb(f"hp{q}", [P, PJ]) for q in range(2)]
        st = sb("st", [P, CH, 6])
        mv = sb("mv", [P, CH, 2])
        rs = sb("rs", [P, 2, CH])
        inv = sb("inv", [P, 2, CH])
        mvc = [sb(f"mvc{q}", [P, CH, 2]) for q in range(2)]
        sm = sb("sm", [P, 8])
        rb = sb("rb", [P, 1])
        var2 = sb("var2", [P, 2])
        var2_i = sb("var2_i", [P, 2], i32)
        rsq_i = sb("rsq_i", [P, 2], i32)
        rsq = rsq_i[:, :].bitcast(f32)
        nwt = sb("nwt", [P, 2])
        std = sb("std", [P, 6])
        mvd = sb("mvd", [P, 2])
        lg = sb("lg", [P, NE])
        gt = sb("gt", [P, NE, NE])
        eq = sb("eq", [P, NE, NE])
        rank = sb("rank", [P, NE])
        ex = sb("ex", [P, NE])
        exs = sb("exs", [P, NE])
        dif = sb("dif", [P, NE])
        wf = [sb(f"wf{q}", [P, NE]) for q in range(2)]
        wfs = [sb(f"wfs{q}", [P, NE]) for q in range(2)]
        wfT = sb("wfT", [NE, P])
        sq = sb("sq", [P, 5])
        nrm = sb("nrm", [P, 5])
        bnd = sb("bnd", [P, 4])
        bnd_i = sb("bnd_i", [P, 4], i32)
        scl_i = sb("scl_i", [P, 4], i32)
        scl = scl_i[:, :].bitcast(f32)
        prod = sb("prod", [P, 2])
        unscl = sb("unscl", [P, 2])
        wts = sb("wts", [P, NB + 1])
        ps = [ctx.enter_context(nc.psum_tensor(f"ps{b}", [P, 512], f32)) for b in range(8)]

        wc = sb("wc", [P, 2])
        brow = sb("brow", [1, D])
        fb2row = row[0:1, R_FB2:R_FB2 + D]
        ki, kj, hi, lo, node, valid, cmpf, msk = (oh[0][:, k, 0:NB] for k in range(8))
        ki, kj = ki.bitcast(i32), kj.bitcast(i32)
        fc = sb("fc", [P, 8])
        bad = sb("bad", [P, 3])
        flag_i = sb("flag_i", [P, 1], i32)
        away = sb("away", [P, 1])
        zero = sb("zero", [P, D])
        dsts = arena[:, 0:ER + 1].bitcast(i32)
        order = arena[:, ER + 1:2 * ER + 1]
        k_cols = sb("k_cols", [P, 3], i32)
        k_f = sb("k_f", [P, 8])
        k_ix = sb("k_ix", [P, 1], i32)
        k_row, k_same, k_low, k_wgt = (oh[0][:, k, :] for k in range(4))
        k_row = k_row.bitcast(i32)
        k_got, k_out = gbuf[:, 0, :], gbuf[:, 1, :]
        k_got16, k_wgt16 = k_got.bitcast(f16), k_wgt.bitcast(f16)[:, 0:P]
        t_rest = [nc.dram_tensor("t_rest0", [(NB + 1) * P, D], f32).ap(), nc.dram_tensor("t_rest1", [(NB + 1) * P, PJ], f32).ap()]
        rest = [[l0(D), l0(D)], [gbuf[:, q, PJ:2 * PJ] for q in range(2)]]
        first_i = sb("first_i", [P, CC], i32)
        first_f = sb("first_f", [P, CC])
        thr_i = sb("thr_i", [P, NB + 1], i32)
        thr_f = sb("thr_f", [P, NB + 1])
        cnt = sb("cnt", [P, NB + 1])
        r0 = sb("r0", [NB, 1])
        r1 = sb("r1", [NB, 1])
        rowi = sb("rowi", [NB, WROWS], i32)

        g_in = [sem(f"gathered{j}") for j in range(WROWS)]
        go_sp, go_gp, go_v, go_t = sem("go_sp"), sem("go_gp"), sem("go_v"), sem("go_t")
        s_dst, s_order, s_flag, s_flagp, s_zero = (sem(n) for n in ("dsts_in", "order_found", "flag_steps", "flag_sum", "zeros"))
        k_zeroed, k_in, k_gather, k_v, k_sum, k_scatter = (sem("general_" + n) for n in ("zeroed", "edges_in", "gathered", "vector", "summed", "scattered"))
        k_low_ready = sem("general_low")
        s_rest = [pair("rest_in_l0_"), pair("rest_in_l1_")]
        s_par, s_first, s_w2 = sem("params"), sem("first_edges"), sem("moe_weights")
        s_iota, s_const, s_cnt, s_cntp, s_row = (sem(n) for n in ("iotas", "consts", "counted", "count_sum", "rows_of_windows"))
        s_win, s_winf, s_tp, s_tab = (sem(n) for n in ("windows", "windows_f", "window_T", "tables"))
        p_ld, p_st, p_bn, p_mv, p_rs, p_ve, p_xn = pair("p_load"), pair("p_store"), sem("p_bn"), sem("p_mv"), sem("p_rs"), sem("p_var_eps"), sem("p_xn")
        p_iv, p_hi, p_lo = sem("p_inverse"), sem("p_high"), sem("p_low")
        s_sq, s_sqp, s_nrm, s_scl, s_whi, s_wlo = (sem(n) for n in ("squares", "squares_sum", "norms", "scales", "weights_high", "weights_low"))
        s_xh, s_xl, s_hh, s_hl = sem("x_high"), sem("x_low"), sem("hidden_high"), sem("hidden_low")
        s_idx, s_oh, s_sum = sem("idx_ready"), sem("onehot_ready"), sem("window_summed")
        s_xb = pair("block_in")
        s_agg, s_T, s_aggT, s_gnn = sem("agg_ready"), sem("aggxn_T"), sem("aggT_ready"), sem("gnn_done")
        s_x0, s_bst, s_rsq, s_xn = (sem(n) for n in ("x0_ready", "b_stat_steps", "scale_steps", "xn_ready"))
        s_var = sem("d_variance")
        s_xnTp, s_xnT, s_lgp, s_lg, s_rt, s_dl, s_ex, s_exs, s_wf = (
            sem(n) for n in ("xn_T", "xnT_ready", "logits", "lg_ready", "route_steps", "lg_less_max",
                             "exp_done", "exp_sel", "wf_ready"))
        s_wfTp, s_wfT = sem("wf_T"), sem("wfT_ready")
        s_hps, s_h, s_y, s_acc = sem("hidden_sum"), sem("hidden_ready"), sem("y_sum"), sem("acc_ready")
        s_x1st = pair("x1_stored")
        s_dst3, s_dn, s_dTp, s_dT, s_hj, s_hT, s_hq, s_hpT, s_hp = (
            sem(n) for n in ("d_stat_steps", "xnd_ready", "xnd_T", "xndT_ready", "proj", "hT_ready", "hsq", "hp_T", "hp_ready"))
        s_htst, s_hpst = pair("ht_stored"), pair("hp_stored")

        u_in, u_bst = pair("l1_in"), pair("base_stored")
        u_idx, u_eq, u_oh, u_sum, u_sq, u_sqTp, u_sqT, u_gnn, u_x2, u_bst3, u_r, u_xn, u_base, u_xnTp, u_xnT, u_wp, u_wc, u_wts, u_hps, u_h, u_y, u_yw = (
            sem("l1_" + n) for n in ("idx", "eq", "onehot", "summed", "sqrt", "sqrt_T", "sqrtT_ready", "gnn", "x2_ready", "stat_steps", "scale",
                                     "xn_ready", "base_ready", "xn_T", "xnT_ready", "w_sum", "w_col", "w_kept", "hidden_sum", "hidden_ready", "y_sum", "yw_ready"))
        u_agg = sem("l1_agg_ready")
        u_iv = sem("l1_inverse")
        f_ld, f_st = pair("base_in"), pair("out_stored")
        f_key, f_cnt, f_tot, f_step, f_out, s_brow = (
            sem("f_" + n) for n in ("keys", "count", "total", "step", "out_ready", "bias_row"))

        S0 = NB + 3
        S1 = NB + 2
        FRONT0 = 6
        LOOP0 = (NB - FRONT0) // 2

        def drive(eng, body, nsteps):
            for s in range(FRONT0):
                body(At(None, s))
            with eng.Fori(0, LOOP0) as i:
                for u in range(2):
                    body(At(i, FRONT0 + u))
            for s in range(FRONT0 + 2 * LOOP0, nsteps):
                body(At(None, s))

        def has(at, d):
            if at.i is not None:
                return True
            return 0 <= at.c - d < NB

        MIDDLE = NCH // 2
        NEWTON = 2 + 3 * 3
        KV = 11

        def flagged(eng):
            eng.wait_ge(s_flag, 6)
            return eng.value_load(flag_i[0:1, 0:1], min_val=0, max_val=1)

        def load_rest(sp, flag, layer, b):
            with sp.If(flag == 1):
                sp.dma_start(rest[layer][b.par], t_rest[layer][bass.ds(b.times(P), P), :]).then_inc(s_rest[layer][b.par], 16)
            with sp.Else():
                sp.sem_inc(s_rest[layer][b.par], 16)
            sp.sem_inc(go_sp)

        block = ctx.enter_context(nc.Block())

        @block.sync
        def _(sp):
            sp.dma_start(first_i[:, :], firsts).then_inc(s_first, 16)
            sp.dma_start(dsts, dstrun).then_inc(s_dst, 16)

            def load_x(n):
                sp.sem_inc(go_sp)
                sp.dma_start(xin[n.par], xpad[bass.ds(n.times(CH * P), CH * P), :].rearrange("(t p) d -> p t d", p=P)).then_inc(p_ld[n.par], 16)

            def store_xn(n):
                sp.sem_inc(go_sp)
                sp.dma_start(t_xn[bass.ds(n.times(CH * P), CH * P), :].rearrange("(t p) d -> p t d", p=P), xno[n.par]).then_inc(p_st[n.par], 16)

            load_x(At(None, 0))
            load_x(At(None, 1))
            for dst, src in ((col[:, :], cols), (row[:, :], rows[0:1, :].broadcast_to([P, NROW])),
                             (wp_s[:, :, :], wp.rearrange("(k p) n -> p k n", p=P)),
                             (gw1_s[:, :, :], gw1.rearrange("(k p) n -> p k n", p=P)),
                             (wf1_s[:, :, :], wf1.rearrange("(k p) n -> p k n", p=P)),
                             (wf2_s[:, :, :], wf2.rearrange("(k p) n -> p k n", p=P)),
                             (b2e_s[:, :], b2e), (gw0_s, gw0.rearrange("(k p) n -> p k n", p=P))):
                sp.dma_start(dst, src).then_inc(s_par, 16)
            with sp.Fori(0, NCH // 2 - 1) as i:
                for q in range(2):
                    n = At(i, 2 + q)
                    after(sp, p_xn, n - 2, CH)
                    load_x(n)
                    after(sp, p_lo, n - 2)
                    store_xn(n - 2)
            for n in (At(None, NCH - 2), At(None, NCH - 1)):
                after(sp, p_lo, n)
                store_xn(n)
            for q in range(2):
                sp.wait_ge(p_st[q], 16 * (NCH // 2))

            flag = flagged(sp)

            def general(layer):
                width = (D, PJ)[layer]
                with sp.If(flag == 1):
                    sp.wait_ge(s_zero, 1)
                    with sp.Fori(0, NB + 1) as i:
                        sp.dma_start(t_rest[layer][bass.ds(i * P, P), :], zero[:, 0:width]).then_inc(k_zeroed, 16)
                    with sp.Fori(0, ER) as r:
                        with sp.If(r > 0):
                            sp.wait_ge(k_scatter, r * 16 + 16 * ER * layer)
                            sp.sem_inc(go_sp)
                        with sp.Else():
                            sp.sem_inc(go_sp)
                        for k in range(3):
                            sp.dma_start(k_cols[:, k:k + 1], edges[bass.ds(r, 1), k * P:(k + 1) * P].rearrange("a k -> k a")).then_inc(k_in, 16)
                        sp.dma_start(k_row, edges[bass.ds(r, 1), P:2 * P].broadcast_to([P, P])).then_inc(k_in, 16)
                sp.sem_inc(go_sp)

            general(0)
            sp.wait_ge(s_zero, 4)

            def body(at):
                if has(at, 0):
                    b, q = at, at.par
                    after(sp, s_x0, b - 2)
                    sp.sem_inc(go_sp)
                    after(sp, s_T, b - 2)
                    after(sp, s_agg, b - 2)
                    sp.sem_inc(go_sp)
                    sp.dma_start(xb[q][:, :], xpad[bass.ds(b.times(P), P), :]).then_inc(s_xb[q], 16)
                    sp.sem_inc(go_sp)
                    sp.dma_start(xnb[q], t_xn[bass.ds(b.times(P), P), :]).then_inc(s_xb[q], 16)
                    load_rest(sp, flag, 0, b)
                if has(at, 3):
                    b, q = at - 3, (at - 3).par
                    after(sp, s_acc, b, NE + 1)
                    sp.sem_inc(go_sp)
                    sp.dma_start(t_x1[bass.ds(b.times(P), P), :], acc[q][:, :]).then_inc(s_x1st[q], 16)
                    after(sp, s_hT, b)
                    sp.sem_inc(go_sp)
                    sp.dma_start(t_ht[bass.ds(b.times(P), P), :], hT[q][:, :]).then_inc(s_htst[q], 16)
                    after(sp, s_hp, b)
                    sp.sem_inc(go_sp)
                    sp.dma_start(t_hp[bass.ds(b.times(P), P), :], hp_s[q][:, :]).then_inc(s_hpst[q], 16)
            drive(sp, body, S0)
            for q in range(2):
                for s in (s_x1st, s_htst, s_hpst):
                    sp.wait_ge(s[q], 16 * (NB // 2))

            sp.wait_ge(s_sum, NB * WROWS)
            general(1)
            sp.wait_ge(s_zero, 6)

            def body1(at):
                if has(at, 0):
                    b, q = at, at.par
                    after(sp, u_x2, b - 2)
                    sp.sem_inc(go_sp)
                    after(sp, u_gnn, b - 2)
                    after(sp, u_agg, b - 2)
                    sp.sem_inc(go_sp)
                    sp.dma_start(xb[q][:, :], t_x1[bass.ds(b.times(P), P), :]).then_inc(u_in[q], 16)
                    sp.sem_inc(go_sp)
                    sp.dma_start(hT[q][:, :], t_ht[bass.ds(b.times(P), P), :]).then_inc(u_in[q], 16)
                    load_rest(sp, flag, 1, b)
                if has(at, 1):
                    b, q = at - 1, (at - 1).par
                    after(sp, u_base, b)
                    sp.sem_inc(go_sp)
                    sp.dma_start(t_base[bass.ds(b.times(P), P), :], acc[q][:, :]).then_inc(u_bst[q], 16)
            drive(sp, body1, S1)

            def load_base(n):
                sp.sem_inc(go_sp)
                sp.dma_start(xin[n.par], t_base[bass.ds(n.times(CH * P), CH * P), :].rearrange("(t p) d -> p t d", p=P)).then_inc(f_ld[n.par], 16)

            def store_out(n):
                sp.sem_inc(go_sp)
                sp.dma_start(out[bass.ds(n.times(CH * P), CH * P), :].rearrange("(t p) d -> p t d", p=P), xin[n.par]).then_inc(f_st[n.par], 16)

            for q in range(2):
                sp.wait_ge(u_bst[q], 16 * (NB // 2))
            sp.wait_ge(u_sum, NB * WROWS)
            load_base(At(None, 0))
            load_base(At(None, 1))
            with sp.Fori(0, NCH // 2 - 1) as i:
                for q in range(2):
                    n = At(i, 2 + q)
                    after(sp, f_out, n - 2, CH)
                    store_out(n - 2)
                    landed(sp, f_st, n - 2)
                    load_base(n)
            for n in (At(None, NCH - 2), At(None, NCH - 1)):
                after(sp, f_out, n, CH)
                store_out(n)
            for q in range(2):
                sp.wait_ge(f_st[q], 16 * (NCH // 2))

        @block.gpsimd
        def _(gp):
            gp.iota(iota_i[:, :], [[1, P]], base=0, channel_multiplier=0).then_inc(s_iota, 1)
            gp.iota(part_i[:, :], [[0, 1]], base=0, channel_multiplier=1).then_inc(s_iota, 1)
            gp.iota(thr_i[:, :], [[P, NB + 1]], base=0, channel_multiplier=0).then_inc(s_iota, 1)
            gp.iota(tri_i[:, :, :], [[-1, NE], [1, NE]], base=0, channel_multiplier=0).then_inc(s_iota, 1)
            gp.wait_ge(s_row, 3)
            for j in range(WROWS):
                gp.indirect_dma_start(win[:, j, :], None, edges, bass.IndirectOffsetOnAxis(ap=rowi[:, j:j + 1], axis=0)).then_inc(s_win, 16)
            with gp.Fori(0, NCH // 2) as i:
                for q in range(2):
                    after(gp, p_hi, At(i, q))
                    gp.sem_inc(go_gp)
                    gp.tensor_tensor(xno[q][:, :, D:2 * D], fch[q], xno[q][:, :, 0:D], ALU.subtract).then_inc(p_lo, 1)
            gp.wait_ge(s_tab, len(BANKS))
            for q in range(2):
                gp.wait_ge(p_st[q], 16 * (NCH // 2))
            flag = flagged(gp)

            def general(layer):
                table = (t_xn, t_hp)[layer]
                width = (D, PJ)[layer]
                with gp.If(flag == 1):
                    gp.wait_ge(k_zeroed, 16 * (NB + 1) * (layer + 1))
                    with gp.Fori(0, ER) as r:
                        gp.wait_ge(k_in, r * 64 + 64 * (ER * layer + 1))
                        gp.sem_inc(go_gp)
                        gp.indirect_dma_start((k_got16, k_got[:, 0:width])[layer], None, table, bass.IndirectOffsetOnAxis(ap=k_cols[:, 0:1], axis=0)).then_inc(k_gather, 16)
                        gp.wait_ge(k_v, r * KV + KV * (ER * layer + 1))
                        gp.sem_inc(go_gp)
                        gp.indirect_dma_start(t_rest[layer], bass.IndirectOffsetOnAxis(ap=k_ix[:, 0:1], axis=0), k_out[:, 0:width], None,
                                              compute_op=ALU.add).then_inc(k_scatter, 16)
                        gp.wait_ge(k_scatter, r * 16 + 16 * (ER * layer + 1))
                        gp.sem_inc(go_gp)
                gp.sem_inc(go_gp)

            general(0)
            gp.tensor_copy(idx[:, 0, :], src_t[:, 0, :]).then_inc(s_idx, 1)

            def body(at):
                if not has(at, 0):
                    return
                b, q = at, at.par
                after(gp, s_idx, b)
                for j in range(WROWS):
                    if j == WROWS - 1 and (at.i is not None or at.c + 1 < NB):
                        after(gp, s_sum, b - 1, WROWS)
                        gp.tensor_copy(idx[:, 1 - q, :], src_t[:, bass.ds((b + 1).times(1), 1), :].rearrange("p a j -> p (a j)")).then_inc(s_idx, 1)
                    after(gp, s_sum, b - 1, WROWS, j + 1 - WROWS)
                    gp.sem_inc(go_gp)
                    gp.indirect_dma_start(gb16[:, j, :], None, t_xn, bass.IndirectOffsetOnAxis(ap=idx[:, q, j:j + 1], axis=0)).then_inc(g_in[j], 16)
            drive(gp, body, S0)

            gp.wait_ge(s_idx, NB + 1)
            for q in range(2):
                gp.wait_ge(s_hpst[q], 16 * (NB // 2))
            general(1)
            gp.tensor_copy(idx[:, 0, :], src_t[:, 0, :]).then_inc(u_idx, 1)

            def body1(at):
                if not has(at, 0):
                    return
                b, q = at, at.par
                after(gp, u_idx, b)
                for j in range(WROWS):
                    if j == WROWS - 1 and (at.i is not None or at.c + 1 < NB):
                        after(gp, u_sum, b - 1, WROWS)
                        gp.tensor_copy(idx[:, 1 - q, :], src_t[:, bass.ds((b + 1).times(1), 1), :].rearrange("p a j -> p (a j)")).then_inc(u_idx, 1)
                    after(gp, u_sum, b - 1, WROWS, j + 1 - WROWS)
                    gp.sem_inc(go_gp)
                    gp.indirect_dma_start(gbuf[:, j, 0:PJ], None, t_hp, bass.IndirectOffsetOnAxis(ap=idx[:, q, j:j + 1], axis=0)).then_inc(g_in[j], 16)
            drive(gp, body1, S1)

        @block.vector
        def _(v):
            v.wait_ge(s_iota, 4)
            v.memset(ones[:, :], 1.0).then_inc(s_const, 1)
            v.memset(src_t[:, NB, :], 0).then_inc(s_const, 1)
            v.memset(dst_t[:, NB, :], -1.0).then_inc(s_const, 1)
            v.memset(wgt_t[:, NB, :], 0.0).then_inc(s_const, 1)
            v.tensor_copy(iota_f[:, :], iota_i[:, :]).then_inc(s_const, 1)
            v.tensor_copy(part_f[:, :], part_i[:, :]).then_inc(s_const, 1)
            v.tensor_copy(thr_f[:, :], thr_i[:, :]).then_inc(s_const, 1)
            v.tensor_scalar(tri[:, :, :], tri_i[:, :, :], 0.0, None, ALU.is_lt).then_inc(s_const, 1)
            v.wait_ge(s_const, 8)
            v.tensor_scalar(ident[:, :], iota_f[:, :], part_f[:, 0:1], None, ALU.is_equal).then_inc(s_const, 1)
            v.tensor_scalar(ident16[:, :], iota_f[:, :], part_f[:, 0:1], None, ALU.is_equal).then_inc(s_const, 1)
            v.tensor_copy(iota_b[:, :], iota_f[:, :]).then_inc(s_const, 1)
            v.wait_ge(s_first, 16)
            v.tensor_copy(first_f[:, :], first_i[:, :]).then_inc(s_cnt, 1)
            v.wait_ge(s_cnt, 1)
            cmp = oh[0][:, 0:11, :].rearrange("p j n -> p (j n)")[:, 0:(NB + 1) * CC].rearrange("p (b c) -> p b c", c=CC)
            v.tensor_tensor(cmp, first_f[:, :].unsqueeze(1).broadcast_to([P, NB + 1, CC]),
                            thr_f[:, :].unsqueeze(2).broadcast_to([P, NB + 1, CC]), ALU.is_lt).then_inc(s_cnt, 1)
            v.wait_ge(s_cnt, 2)
            v.tensor_reduce(cnt[:, :], cmp, AX.X, ALU.add).then_inc(s_cnt, 1)
            v.wait_ge(s_cntp, 1)
            v.tensor_scalar(r0[:, :], ps[0][0:NB, 0:1], -1.0, 0.0, ALU.add, ALU.max).then_inc(s_row, 1)
            v.wait_ge(s_row, 1)
            v.tensor_scalar(r1[:, :], r0[:, :], float(ER - WROWS), None, ALU.min).then_inc(s_row, 1)
            v.wait_ge(s_row, 2)
            v.tensor_scalar(rowi[:, :], iota_f[0:NB, 0:WROWS], r1[:, 0:1], None, ALU.add).then_inc(s_row, 1)

            v.memset(bad[:, :], 0.0).then_inc(s_flag, 1)
            v.wait_ge(s_flag, 1)
            v.tensor_scalar(bad[0:NB, 0:1], r1[:, :], float(WROWS), ps[0][0:NB, 1:2], ALU.add, ALU.is_lt).then_inc(s_flag, 1)
            v.memset(zero[:, :], 0.0).then_inc(s_zero, 1)

            def chunk_stats(n):
                q = n.par
                landed(v, p_ld, n)
                for t in range(CH):
                    v.bn_stats(st[:, t, :], xin[q][:, t, :]).then_inc(p_bn, 1)
                after(v, p_bn, n, CH)
                v.sem_inc(go_v)
                for t in range(CH):
                    v.bn_aggr(mvc[q][:, t, :], st[:, t, :]).then_inc(p_mv, 1)
                after(v, p_mv, n, CH)
                v.tensor_scalar(rs[:, q, :], mvc[q][:, :, 1], EPS, None, ALU.add).then_inc(p_ve, 1)
                after(v, p_ve, n)
                after(v, p_rs, n - 2)
                v.reciprocal(inv[:, q, :], rs[:, q, :]).then_inc(p_iv, 1)

            def chunk_norm(n):
                q = n.par
                after(v, p_rs, n)
                after(v, p_lo, n - 2)
                for t in range(CH):
                    v.tensor_scalar(fch[q][:, t, :], xin[q][:, t, :], mvc[q][:, t, 0:1], rs[:, q, t:t + 1], ALU.subtract, ALU.mult).then_inc(p_xn, 1)

            def chunk_step(n):
                chunk_stats(n + 1)
                chunk_norm(n + 1)

            chunk_stats(At(None, 0))
            chunk_norm(At(None, 0))
            for n in range(3):
                chunk_step(At(None, n))
            with v.Fori(0, (MIDDLE - 3) // 2) as i:
                for q in range(2):
                    chunk_step(At(i, 3 + q))

            v.wait_ge(s_dst, 16)
            v.tensor_tensor(order, dsts[:, 0:ER], dsts[:, 1:ER + 1], ALU.is_gt).then_inc(s_order, 1)
            v.wait_ge(s_order, 1)
            v.tensor_reduce(bad[:, 1:2], order, AX.X, ALU.add).then_inc(s_flag, 1)
            v.wait_ge(s_flag, 3)
            v.tensor_tensor(bad[:, 2:3], bad[:, 0:1], bad[:, 1:2], ALU.add).then_inc(s_flag, 1)
            v.wait_ge(s_flagp, 1)
            v.tensor_scalar(flag_i[:, :], ps[0][:, 2:3], 0.0, None, ALU.is_gt).then_inc(s_flag, 1)
            v.tensor_scalar(away[:, :], ps[0][:, 2:3], 0.0, float(1 << 20), ALU.is_gt, ALU.mult).then_inc(s_flag, 1)

            v.wait_ge(s_win, 16 * WROWS)
            blk0 = sm[0:NB, 0:1]
            v.tensor_scalar(blk0, part_f[0:NB, 0:1], float(P), None, ALU.mult).then_inc(s_winf, 1)
            v.wait_ge(s_winf, 1)
            v.tensor_scalar(winf[0], win[:, :, P:2 * P], blk0, None, ALU.subtract).then_inc(s_winf, 1)
            v.tensor_copy(winf[1], win[:, :, 0:P]).then_inc(s_winf, 1)
            for g, (k, js) in enumerate(BANKS):
                v.wait_ge(s_tp, g + 1)
                dst = (dst_t, src_t, wgt_t)[k]
                to = dst[:, 0:NB, js[0]:js[-1] + 1].rearrange("p b j -> p j b")
                of = ps[g % 8][:, 0:len(js) * NB].rearrange("p (j b) -> p j b", j=len(js))
                if k == 0:
                    v.tensor_scalar(to, of, away[:, 0:1], None, ALU.subtract).then_inc(s_tab, 1)
                else:
                    v.tensor_copy(to, of).then_inc(s_tab, 1)

            with v.Fori(0, (NCH - 1 - MIDDLE) // 2) as i:
                for q in range(2):
                    chunk_step(At(i, MIDDLE + q))

            v.wait_ge(s_par, 16 * 8)

            def onehot(b, g):
                q = b.par
                if g == 0:
                    after(v, s_sum, b - 2, WROWS)
                j0, size = GROUP[g][0], len(GROUP[g])
                d = dst_t[:, bass.ds(b.times(1), 1), j0:j0 + size].rearrange("p a j -> p (a j)")
                v.tensor_tensor(oh16[q][:, j0:j0 + size, :], iota_b[:, :].unsqueeze(1).broadcast_to([P, size, P]),
                                d.unsqueeze(2).broadcast_to([P, size, P]), ALU.is_equal).then_inc(s_oh, 1)

            v.wait_ge(s_tab, len(BANKS))
            v.wait_ge(s_tp, len(BANKS))
            for q in range(2):
                v.wait_ge(p_st[q], 16 * (NCH // 2))
            for q in range(2):
                v.memset(rest[0][q], 0.0).then_inc(s_zero, 1)
            v.memset(var2[:, :], 1.0).then_inc(s_zero, 1)
            flag = flagged(v)

            def general(layer):
                width = (D, PJ)[layer]
                dst_f, before, ok, here, off, to, dump, wone = (k_f[:, k:k + 1] for k in range(8))
                with v.If(flag == 1):
                    v.tensor_scalar(k_low, iota_f[:, :], part_f[:, 0:1], None, ALU.is_lt).then_inc(k_low_ready, 1)
                    v.tensor_scalar(dump, part_f[:, 0:1], float(NB * P), None, ALU.add).then_inc(k_low_ready, 1)
                    v.wait_ge(k_low_ready, 2 * layer + 2)
                    with v.Fori(0, ER) as r:
                        v.wait_ge(k_in, r * 64 + 64 * (ER * layer + 1))
                        n = [0]

                        def link(ins):
                            n[0] += 1
                            ins.then_inc(k_v, 1)
                            v.wait_ge(k_v, r * KV + (KV * ER * layer + n[0]))

                        link(v.tensor_copy(dst_f, k_cols[:, 1:2]))
                        link(v.tensor_scalar(k_same, k_row, dst_f, None, ALU.is_equal))
                        link(v.tensor_tensor(k_wgt, k_same, k_low, ALU.mult))
                        link(v.tensor_reduce(before, k_wgt, AX.X, ALU.add))
                        link(v.tensor_scalar(ok, before, 0.0, None, ALU.is_equal))
                        link(v.tensor_scalar(here, dst_f, float(N), ok, ALU.is_lt, ALU.mult))
                        link(v.tensor_scalar(off, dst_f, dump, None, ALU.subtract))
                        link(v.tensor_scalar(to, off, here, dump, ALU.mult, ALU.add))
                        link(v.tensor_copy(k_ix[:, :], to))
                        if layer:
                            link(v.tensor_scalar(k_wgt, k_same, k_cols[:, 2:3].bitcast(f32), None, ALU.mult))
                        else:
                            link(v.tensor_copy(k_wgt16, k_same))
                        v.wait_ge(k_sum, r + (ER * layer + 1))
                        link(v.tensor_copy(k_out[:, 0:width], ps[0][:, 0:width]))
                v.sem_inc(go_v)

            general(0)
            for g in range(GRP):
                onehot(At(None, 0), g)

            v.wait_ge(s_nrm, 1)
            v.tensor_copy(bnd[:, 0:2], nrm[:, 0:2]).then_inc(s_scl, 1)
            v.tensor_scalar(bnd[:, 2:3], nrm[:, 3:4], float(D) ** 0.5, nrm[:, 4:5], ALU.mult, ALU.add).then_inc(s_scl, 1)
            v.wait_ge(s_scl, 2)
            v.tensor_scalar(bnd[:, 3:4], bnd[:, 2:3], nrm[:, 0:1], nrm[:, 2:3], ALU.mult, ALU.add).then_inc(s_scl, 1)
            v.wait_ge(s_scl, 3)
            v.tensor_scalar(bnd[:, :], bnd[:, :], 2.0 ** -40, None, ALU.max).then_inc(s_scl, 1)
            v.wait_ge(s_scl, 4)
            v.tensor_scalar(bnd_i[:, :], bnd[:, :].bitcast(i32), 0x7f800000, None, ALU.bitwise_and).then_inc(s_scl, 1)
            v.wait_ge(s_scl, 5)
            v.tensor_scalar(scl_i[:, :], bnd_i[:, :], -1.0, float((127 + 127 + 14) << 23), ALU.mult, ALU.add).then_inc(s_scl, 1)
            v.wait_ge(s_scl, 6)
            v.tensor_tensor(prod[:, :], scl[:, 0:2], scl[:, 2:4], ALU.mult).then_inc(s_scl, 1)
            v.wait_ge(s_scl, 7)
            v.reciprocal(unscl[:, :], prod[:, :]).then_inc(s_scl, 1)
            v.wait_ge(s_scl, 8)
            for n, c in enumerate(reversed(range(WCH))):
                w = 2 * c // WCH
                v.wait_ge(s_whi, n + 1)
                v.scalar_tensor_tensor(part(c, 1), raw(c), scl[:, w:w + 1], part(c, 0), ALU.mult, ALU.subtract).then_inc(s_wlo, 1)

            def body(at):
                A, B, C, Dd = has(at, 0), has(at, 1), has(at, 2), has(at, 3)
                nxt = at + 1
                N1 = at.i is not None or at.c + 1 < NB
                b, c, d = at - 1, at - 2, at - 3
                def low(e):
                    k = e % 2
                    after(v, s_hh, c, NE, e + 1 - NE)
                    v.scalar_tensor_tensor(hp16[k][1], hs[k][:, :, :], scl[:, 3:4], hp16[k][0], ALU.mult, ALU.subtract).then_inc(s_hl, 1)

                def accumulate(e):
                    yp = ps[(3, 7)[(e + 1) % 2]][:, 0:D]
                    after(v, s_y, c, NE + 1, e + 1 - NE)
                    if e < 0:
                        landed(v, s_x1st, c - 2)
                        v.tensor_tensor(acc[c.par][:, :], yp, x0[c.par][:, :], ALU.add).then_inc(s_acc, 1)
                    else:
                        after(v, s_acc, c, NE + 1, e - NE)
                        v.scalar_tensor_tensor(acc[c.par][:, :], yp, wfs[c.par][:, e:e + 1], acc[c.par][:, :], ALU.mult, ALU.add).then_inc(s_acc, 1)

                if Dd:
                    after(v, s_acc, d, NE + 1)
                    v.bn_stats(std[:, :], acc[d.par][:, :]).then_inc(s_dst3, 1)
                    after(v, s_dst3, d, 2, -1)
                    v.sem_inc(go_v)
                    v.bn_aggr(mvd[:, :], std[:, :]).then_inc(s_dst3, 1)
                    after(v, s_dst3, d, 2, 0)
                    v.tensor_scalar(var2[:, 1:2], mvd[:, 1:2], EPS, None, ALU.add).then_inc(s_var, 1)
                if B:
                    after(v, s_gnn, b)
                    landed(v, s_xb, b, 32)
                    after(v, s_acc, b - 2, NE + 1, -NE)
                    v.scalar_tensor_tensor(x0[b.par][:, :], ps[4][:, 0:D], 0.0, xb[b.par][:, :], ALU.max, ALU.add).then_inc(s_x0, 1)
                    after(v, s_x0, b)
                    v.bn_stats(st[:, 0, :], x0[b.par][:, :]).then_inc(s_bst, 1)
                    after(v, s_bst, b, 6, -5)
                    v.sem_inc(go_v)
                    v.bn_aggr(mv[:, 0, :], st[:, 0, :]).then_inc(s_bst, 1)
                if C:
                    low(0)
                if B:
                    after(v, s_bst, b, 6, -4)
                    v.tensor_scalar(sm[:, 0:1], mv[:, 0, 1:2], EPS, None, ALU.add).then_inc(s_bst, 1)
                    after(v, s_bst, b, 6, -3)
                    v.reciprocal(sm[:, 1:2], sm[:, 0:1]).then_inc(s_bst, 1)
                    after(v, s_bst, b, 6, -2)
                    v.tensor_scalar(sm[:, 2:3], mv[:, 0, 1:2], sm[:, 1:2], EPS, ALU.mult, ALU.add).then_inc(s_bst, 1)
                    after(v, s_bst, b, 6, -1)
                    v.tensor_tensor(var2[:, 0:1], sm[:, 0:1], sm[:, 2:3], ALU.mult).then_inc(s_bst, 1)
                if C:
                    accumulate(-1)
                    low(1)
                if B or Dd:
                    if at.i is None and at.c == 1:
                        v.wait_ge(s_zero, 4)
                    if B:
                        after(v, s_bst, b, 6, 0)
                    if Dd:
                        after(v, s_var, d)
                    v.tensor_scalar(var2_i[:, :], var2[:, :].bitcast(i32), 1, None, ALU.arith_shift_right).then_inc(s_rsq, 1)
                    after(v, s_rsq, b, NEWTON, 1 - NEWTON)
                    if C:
                        after(v, s_xn, b - 1)
                    after(v, s_dn, d - 1)
                    v.tensor_scalar(rsq_i[:, :], var2_i[:, :], -1.0, float(0x5f3759df), ALU.mult, ALU.add).then_inc(s_rsq, 1)
                    for n in range(3):
                        after(v, s_rsq, b, NEWTON, 3 * n + 2 - NEWTON)
                        v.tensor_tensor(nwt[:, :], var2[:, :], rsq, ALU.mult).then_inc(s_rsq, 1)
                        after(v, s_rsq, b, NEWTON, 3 * n + 3 - NEWTON)
                        v.scalar_tensor_tensor(nwt[:, :], nwt[:, :], -0.5, rsq, ALU.mult, ALU.mult).then_inc(s_rsq, 1)
                        after(v, s_rsq, b, NEWTON, 3 * n + 4 - NEWTON)
                        v.scalar_tensor_tensor(rsq, nwt[:, :], 1.5, rsq, ALU.add, ALU.mult).then_inc(s_rsq, 1)
                    after(v, s_rsq, b, NEWTON, 0)
                if B:
                    after(v, s_xnTp, b - 1)
                    v.tensor_scalar(xn[:, :], x0[b.par][:, :], mv[:, 0, 0:1], rsq[:, 0:1], ALU.subtract, ALU.mult).then_inc(s_xn, 1)
                if Dd:
                    after(v, s_dTp, d - 1)
                    v.tensor_scalar(xnd, acc[d.par][:, :], mvd[:, 0:1], rsq[:, 1:2], ALU.subtract, ALU.mult).then_inc(s_dn, 1)

                if C:
                    low(2)
                    accumulate(0)
                if N1:
                    onehot(nxt, 0)
                if C:
                    low(3)
                    accumulate(1)
                if B:
                    after(v, s_xh, b)
                    v.scalar_tensor_tensor(xs[b.par][1], xnT[b.par][:, :, :], scl[:, 2:3], xs[b.par][0], ALU.mult, ALU.subtract).then_inc(s_xl, 1)
                    after(v, s_lgp, b)
                    v.tensor_tensor(lg[:, :], ps[4][:, D:D + NE], row[:, R_BR0:R_BR0 + NE], ALU.add).then_inc(s_lg, 1)
                    after(v, s_lg, b)
                    lj = lg[:, :].unsqueeze(1).broadcast_to([P, NE, NE])
                    le = lg[:, :].unsqueeze(2).broadcast_to([P, NE, NE])
                    v.tensor_tensor(gt[:, :, :], lj, le, ALU.is_gt).then_inc(s_rt, 1)
                    v.tensor_tensor(eq[:, :, :], lj, le, ALU.is_equal).then_inc(s_rt, 1)
                    after(v, s_rt, b, 7, -5)
                    v.tensor_tensor(eq[:, :, :], eq[:, :, :], tri[:, :, :], ALU.mult).then_inc(s_rt, 1)
                    after(v, s_rt, b, 7, -4)
                    v.tensor_tensor(gt[:, :, :], gt[:, :, :], eq[:, :, :], ALU.add).then_inc(s_rt, 1)
                    after(v, s_rt, b, 7, -3)
                    v.tensor_reduce(rank[:, :], gt[:, :, :], AX.X, ALU.add).then_inc(s_rt, 1)
                    after(v, s_rt, b, 7, -2)
                    v.scalar_tensor_tensor(gt[:, 0, :], rank[:, :], 2.0, lg[:, :], ALU.is_lt, ALU.mult).then_inc(s_rt, 1)
                    after(v, s_rt, b, 7, -1)
                    v.tensor_reduce(sm[:, 5:6], gt[:, 0, :], AX.X, ALU.add).then_inc(s_rt, 1)
                    after(v, s_rt, b, 7, 0)
                    after(v, s_ex, b - 1)
                    v.scalar_tensor_tensor(dif[:, :], sm[:, 5:6].broadcast_to([P, NE]), -0.5, lg[:, :], ALU.mult, ALU.add).then_inc(s_dl, 1)
                if C:
                    low(4)
                    accumulate(2)
                if Dd:
                    after(v, s_hT, d)
                    after(v, s_hpT, d - 1)
                    v.tensor_tensor(hq, hT[d.par][:, :], hT[d.par][:, :], ALU.mult).then_inc(s_hq, 1)
                if B:
                    after(v, s_ex, b)
                    v.tensor_scalar(exs[:, :], ex[:, :], 0.5, 0.5, ALU.mult, ALU.add).then_inc(s_exs, 1)
                    after(v, s_exs, b)
                    after(v, s_acc, b - 2, NE + 1)
                    v.scalar_tensor_tensor(wf[b.par][:, :], rank[:, :], 2.0, exs[:, :], ALU.is_lt, ALU.mult).then_inc(s_wf, 1)
                    after(v, s_wf, b, 2, -1)
                    v.tensor_scalar(wfs[b.par][:, :], wf[b.par][:, :], unscl[:, 1:2], None, ALU.mult).then_inc(s_wf, 1)
                if C:
                    low(5)
                    accumulate(3)
                if N1:
                    onehot(nxt, 1)
                if C:
                    low(6)
                    accumulate(4)
                    low(7)
                    accumulate(5)
                    accumulate(6)
                if A:
                    after(v, s_sum, at, WROWS)
                    after(v, s_T, at - 1)
                    landed(v, s_rest[0], at)
                    v.tensor_tensor(agg_s[:, :], ps[at.par][:, 0:D], rest[0][at.par], ALU.add).then_inc(s_agg, 1)
                if C:
                    accumulate(7)
            drive(v, body, S0)

            v.tensor_tensor(brow[:, :], row[0:1, R_GB1:R_GB1 + D], row[0:1, R_GB2:R_GB2 + D], ALU.add).then_inc(s_brow, 1)

            def onehot1(b, g):
                q = b.par
                if g == 0:
                    after(v, u_sum, b - 2, WROWS)
                j0, size = GROUP[g][0], len(GROUP[g])
                d = dst_t[:, bass.ds(b.times(1), 1), j0:j0 + size].rearrange("p a j -> p (a j)")
                w = wgt_t[:, bass.ds(b.times(1), 1), j0:j0 + size].rearrange("p a j -> p (a j)")
                o = oh[q][:, j0:j0 + size, :]
                v.tensor_tensor(o, iota_f[:, :].unsqueeze(1).broadcast_to([P, size, P]), d.unsqueeze(2).broadcast_to([P, size, P]), ALU.is_equal).then_inc(u_eq, 1)
                after(v, u_eq, b, GRP, g + 1 - GRP)
                v.tensor_tensor(o, o, w.unsqueeze(2).broadcast_to([P, size, P]), ALU.mult).then_inc(u_oh, 1)

            v.wait_ge(s_sum, NB * WROWS)
            v.wait_ge(s_oh, GRP * (NB + 1))
            v.wait_ge(s_hp, NB)
            general(1)
            for q in range(2):
                v.memset(rest[1][q], 0.0).then_inc(s_zero, 1)
            v.wait_ge(s_zero, 6)
            for g in range(GRP):
                onehot1(At(None, 0), g)

            def body1(at):
                B, C = has(at, 1), has(at, 2)
                N1 = at.i is not None or at.c + 1 < NB
                b, c = at - 1, at - 2
                if B:
                    after(v, u_sum, b, WROWS)
                    after(v, u_sqTp, b - 1)
                    landed(v, s_rest[1], b)
                    v.tensor_tensor(agg_s[:, 0:PJ], ps[b.par][:, 0:PJ], rest[1][b.par], ALU.add).then_inc(u_agg, 1)
                if N1:
                    onehot1(at + 1, 0)
                if B:
                    after(v, u_gnn, b)
                    landed(v, u_in, b, 32)
                    v.tensor_tensor(x0[b.par][:, :], ps[4][:, 0:D], xb[b.par][:, :], ALU.add).then_inc(u_x2, 1)
                    after(v, u_x2, b)
                    v.bn_stats(st[:, 0, :], x0[b.par][:, :]).then_inc(u_bst3, 1)
                    after(v, u_bst3, b, 3, -2)
                    v.sem_inc(go_v)
                    v.bn_aggr(mv[:, 0, :], st[:, 0, :]).then_inc(u_bst3, 1)
                    after(v, u_bst3, b, 3, -1)
                    v.tensor_scalar(sm[:, 0:1], mv[:, 0, 1:2], EPS, None, ALU.add).then_inc(u_bst3, 1)
                    after(v, u_bst3, b, 3, 0)
                    v.reciprocal(sm[:, 1:2], sm[:, 0:1]).then_inc(u_iv, 1)
                    after(v, u_r, b)
                    after(v, u_xnTp, b - 1)
                    v.tensor_scalar(xn[:, :], x0[b.par][:, :], mv[:, 0, 0:1], rb[:, 0:1], ALU.subtract, ALU.mult).then_inc(u_xn, 1)
                    after(v, u_xn, b)
                    landed(v, u_bst, b - 2)
                    v.tensor_tensor(acc[b.par][:, :], x0[b.par][:, :], xn[:, :], ALU.add).then_inc(u_base, 1)
                if N1:
                    onehot1(at + 1, 1)
                if C:
                    after(v, u_y, c)
                    after(v, u_wc, c)
                    v.tensor_scalar(yw[:, bass.ds(c.times(D), D)], ps[(3, 7)[c.par]][:, 0:D], wc[:, c.par:c.par + 1], None, ALU.mult).then_inc(u_yw, 1)
                if B:
                    after(v, u_wp, b)
                    after(v, u_yw, b - 2)
                    after(v, u_wts, b - 2)
                    v.tensor_tensor(wc[:, b.par:b.par + 1], ps[4][:, D:D + 1], row[:, R_BR1:R_BR1 + 1], ALU.add).then_inc(u_wc, 1)
                    after(v, u_wc, b)
                    v.tensor_copy(wts[:, bass.ds(b.times(1), 1)], wc[:, b.par:b.par + 1]).then_inc(u_wts, 1)
            drive(v, body1, S1)

            nf = [0]

            def link(ins):
                nf[0] += 1
                ins.then_inc(f_key, 1)
                v.wait_ge(f_key, nf[0])

            v.wait_ge(u_wts, NB)
            v.wait_ge(s_const, 11)
            link(v.tensor_scalar(node, thr_f[:, 0:NB], part_f[:, 0:1], None, ALU.add))
            link(v.tensor_scalar(valid, node, float(N), None, ALU.is_lt))
            link(v.tensor_scalar(cmpf, wts[:, 0:NB], 0.0, None, ALU.add))
            bits = cmpf.bitcast(i32)
            link(v.tensor_scalar(ki, bits, 31, 0x7fffffff, ALU.arith_shift_right, ALU.bitwise_and))
            link(v.tensor_tensor(kj, ki, bits, ALU.bitwise_xor))
            link(v.tensor_scalar(ki, kj, 16, None, ALU.arith_shift_right))
            link(v.tensor_copy(hi, ki))
            link(v.tensor_scalar(ki, kj, 0xffff, None, ALU.bitwise_and))
            link(v.tensor_copy(lo, ki))
            LOW = 65536.0
            link(v.scalar_tensor_tensor(hi, hi, LOW, valid, ALU.add, ALU.mult))
            link(v.tensor_scalar(hi, hi, LOW, None, ALU.subtract))
            cand, step, grow, count, want, hstar, lstar, nstar = (fc[:, k:k + 1] for k in range(8))
            link(v.memset(want, float(KEEP)))
            done = [0]

            def search(key, base, bits_, star):
                link(v.memset(cand, base + 2.0 ** (bits_ - 1)))
                link(v.memset(step, 2.0 ** (bits_ - 1)))
                n0 = done[0]
                with v.Fori(0, bits_) as i:
                    v.tensor_scalar(cmpf, key, cand, 0.0, ALU.is_ge, ALU.add, accum_out=count).then_inc(f_cnt, 1)
                    v.wait_ge(f_tot, i + (n0 + 1))
                    v.tensor_scalar(grow, ps[0][:, 0:1], want, step, ALU.is_ge, ALU.mult).then_inc(f_step, 1)
                    v.wait_ge(f_step, i * 3 + (3 * (n0 - extra[0]) + 1))
                    v.tensor_scalar(step, step, 0.5, None, ALU.mult).then_inc(f_step, 1)
                    v.wait_ge(f_step, i * 3 + (3 * (n0 - extra[0]) + 2))
                    v.tensor_scalar(cand, grow, cand, step, ALU.add, ALU.subtract).then_inc(f_step, 1)
                    v.wait_ge(f_step, i * 3 + (3 * (n0 - extra[0]) + 3))
                done[0] += bits_
                link(v.tensor_scalar(star, cand, -0.5, None, ALU.add))

            extra = [0]

            def wanted_less_above(key, star):
                v.tensor_scalar(cmpf, key, star, 0.0, ALU.is_gt, ALU.add, accum_out=count).then_inc(f_cnt, 1)
                done[0] += 1
                extra[0] += 1
                v.wait_ge(f_tot, done[0])
                link(v.tensor_tensor(want, want, ps[0][:, 0:1], ALU.subtract))

            search(hi, -32768.0, 16, hstar)
            wanted_less_above(hi, hstar)
            link(v.tensor_scalar(cmpf, hi, hstar, None, ALU.is_equal))
            link(v.scalar_tensor_tensor(lo, lo, 1.0, cmpf, ALU.add, ALU.mult))
            link(v.tensor_scalar(lo, lo, 1.0, None, ALU.subtract))
            search(lo, 0.0, 16, lstar)
            wanted_less_above(lo, lstar)
            link(v.tensor_scalar(cmpf, lo, lstar, None, ALU.is_equal))
            link(v.tensor_scalar(node, node, -1.0, float(NB * P), ALU.mult, ALU.add))
            link(v.tensor_tensor(node, node, cmpf, ALU.mult))
            link(v.tensor_scalar(node, node, 1.0, None, ALU.subtract))
            search(node, 0.0, 14, nstar)
            link(v.tensor_scalar(msk, hi, hstar, None, ALU.is_gt))
            link(v.scalar_tensor_tensor(msk, lo, lstar, msk, ALU.is_gt, ALU.add))
            link(v.scalar_tensor_tensor(msk, node, nstar, msk, ALU.is_ge, ALU.add))

            v.wait_ge(u_yw, NB)
            with v.Fori(0, NCH // 2) as i:
                for q in range(2):
                    n = At(i, q)
                    landed(v, f_ld, n)
                    for k in range(CH):
                        v.scalar_tensor_tensor(xin[q][:, k, :], yw[:, bass.ds(n.times(CH * D, k * D), D)], oh[0][:, 7, bass.ds(n.times(CH, k), 1)],
                                               xin[q][:, k, :], ALU.mult, ALU.add).then_inc(f_out, 1)

        @block.scalar
        def _(a):
            def chunk_scale(n):
                after(a, p_iv, n)
                after(a, p_xn, n - 2, CH)
                a.activation(rs[:, n.par, :], inv[:, n.par, :], ACT.Sqrt).then_inc(p_rs, 1)
            def chunk_high(n):
                after(a, p_xn, n, CH)
                landed(a, p_st, n - 2)
                a.copy(xno[n.par][:, :, 0:D], fch[n.par]).then_inc(p_hi, 1)

            def chunk_step(n):
                chunk_high(n)
                chunk_scale(n + 1)

            chunk_scale(At(None, 0))
            for n in range(3):
                chunk_step(At(None, n))
            with a.Fori(0, (MIDDLE - 3) // 2) as i:
                for q in range(2):
                    chunk_step(At(i, 3 + q))
            a.wait_ge(s_tab, len(BANKS))
            a.dma_start(w1e, wmoe1.rearrange("e (k p) h -> p e k h", p=P)).then_inc(s_w2, 16)
            a.dma_start(w2e, wmoe2.rearrange("e (t p) d -> p e t d", p=P)).then_inc(s_w2, 16)
            with a.Fori(0, (NCH - 1 - MIDDLE) // 2) as i:
                for q in range(2):
                    chunk_step(At(i, MIDDLE + q))
            chunk_high(At(None, NCH - 1))
            a.wait_ge(s_par, 16 * 8)

            a.wait_ge(s_w2, 32)
            a.wait_ge(p_lo, NCH)
            waste = arena[:, WCH * WSZ:WCH * WSZ + gap].bitcast(f16)
            for k, of in enumerate((arena[:, 0:2 * gap], arena[:, 2 * gap:4 * gap], col[:, C_B1:C_B1 + NE * HT0],
                                    col[:, C_GAMMA:C_GAMMA + KD], col[:, C_BETA:C_BETA + KD])):
                if k:
                    a.wait_ge(s_sq, k)
                a.activation(waste[:, 0:of.shape[1]], of, ACT.Square, accum_out=sq[:, k:k + 1]).then_inc(s_sq, 1)
            a.wait_ge(s_sqp, 1)
            a.activation(nrm[:, :], ps[7][:, 0:5], ACT.Sqrt).then_inc(s_nrm, 1)
            a.wait_ge(s_scl, 8)
            for n, c in enumerate(reversed(range(WCH))):
                w = 2 * c // WCH
                if n >= 2:
                    a.wait_ge(s_wlo, n - 1)
                a.activation(part(c, 0), raw(c), ACT.Identity, scale=scl[:, w:w + 1]).then_inc(s_whi, 1)
            a.wait_ge(s_wlo, WCH)

            def body(at):
                B, C, Dd = has(at, 1), has(at, 2), has(at, 3)
                b, c, d = at - 1, at - 2, at - 3

                def gelu(e):
                    k = e % 2
                    for t in range(HT0):
                        if t == 0:
                            after(a, s_hps, c, NE, e + 1 - NE)
                            after(a, s_hl, c, NE, e - 1 - NE)
                        a.activation(hs[k][:, t, :], ps[5 + k][:, t * P:(t + 1) * P], ACT.Gelu,
                                     bias=col[:, C_B1 + e * HT0 + t:C_B1 + e * HT0 + t + 1], scale=unscl[:, 0:1]).then_inc(s_h, 1)
                    after(a, s_h, c, NE * HT0, (e + 1 - NE) * HT0)
                    after(a, s_y, c, NE + 1, e - NE - 1)
                    a.activation(hp16[k][0], hs[k][:, :, :], ACT.Identity, scale=scl[:, 3:4]).then_inc(s_hh, 1)

                if B:
                    after(a, s_T, b)
                    after(a, s_gnn, b - 1)
                    a.copy(xaT[:, :, :], ps[2][:, :].rearrange("p (k n) -> p k n", k=2 * KD)).then_inc(s_aggT, 1)
                if C:
                    gelu(0)
                    gelu(1)
                    gelu(2)
                    gelu(3)
                if B:
                    after(a, s_xnTp, b)
                    if Dd:
                        after(a, s_dTp, d)
                    after(a, s_lgp, b - 2)
                    after(a, s_xl, b - 2)
                    for k in range(KD):
                        a.activation(xnT[b.par][:, k, :], ps[2][:, k * P:(k + 1) * P], ACT.Identity,
                                     bias=col[:, C_BETA + k:C_BETA + k + 1], scale=col[:, C_GAMMA + k:C_GAMMA + k + 1]).then_inc(s_xnT, 1)
                    after(a, s_xnT, b, KD)
                    after(a, s_hps, b - 2, NE)
                    a.activation(xs[b.par][0], xnT[b.par][:, :, :], ACT.Identity, scale=scl[:, 2:3]).then_inc(s_xh, 1)
                if Dd:
                    after(a, s_dTp, d)
                    after(a, s_hj, d - 1)
                    a.copy(xndT, ps[2][:, D:2 * D].rearrange("p (k n) -> p k n", k=KD)).then_inc(s_dT, 1)
                if C:
                    gelu(4)
                if Dd:
                    after(a, s_hj, d)
                    landed(a, s_htst, d - 2)
                    after(a, s_hq, d - 2)
                    a.activation(hT[d.par][:, :], ps[1 - at.par][:, D:D + P], ACT.Relu, bias=col[:, C_BP:C_BP + 1]).then_inc(s_hT, 1)
                if B:
                    after(a, s_dl, b)
                    after(a, s_exs, b - 1)
                    a.activation(ex[:, :], dif[:, :], ACT.Tanh).then_inc(s_ex, 1)
                if C:
                    gelu(5)
                    gelu(6)
                if B:
                    after(a, s_wfTp, b)
                    after(a, s_y, b - 1, NE + 1, -NE)
                    a.copy(wfT[:, :], ps[4][0:NE, D + NE:D + NE + P]).then_inc(s_wfT, 1)
                if Dd:
                    after(a, s_hpT, d)
                    landed(a, s_hpst, d - 2)
                    a.copy(hp_s[d.par][:, :], ps[1 - at.par][:, D + P:D + 2 * P]).then_inc(s_hp, 1)
                if C:
                    gelu(7)
            drive(a, body, S0)

            def body1(at):
                B, C = has(at, 1), has(at, 2)
                b, c = at - 1, at - 2
                if B:
                    after(a, u_agg, b)
                    a.activation(agg_s[:, PJ:2 * PJ], agg_s[:, 0:PJ], ACT.Sqrt).then_inc(u_sq, 1)
                    after(a, u_sqTp, b)
                    after(a, u_gnn, b - 1)
                    a.copy(xaT[:, 0, :], ps[2][:, 0:P]).then_inc(u_sqT, 1)
                    after(a, u_iv, b)
                    after(a, u_xn, b - 1)
                    a.activation(rb[:, :], sm[:, 1:2], ACT.Sqrt).then_inc(u_r, 1)
                if C:
                    for t in range(HT1):
                        after(a, u_hps, c, 2, t // HT0 - 1)
                        after(a, u_y, c - 1)
                        a.activation(hs[t // HT0][:, t % HT0, :], ps[5 + t // HT0][:, t % HT0 * P:(t % HT0 + 1) * P], ACT.Gelu_apprx_tanh,
                                     bias=col[:, C_FB1 + t:C_FB1 + t + 1]).then_inc(u_h, 1)
                if B:
                    after(a, u_xnTp, b)
                    after(a, u_hps, b - 2, 2)
                    a.copy(xnT[b.par][:, :, :], ps[2][:, 0:D].rearrange("p (k n) -> p k n", k=KD)).then_inc(u_xnT, 1)
            drive(a, body1, S1)

        @block.tensor
        def _(t):
            t.wait_ge(s_const, 11)
            t.wait_ge(s_cnt, 3)
            t.matmul(ps[0][0:NB, 0:1], cnt[:, 0:NB], ones[:, 0:1], start=True, stop=True)
            t.matmul(ps[0][0:NB, 1:2], cnt[:, 1:NB + 1], ones[:, 0:1], start=True, stop=True).then_inc(s_cntp, 1)
            t.wait_ge(s_flag, 4)
            t.matmul(ps[0][:, 2:3], ones[:, :], bad[:, 2:3], start=True, stop=True).then_inc(s_flagp, 1)
            t.wait_ge(s_flag, 6)
            t.wait_ge(s_winf, 3)
            for g, (k, js) in enumerate(BANKS):
                if g >= 8:
                    t.wait_ge(s_tab, g - 7)
                w = (winf[0], winf[1], win[:, :, 2 * P:3 * P].bitcast(f32))[k]
                for n, j in enumerate(js):
                    last = t.transpose(ps[g % 8][:, n * NB:(n + 1) * NB], w[:, j, :], ident[0:NB, 0:NB])
                last.then_inc(s_tp, 1)
            t.wait_ge(s_tab, len(BANKS))
            t.wait_ge(s_par, 16 * 8)
            t.wait_ge(s_sq, 5)
            t.matmul(ps[7][:, 0:5], ones[:, :], sq[:, :], start=True, stop=True).then_inc(s_sqp, 1)
            flag = flagged(t)

            def general(layer):
                width = (D, PJ)[layer]
                with t.If(flag == 1):
                    with t.Fori(0, ER) as r:
                        t.wait_ge(k_v, r * KV + KV * (ER * layer + 1) - 1)
                        t.wait_ge(k_gather, r * 16 + 16 * (ER * layer + 1))
                        if layer:
                            t.matmul(ps[0][:, 0:width], k_wgt, k_got[:, 0:width], start=True, stop=True).then_inc(k_sum, 1)
                        else:
                            t.matmul(ps[0][:, 0:D], k_wgt16, k_got16[:, 0:D], start=True, stop=False)
                            t.matmul(ps[0][:, 0:D], k_wgt16, k_got16[:, D:2 * D], start=False, stop=True).then_inc(k_sum, 1)
                t.sem_inc(go_t)

            general(0)

            def body(at):
                A, B, C, Dd = has(at, 0), has(at, 1), has(at, 2), has(at, 3)
                b, c, d = at - 1, at - 2, at - 3

                def sums(g):
                    if g == 0:
                        after(t, s_agg, at - 2)
                        after(t, s_hp, at - 4)
                    after(t, s_oh, at, GRP, g + 1 - GRP)
                    for j in GROUP[g]:
                        t.wait_ge(g_in[j], at.times(16, 16))
                        t.matmul(ps[at.par][:, 0:D], oh16[at.par][:, j, :], gb16[:, j, 0:D], start=(j == 0), stop=False)
                        t.matmul(ps[at.par][:, 0:D], oh16[at.par][:, j, :], gb16[:, j, D:2 * D], start=False, stop=(j == WROWS - 1)).then_inc(s_sum, 1)

                PARTS = ((0, 0), (0, 1), (1, 0))

                def hidden(e):
                    k = e % 2
                    after(t, s_h, c, NE * HT0, (e - 1 - NE) * HT0)
                    if e == 0:
                        after(t, s_xl, c)
                        after(t, s_wlo, At(None, 0), WCH)
                    for h in range(HT0):
                        for kk in range(KD):
                            for n, (wl, xl) in enumerate(PARTS):
                                last = t.matmul(ps[5 + k][:, h * P:(h + 1) * P], w1s[e][wl][:, kk, h * P:(h + 1) * P], xs[c.par][xl][:, kk, :],
                                                start=(kk == 0 and n == 0), stop=(kk == KD - 1 and n == 2))
                    last.then_inc(s_hps, 1)

                def y(e):
                    yp = ps[(3, 7)[(e + 1) % 2]][:, 0:D]
                    after(t, s_acc, c, NE + 1, max(e, 0) - 1 - NE)
                    if e < 0:
                        after(t, s_wfT, c)
                        t.matmul(yp, wfT[:, :], b2e_s[:, :], start=True, stop=True).then_inc(s_y, 1)
                        return
                    after(t, s_hl, c, NE, e + 1 - NE)
                    for h in range(HT0):
                        for n, (wl, hl) in enumerate(PARTS):
                            last = t.matmul(yp, hp16[e % 2][hl][:, h, :], w2s[e][wl][:, h, :], start=(h == 0 and n == 0), stop=(h == HT0 - 1 and n == 2))
                    last.then_inc(s_y, 1)

                if B:
                    after(t, s_xnT, b - 1, KD)
                    after(t, s_dT, d - 1)
                    landed(t, s_xb, b, 32)
                    for k in range(KD):
                        for low in range(2):
                            t.matmul(ps[2][:, k * P:(k + 1) * P], xnb[b.par][:, low * D + k * P:low * D + (k + 1) * P], ident16[:, :],
                                     start=(low == 0), stop=(low == 1))
                    after(t, s_agg, b)
                    for k in range(KD):
                        last = t.transpose(ps[2][:, D + k * P:D + (k + 1) * P], agg_s[:, k * P:(k + 1) * P], ident[:, :])
                    last.then_inc(s_T, 1)
                if C:
                    hidden(0)
                    y(-1)
                if B:
                    after(t, s_aggT, b)
                    after(t, s_wfT, b - 1)
                    for k in range(2 * KD):
                        last = t.matmul(ps[4][:, 0:D], xaT[:, k, :], gw0_s[:, k % KD, k // KD * D:k // KD * D + D],
                                        start=(k == 0), stop=(k == 2 * KD - 1))
                    last.then_inc(s_gnn, 1)
                if C:
                    hidden(1)
                    hidden(2)
                    y(0)
                    hidden(3)
                    y(1)
                    hidden(4)
                if B:
                    after(t, s_xn, b)
                    for k in range(KD):
                        last = t.transpose(ps[2][:, k * P:(k + 1) * P], xn[:, k * P:(k + 1) * P], ident[:, :])
                    last.then_inc(s_xnTp, 1)
                if Dd:
                    after(t, s_dn, d)
                    if not B:
                        after(t, s_dT, d - 1)
                    for k in range(KD):
                        last = t.transpose(ps[2][:, D + k * P:D + (k + 1) * P], xnd[:, k * P:(k + 1) * P], ident[:, :])
                    last.then_inc(s_dTp, 1)
                if C:
                    y(2)
                    hidden(5)
                if B:
                    after(t, s_xnT, b, KD)
                    after(t, s_x0, b)
                    for k in range(KD):
                        last = t.matmul(ps[4][:, D:D + NE], xnT[b.par][:, k, :], col[:, C_WR0 + k * NE:C_WR0 + (k + 1) * NE],
                                        start=(k == 0), stop=(k == KD - 1))
                    last.then_inc(s_lgp, 1)
                if Dd:
                    after(t, s_dT, d)
                    if B:
                        after(t, s_agg, b)
                    after(t, s_hp, d - 1)
                    for k in range(KD):
                        last = t.matmul(ps[1 - at.par][:, D:D + P], wp_s[:, k, :], xndT[:, k, :], start=(k == 0), stop=(k == KD - 1))
                    last.then_inc(s_hj, 1)
                if C:
                    y(3)
                if A:
                    sums(0)
                if C:
                    hidden(6)
                    y(4)
                if B:
                    after(t, s_wf, b, 2, -1)
                    t.transpose(ps[4][0:NE, D + NE:D + NE + P], wf[b.par][:, :], ident[:, :]).then_inc(s_wfTp, 1)
                if Dd:
                    after(t, s_hq, d)
                    t.transpose(ps[1 - at.par][:, D + P:D + 2 * P], hq, ident[:, :]).then_inc(s_hpT, 1)
                if C:
                    hidden(7)
                    y(5)
                    y(6)
                if A:
                    sums(1)
                if C:
                    y(7)
            drive(t, body, S0)

            t.wait_ge(s_brow, 1)
            general(1)

            def body1(at):
                A, B, C = has(at, 0), has(at, 1), has(at, 2)
                b, c = at - 1, at - 2

                def sums(g):
                    if g == 0:
                        after(t, u_agg, at - 2)
                    after(t, u_oh, at, GRP, g + 1 - GRP)
                    for j in GROUP[g]:
                        t.wait_ge(g_in[j], at.times(16, 16 * (NB + 1)))
                        t.matmul(ps[at.par][:, 0:PJ], oh[at.par][:, j, :], gbuf[:, j, 0:PJ], start=(j == 0), stop=(j == WROWS - 1)).then_inc(u_sum, 1)

                if A:
                    sums(0)
                if B:
                    after(t, u_sq, b)
                    after(t, u_xnT, b - 1)
                    t.transpose(ps[2][:, 0:P], agg_s[:, PJ:2 * PJ], ident[:, :]).then_inc(u_sqTp, 1)
                if A:
                    sums(1)
                if B:
                    after(t, u_sqT, b)
                    landed(t, u_in, b, 32)
                    after(t, u_wc, b - 1)
                    t.matmul(ps[4][:, 0:D], hT[b.par][:, :], gw1_s[:, 0, :], start=True, stop=False)
                    t.matmul(ps[4][:, 0:D], xaT[:, 0, :], gw1_s[:, 1, :], start=False, stop=False)
                    t.matmul(ps[4][:, 0:D], ones[0:1, :], brow[:, :], start=False, stop=True).then_inc(u_gnn, 1)
                if C:
                    for h in range(HT1):
                        if h % HT0 == 0:
                            after(t, u_h, c - 1, HT1, h + HT0 - HT1)
                        if h == 0:
                            after(t, u_xnT, c)
                        for k in range(KD):
                            last = t.matmul(ps[5 + h // HT0][:, h % HT0 * P:(h % HT0 + 1) * P], wf1_s[:, k, h * P:(h + 1) * P], xnT[c.par][:, k, :],
                                            start=(k == 0), stop=(k == KD - 1))
                        if h % HT0 == HT0 - 1:
                            last.then_inc(u_hps, 1)
                if B:
                    after(t, u_xn, b)
                    for k in range(KD):
                        last = t.transpose(ps[2][:, k * P:(k + 1) * P], xn[:, k * P:(k + 1) * P], ident[:, :])
                    last.then_inc(u_xnTp, 1)
                if C:
                    yp = ps[(3, 7)[c.par]][:, 0:D]
                    after(t, u_yw, c - 2)
                    t.matmul(yp, ones[0:1, :], fb2row, start=True, stop=False)
                    for h in range(HT1):
                        after(t, u_h, c, HT1, h + 1 - HT1)
                        last = t.matmul(yp, hs[h // HT0][:, h % HT0, :], wf2_s[:, h, :], start=False, stop=(h == HT1 - 1))
                    last.then_inc(u_y, 1)
                if B:
                    after(t, u_xnT, b)
                    after(t, u_x2, b)
                    for k in range(KD):
                        last = t.matmul(ps[4][:, D:D + 1], xnT[b.par][:, k, :], col[:, C_WR1 + k:C_WR1 + k + 1], start=(k == 0), stop=(k == KD - 1))
                    last.then_inc(u_wp, 1)
            drive(t, body1, S1)

            t.wait_ge(u_agg, NB)
            with t.Fori(0, 16 + 1 + 16 + 1 + 14) as i:
                t.wait_ge(f_cnt, i + 1)
                t.matmul(ps[0][:, 0:1], ones[:, :], fc[:, 3:4], start=True, stop=True).then_inc(f_tot, 1)




def kernel(x, src, dst, edge_weight, L0_gnn_W1, L0_gnn_W2, L0_ffn_gamma, L0_ffn_beta, L0_ffn_Wr, L0_ffn_br, L0_ffn_W1,
           L0_ffn_b1, L0_ffn_W2, L0_ffn_b2, L1_gnn_Wp, L1_gnn_bp, L1_gnn_W1, L1_gnn_b1, L1_gnn_W2, L1_gnn_b2,
           L1_ffn_attention_mask, L1_ffn_wr, L1_ffn_br, L1_ffn_w1, L1_ffn_b1, L1_ffn_w2, L1_ffn_b2):
    import concourse.bacc as bacc
    from concourse.bass_utils import run_bass_kernel_spmd

    a = np.asarray
    xpad = np.concatenate([a(x), np.zeros((NB * P - N, D), np.float32)])
    pad = ER * P - E

    def edge_rows(v, fill):
        return np.concatenate([a(v), np.full(pad, fill, a(v).dtype)]).reshape(ER, P)

    dst_r = edge_rows(dst, 1 << 20)
    flat = dst_r.reshape(P, ER)
    dstrun = np.concatenate([flat, np.append(flat[1:, 0], flat[-1, -1])[:, None].astype(flat.dtype)], 1)
    edges = np.concatenate([edge_rows(src, 0), dst_r, edge_rows(edge_weight, 0).view(np.int32)], 1)
    cols = np.concatenate([
        a(L0_ffn_b1).reshape(NE * HT0, P).T, a(L0_ffn_gamma).reshape(KD, P).T, a(L0_ffn_beta).reshape(KD, P).T,
        a(L1_gnn_bp).reshape(1, P).T, a(L1_ffn_b1).reshape(HT1, P).T,
        a(L0_ffn_Wr).reshape(KD, P, NE).transpose(1, 0, 2).reshape(P, KD * NE), a(L1_ffn_wr).reshape(KD, P).T], 1)
    rows = np.concatenate([a(L0_ffn_br), a(L1_ffn_br), a(L1_gnn_b1), a(L1_gnn_b2), a(L1_ffn_b2)])[None]
    ins = dict(
        xpad=xpad, edges=edges, firsts=dst_r[:, 0].reshape(P, CC), dstrun=dstrun, wmoe1=a(L0_ffn_W1), wmoe2=a(L0_ffn_W2),
        gw0=np.concatenate([a(L0_gnn_W1).T, a(L0_gnn_W2).T], 1), wp=a(L1_gnn_Wp).T,
        gw1=np.concatenate([a(L1_gnn_W1).T, a(L1_gnn_W2).T], 0), wf1=a(L1_ffn_w1), wf2=a(L1_ffn_w2), b2e=a(L0_ffn_b2),
        cols=cols, rows=rows)
    ins = {k: np.ascontiguousarray(v) for k, v in ins.items()}
    nc = bacc.Bacc("TRN2", target_bir_lowering=False, num_devices=1)
    aps = {k: nc.dram_tensor("in_" + k, v.shape, mybir.dt.from_np(v.dtype), kind="ExternalInput").ap() for k, v in ins.items()}
    out = nc.dram_tensor("out_0", (NB * P, D), f32, kind="ExternalOutput").ap()
    gnn_kernel(nc, **aps, out=out)
    r = run_bass_kernel_spmd(nc, [{"in_" + k: v for k, v in ins.items()}], core_ids=[0])
    return r.results[0]["out_0"][:N]
```

```python
import numpy as np
import concourse.bass as bass
from concourse import mybir
from contextlib import ExitStack

f32 = mybir.dt.float32
i32 = mybir.dt.int32
bf16 = mybir.dt.bfloat16
f16 = mybir.dt.float16
ALU = mybir.AluOpType
ACT = mybir.ActivationFunctionType
AX = mybir.AxisListType

P = 128
N = 12500
E = 212500
D = 256
NB = -(-N // P)
CC = 13
ER = P * CC
WROWS = 19
FIXED = WROWS - 2
KD = D // P
NE, H0 = 8, 512
HT0 = H0 // P
PJ = 128
H1 = 1024
HT1 = H1 // P
KEEP = int(0.5 * N) - 1
EPS = 1e-5
GRP = 2
GROUP = [range(0, WROWS // 2 + 1), range(WROWS // 2 + 1, WROWS)]
GT = 5
BANKS = [(k, range(j, min(j + GT, WROWS))) for k in range(3) for j in range(0, WROWS, GT)]
WCH = 8
WSZ = 2 * NE * 2 * P * H0 // P // WCH
CH = 7
NCH = NB // CH
RADIX = 16
NBUF = 7
DIGITS = 4

C_B1 = 0
C_GAMMA = C_B1 + NE * HT0
C_BETA = C_GAMMA + KD
C_BP = C_BETA + KD
C_FB1 = C_BP + 1
C_WR0 = C_FB1 + HT1
C_WR1 = C_WR0 + KD * NE
NCOL = C_WR1 + KD
R_BR0 = 0
R_BR1 = R_BR0 + NE
R_GB1 = R_BR1 + 1
R_GB2 = R_GB1 + D
R_FB2 = R_GB2 + D
NROW = R_FB2 + D


class At:

    def __init__(self, i, c):
        self.i, self.c = i, c

    def __sub__(self, d):
        return At(self.i, self.c - d)

    def __add__(self, d):
        return At(self.i, self.c + d)

    @property
    def par(self):
        return self.c % 2

    def times(self, m, add=0):
        if self.i is None:
            return self.c * m + add
        return self.i * (2 * m) + (self.c * m + add)

    def uses(self, m, add=0):
        if self.i is None:
            return (self.c // 2 + 1) * m + add
        return self.i * m + ((self.c // 2 + 1) * m + add)


def after(eng, sem, at, m=1, add=0):
    if at.i is not None:
        assert at.c * m + m + add > 0
    if at.c * m + m + add > 0:
        eng.wait_ge(sem, at.times(m, m + add))


def landed(eng, sems, at, m=16):
    assert at.i is None or at.c >= 0
    if at.c >= 0:
        eng.wait_ge(sems[at.par], at.uses(m))


def gnn_kernel(nc, xpad, edges, firsts, dstrun, wmoe1, wmoe2, gw0, wp, gw1, wf1, wf2, b2e, cols, rows, out):
    ctx = ExitStack()
    with ctx:
        def sb(name, shape, dt=f32):
            return ctx.enter_context(nc.sbuf_tensor(name, shape, dt))

        def sem(name):
            return ctx.enter_context(nc.semaphore(name))

        def pair(name):
            return [sem(name + "0"), sem(name + "1")]

        t_xn = nc.dram_tensor("t_xn", [NB * P, 2 * D], f16).ap()
        t_x1 = nc.dram_tensor("t_x1", [NB * P, D], f32).ap()
        t_ht = nc.dram_tensor("t_ht", [NB * P, PJ], f32).ap()
        t_hp = nc.dram_tensor("t_hp", [NB * P, PJ], f32).ap()
        t_base = nc.dram_tensor("t_base", [NB * P, D], f32).ap()

        ARENA = NB * D
        arena = sb("arena", [P, ARENA])
        gap = 2 * WSZ

        def raw(c):
            return arena[:, c * WSZ:(c + 1) * WSZ]

        def part(c, low):
            return arena[:, gap + c * WSZ:gap + (c + 1) * WSZ].bitcast(f16)[:, low * WSZ:(low + 1) * WSZ]

        w1e = arena[:, 0:NE * KD * H0].rearrange("p (e k h) -> p e k h", e=NE, k=KD)
        w2e = arena[:, NE * KD * H0:NE * (KD * H0 + HT0 * D)].rearrange("p (e t d) -> p e t d", e=NE, t=HT0)
        w1s = [[part(e // 2, low)[:, e % 2 * KD * H0:(e % 2 + 1) * KD * H0].rearrange("p (k h) -> p k h", k=KD) for low in range(2)]
               for e in range(NE)]
        w2s = [[part(WCH // 2 + e // 2, low)[:, e % 2 * HT0 * D:(e % 2 + 1) * HT0 * D].rearrange("p (t d) -> p t d", t=HT0) for low in range(2)]
               for e in range(NE)]
        at_win = 2 * WSZ
        win = arena[0:NB, at_win:at_win + WROWS * 3 * P].bitcast(i32).rearrange("p (j k) -> p j k", j=WROWS)
        at_wf = at_win + WROWS * 3 * P
        winf = [arena[0:NB, at_wf + k * WROWS * P:at_wf + (k + 1) * WROWS * P].rearrange("p (j k) -> p j k", j=WROWS) for k in range(2)]
        at0 = gap + WCH * WSZ
        xs = [[arena[:, (2 * q + low) * P:(2 * q + low + 1) * P].bitcast(f16).rearrange("p (k n) -> p k n", k=KD) for low in range(2)]
              for q in range(2)]
        hp16 = [[arena[:, 4 * P + (2 * q + low) * D:4 * P + (2 * q + low + 1) * D].bitcast(f16).rearrange("p (t n) -> p t n", t=HT0)
                 for low in range(2)] for q in range(2)]
        spot = [at0]

        def l0(*shape):
            size = int(np.prod(shape))
            spot[0] += size
            assert spot[0] <= ARENA
            flat = arena[:, spot[0] - size:spot[0]]
            if len(shape) == 1:
                return flat
            return flat.rearrange("p (a b) -> p a b", a=shape[0])

        gw0_s = l0(KD, 2 * D)
        xnb = [l0(D).bitcast(f16), l0(D).bitcast(f16)]
        xnd = l0(D)
        xndT = l0(KD, P)
        hq = l0(P)
        fch = [l0(CH * D), arena[:, at0 - CH * D:at0]]
        yw = arena

        src_t = sb("src_t", [P, NB + 1, WROWS], i32)
        dst_t = sb("dst_t", [P, NB + 1, WROWS], bf16)
        wgt_t = sb("wgt_t", [P, NB + 1, WROWS])
        gbuf = sb("gbuf", [P, WROWS, D])
        oh = [sb(f"oh{q}", [P, WROWS, P]) for q in range(2)]
        gflat = gbuf[:, :, :].rearrange("p j d -> p (j d)")
        gb16 = gflat.bitcast(f16).rearrange("p (j d) -> p j d", j=WROWS)
        oh16 = [oh[0][:, :, :].rearrange("p j n -> p (j n)").bitcast(f16)[:, q * WROWS * P:(q + 1) * WROWS * P].rearrange("p (j n) -> p j n", j=WROWS)
                for q in range(2)]
        xin = [gflat[:, q * CH * D:(q + 1) * CH * D].rearrange("p (t d) -> p t d", t=CH) for q in range(2)]
        xno = [oh[q][:, 0:CH * D // P, :].rearrange("p j n -> p (j n)").bitcast(f16).rearrange("p (t d) -> p t d", t=CH)
               for q in range(2)]
        fch = [f.rearrange("p (t d) -> p t d", t=CH) for f in fch]
        idx = sb("idx", [P, 2, WROWS], i32)
        iota_f = sb("iota_f", [P, P])
        iota_i = sb("iota_i", [P, P], i32)
        part_i = sb("part_i", [P, 1], i32)
        part_f = sb("part_f", [P, 1])
        ident = sb("ident", [P, P])
        ident16 = sb("ident16", [P, P], f16)
        iota_b = sb("iota_b", [P, P], bf16)
        ones = sb("ones", [P, P])
        tri_i = sb("tri_i", [P, NE, NE], i32)
        tri = sb("tri", [P, NE, NE])
        wp_s = sb("wp_s", [P, KD, PJ])
        gw1_s = sb("gw1_s", [P, 2, D])
        wf1_s = sb("wf1_s", [P, KD, H1])
        wf2_s = sb("wf2_s", [P, HT1, D])
        b2e_s = sb("b2e_s", [NE, D])
        col = sb("col", [P, NCOL])
        row = sb("row", [P, NROW])
        xb = [sb(f"xb{q}", [P, D]) for q in range(2)]
        agg_s = sb("agg_s", [P, D])
        xaT = sb("xaT", [P, 2 * KD, P])
        x0 = [sb(f"x0_{q}", [P, D]) for q in range(2)]
        xn = sb("xn", [P, D])
        xnT = [sb(f"xnT{q}", [P, KD, P]) for q in range(2)]
        hs = [sb(f"hs{q}", [P, HT0, P]) for q in range(2)]
        acc = [sb(f"acc{q}", [P, D]) for q in range(2)]
        hT = [sb(f"hT{q}", [P, P]) for q in range(2)]
        hp_s = [sb(f"hp{q}", [P, PJ]) for q in range(2)]
        st = sb("st", [P, CH, 6])
        mv = sb("mv", [P, CH, 2])
        rs = sb("rs", [P, 2, CH])
        inv = sb("inv", [P, 2, CH])
        mvc = [sb(f"mvc{q}", [P, CH, 2]) for q in range(2)]
        sm = sb("sm", [P, 8])
        rb = sb("rb", [P, 1])
        var2 = sb("var2", [P, 2])
        var2_i = sb("var2_i", [P, 2], i32)
        rsq_i = sb("rsq_i", [P, 2], i32)
        rsq = rsq_i[:, :].bitcast(f32)
        nwt = sb("nwt", [P, 2])
        std = sb("std", [P, 6])
        mvd = sb("mvd", [P, 2])
        lg = sb("lg", [P, NE])
        gt = sb("gt", [P, NE, NE])
        eq = sb("eq", [P, NE, NE])
        rank = sb("rank", [P, NE])
        ex = sb("ex", [P, NE])
        exs = sb("exs", [P, NE])
        dif = sb("dif", [P, NE])
        wf = [sb(f"wf{q}", [P, NE]) for q in range(2)]
        wfs = [sb(f"wfs{q}", [P, NE]) for q in range(2)]
        wfT = sb("wfT", [NE, P])
        sq = sb("sq", [P, 5])
        nrm = sb("nrm", [P, 5])
        bnd = sb("bnd", [P, 4])
        bnd_i = sb("bnd_i", [P, 4], i32)
        scl_i = sb("scl_i", [P, 4], i32)
        scl = scl_i[:, :].bitcast(f32)
        prod = sb("prod", [P, 2])
        unscl = sb("unscl", [P, 2])
        wts = sb("wts", [P, NB + 1])
        ps = [ctx.enter_context(nc.psum_tensor(f"ps{b}", [P, 512], f32)) for b in range(8)]

        wc = sb("wc", [P, 2])
        brow = sb("brow", [1, D])
        fb2row = row[0:1, R_FB2:R_FB2 + D]
        ki, kj, hi, lo, equal, valid, cmpf, msk = (oh[0][:, k, 0:NB] for k in range(8))
        ki, kj = ki.bitcast(i32), kj.bitcast(i32)
        ge = oh[0][:, 8:8 + (RADIX * NB + 2 * P - 1) // (2 * P), :].rearrange("p j n -> p (j n)").bitcast(bf16)[:, 0:(RADIX - 1) * NB].rearrange("p (c b) -> p c b", b=NB)
        scan = [oh[0][:, 14 + 2 * k:16 + 2 * k, :].rearrange("p j n -> p (j n)") for k in range(2)]
        before = oh[0][:, 18, :]
        fc = sb("fc", [P, 6])
        thr = sb("thr", [P, RADIX - 1])
        low_tri = hs[0][:, 0, :]
        count = sb("count", [P, RADIX - 1])
        fbuf = [gflat[:, 0:CH * D], gflat[:, CH * D:2 * CH * D], oh[1][:, :, :].rearrange("p j n -> p (j n)"),
                wf1_s[:, :, :].rearrange("p k n -> p (k n)"), wf2_s[:, :, :].rearrange("p k n -> p (k n)"),
                src_t[:, :, :].rearrange("p b j -> p (b j)").bitcast(f32), wgt_t[:, :, :].rearrange("p b j -> p (b j)")]
        fbuf = [f[:, 0:CH * D].rearrange("p (t d) -> p t d", t=CH) for f in fbuf]
        bad = sb("bad", [P, 3])
        flag_i = sb("flag_i", [P, 1], i32)
        away = sb("away", [P, 1])
        zero = sb("zero", [P, D])
        dsts = arena[:, 0:ER + 1].bitcast(i32)
        order = arena[:, ER + 1:2 * ER + 1]
        k_cols = sb("k_cols", [P, 3], i32)
        k_f = sb("k_f", [P, 8])
        k_ix = sb("k_ix", [P, 1], i32)
        k_row, k_same, k_low, k_wgt = (oh[0][:, k, :] for k in range(4))
        k_row = k_row.bitcast(i32)
        k_got, k_out = gbuf[:, 0, :], gbuf[:, 1, :]
        k_got16, k_wgt16 = k_got.bitcast(f16), k_wgt.bitcast(f16)[:, 0:P]
        t_rest = [nc.dram_tensor(f"t_rest{layer}", [(NB + 1) * P, width], f32).ap() for layer, width in enumerate((D, PJ))]
        rest = [[l0(D), l0(D)], [gbuf[:, q, PJ:2 * PJ] for q in range(2)]]
        first_i = sb("first_i", [P, CC], i32)
        first_f = sb("first_f", [P, CC])
        thr_i = sb("thr_i", [P, NB + 1], i32)
        thr_f = sb("thr_f", [P, NB + 1])
        cnt = sb("cnt", [P, NB + 1])
        r0 = sb("r0", [NB, 1])
        r1 = sb("r1", [NB, 1])
        rowi = sb("rowi", [NB, WROWS], i32)
        unused = sb("unused", [NB, 1])
        edged = sb("edged", [NB, WROWS - FIXED])
        to_here = oh[1][0:NB, 0, 0:NB]
        extra_i = sb("extra_i", [1, 1 + WROWS - FIXED, NB], i32)

        g_in = [sem(f"gathered{j}") for j in range(WROWS)]
        go_sp, go_gp, go_v, go_t = sem("go_sp"), sem("go_gp"), sem("go_v"), sem("go_t")
        s_dst, s_flag, s_flagp, s_zero = (sem(n) for n in ("dsts_in", "flag_steps", "flag_sum", "zeros"))
        k_zeroed, k_in, k_gather, k_v, k_sum, k_scatter = (sem("general_" + n) for n in ("zeroed", "edges_in", "gathered", "vector", "summed", "scattered"))
        k_low_ready = sem("general_low")
        s_rest = [pair("rest_in_l0_"), pair("rest_in_l1_")]
        s_par, s_first, s_w2 = sem("params"), sem("first_edges"), sem("moe_weights")
        s_iota, s_const, s_cnt, s_cntp, s_row = (sem(n) for n in ("iotas", "consts", "counted", "count_sum", "rows_of_windows"))
        s_win, s_winf, s_tp, s_tab, s_tab_a, s_srcf = (sem(n) for n in ("windows", "windows_f", "window_T", "tables_dst", "tables_src_wgt", "sources_f"))
        p_ld, p_st, p_stat, p_rs, p_xn = pair("p_load"), pair("p_store"), sem("p_stat_steps"), sem("p_rs"), sem("p_xn")
        p_iv, p_hi, p_lo = sem("p_inverse"), sem("p_high"), sem("p_low")
        s_sq, s_sqp, s_nrm, s_scl, s_whi, s_wlo = (sem(n) for n in ("squares", "squares_sum", "norms", "scales", "weights_high", "weights_low"))
        s_xh, s_xl, s_hh, s_hl = sem("x_high"), sem("x_low"), sem("hidden_high"), sem("hidden_low")
        s_idx, s_oh, s_sum = sem("idx_ready"), sem("onehot_ready"), sem("window_summed")
        s_xb = pair("block_in")
        s_agg, s_T, s_aggT, s_gnn = sem("agg_ready"), sem("aggxn_T"), sem("aggT_ready"), sem("gnn_done")
        s_x0, s_bst, s_rsq, s_xn = (sem(n) for n in ("x0_ready", "b_stat_steps", "scale_steps", "xn_ready"))
        s_var = sem("d_variance")
        s_xnTp, s_xnT, s_lgp, s_rt, s_dl, s_ex, s_exs, s_wf = (
            sem(n) for n in ("xn_T", "xnT_ready", "logits", "route_steps", "lg_less_max",
                             "exp_done", "exp_sel", "wf_ready"))
        s_wfTp, s_wfT = sem("wf_T"), sem("wfT_ready")
        s_hps, s_h, s_y, s_acc = sem("hidden_sum"), sem("hidden_ready"), sem("y_sum"), sem("acc_ready")
        s_x1st = pair("x1_stored")
        s_dst3, s_dn, s_dTp, s_dT, s_hj, s_hT, s_hq, s_hpT, s_hp = (
            sem(n) for n in ("d_stat_steps", "xnd_ready", "xnd_T", "xndT_ready", "proj", "hT_ready", "hsq", "hp_T", "hp_ready"))
        s_htst, s_hpst = pair("ht_stored"), pair("hp_stored")

        u_in, u_bst = pair("l1_in"), pair("base_stored")
        u_idx, u_eq, u_oh, u_sum, u_sq, u_sqTp, u_sqT, u_gnn, u_x2, u_bst3, u_r, u_xn, u_base, u_xnTp, u_xnT, u_wp, u_wc, u_wts, u_hps, u_h, u_y, u_yw = (
            sem("l1_" + n) for n in ("idx", "eq", "onehot", "summed", "sqrt", "sqrt_T", "sqrtT_ready", "gnn", "x2_ready", "stat_steps", "scale",
                                     "xn_ready", "base_ready", "xn_T", "xnT_ready", "w_sum", "w_col", "w_kept", "hidden_sum", "hidden_ready", "y_sum", "yw_ready"))
        u_agg = sem("l1_agg_ready")
        u_iv = sem("l1_inverse")
        f_io = [sem(f"last_pass_buffer{k}") for k in range(len(fbuf))]
        f_key, f_cnt, f_tot, f_step, f_out, s_brow = (
            sem("f_" + n) for n in ("keys", "count", "total", "step", "out_ready", "bias_row"))

        S0 = NB + 3
        S1 = NB + 2
        FRONT0 = 6
        LOOP0 = (NB - FRONT0) // 2

        def drive(eng, body, nsteps):
            for s in range(FRONT0):
                body(At(None, s))
            with eng.Fori(0, LOOP0) as i:
                for u in range(2):
                    body(At(i, FRONT0 + u))
            for s in range(FRONT0 + 2 * LOOP0, nsteps):
                body(At(None, s))

        def has(at, d):
            if at.i is not None:
                return True
            return 0 <= at.c - d < NB

        MIDDLE = NCH // 2
        DST_BANKS = len(BANKS) // 3

        def table_bank(g):
            k, js = BANKS[g]
            table = (dst_t, src_t, wgt_t)[k]
            return (table[:, 0:NB, js[0]:js[-1] + 1].rearrange("p b j -> p j b"),
                    ps[g % 8][:, 0:len(js) * NB].rearrange("p (j b) -> p j b", j=len(js)))

        def tables_done(eng):
            eng.wait_ge(s_tab, DST_BANKS)
            eng.wait_ge(s_tab_a, len(BANKS) - DST_BANKS)

        LOW_V = 4
        NORM_STEPS, ROUTE_STEPS = 6, 8
        NEWTON = 2 + 3 * 3
        KV = 11

        def flagged(eng):
            eng.wait_ge(s_flag, 7)
            return eng.value_load(flag_i[0:1, 0:1], min_val=0, max_val=1)

        def load_rest(sp, flag, layer, b):
            with sp.If(flag == 1):
                sp.dma_start(rest[layer][b.par], t_rest[layer][bass.ds(b.times(P), P), :]).then_inc(s_rest[layer][b.par], 16)
            with sp.Else():
                sp.sem_inc(s_rest[layer][b.par], 16)
            sp.sem_inc(go_sp)

        block = ctx.enter_context(nc.Block())

        @block.sync
        def _(sp):
            sp.dma_start(first_i[:, :], firsts).then_inc(s_first, 16)
            sp.dma_start(dsts, dstrun).then_inc(s_dst, 16)

            def load_x(n):
                sp.sem_inc(go_sp)
                sp.dma_start(xin[n.par], xpad[bass.ds(n.times(CH * P), CH * P), :].rearrange("(t p) d -> p t d", p=P)).then_inc(p_ld[n.par], 16)

            def store_xn(n):
                sp.sem_inc(go_sp)
                sp.dma_start(t_xn[bass.ds(n.times(CH * P), CH * P), :].rearrange("(t p) d -> p t d", p=P), xno[n.par]).then_inc(p_st[n.par], 16)

            load_x(At(None, 0))
            load_x(At(None, 1))
            for dst, src in ((col[:, :], cols), (row[:, :], rows[0:1, :].broadcast_to([P, NROW])),
                             (wp_s[:, :, :], wp.rearrange("(k p) n -> p k n", p=P)),
                             (gw1_s[:, :, :], gw1.rearrange("(k p) n -> p k n", p=P)),
                             (wf1_s[:, :, :], wf1.rearrange("(k p) n -> p k n", p=P)),
                             (wf2_s[:, :, :], wf2.rearrange("(k p) n -> p k n", p=P)),
                             (b2e_s[:, :], b2e), (gw0_s, gw0.rearrange("(k p) n -> p k n", p=P))):
                sp.dma_start(dst, src).then_inc(s_par, 16)
            with sp.Fori(0, NCH // 2 - 1) as i:
                for q in range(2):
                    n = At(i, 2 + q)
                    after(sp, p_xn, n - 2, CH)
                    load_x(n)
                    after(sp, p_lo, n - 2)
                    store_xn(n - 2)
            for n in (At(None, NCH - 2), At(None, NCH - 1)):
                after(sp, p_lo, n)
                store_xn(n)
            for q in range(2):
                sp.wait_ge(p_st[q], 16 * (NCH // 2))

            flag = flagged(sp)

            def general(layer):
                width = (D, PJ)[layer]
                with sp.If(flag == 1):
                    sp.wait_ge(s_zero, 1)
                    with sp.Fori(0, NB + 1) as i:
                        sp.dma_start(t_rest[layer][bass.ds(i * P, P), :], zero[:, 0:width]).then_inc(k_zeroed, 16)
                    with sp.Fori(0, ER) as r:
                        with sp.If(r > 0):
                            sp.wait_ge(k_scatter, r * 16 + 16 * ER * layer)
                            sp.sem_inc(go_sp)
                        with sp.Else():
                            sp.sem_inc(go_sp)
                        for k in range(3):
                            sp.dma_start(k_cols[:, k:k + 1], edges[bass.ds(r, 1), k * P:(k + 1) * P].rearrange("a k -> k a")).then_inc(k_in, 16)
                        sp.dma_start(k_row, edges[bass.ds(r, 1), P:2 * P].broadcast_to([P, P])).then_inc(k_in, 16)
                sp.sem_inc(go_sp)

            general(0)
            sp.wait_ge(s_zero, 4)

            def body(at):
                if has(at, 0):
                    b, q = at, at.par
                    after(sp, s_x0, b - 2)
                    sp.sem_inc(go_sp)
                    after(sp, s_T, b - 2)
                    after(sp, s_agg, b - 2)
                    sp.sem_inc(go_sp)
                    sp.dma_start(xb[q][:, :], xpad[bass.ds(b.times(P), P), :]).then_inc(s_xb[q], 16)
                    sp.sem_inc(go_sp)
                    sp.dma_start(xnb[q], t_xn[bass.ds(b.times(P), P), :]).then_inc(s_xb[q], 16)
                    load_rest(sp, flag, 0, b)
                if has(at, 3):
                    b, q = at - 3, (at - 3).par
                    after(sp, s_acc, b, NE + 1)
                    sp.sem_inc(go_sp)
                    sp.dma_start(t_x1[bass.ds(b.times(P), P), :], acc[q][:, :]).then_inc(s_x1st[q], 16)
                    after(sp, s_hT, b)
                    sp.sem_inc(go_sp)
                    sp.dma_start(t_ht[bass.ds(b.times(P), P), :], hT[q][:, :]).then_inc(s_htst[q], 16)
                    after(sp, s_hp, b)
                    sp.sem_inc(go_sp)
                    sp.dma_start(t_hp[bass.ds(b.times(P), P), :], hp_s[q][:, :]).then_inc(s_hpst[q], 16)
            drive(sp, body, S0)
            for q in range(2):
                for s in (s_x1st, s_htst, s_hpst):
                    sp.wait_ge(s[q], 16 * (NB // 2))

            sp.wait_ge(s_sum, NB * WROWS)
            general(1)
            sp.wait_ge(s_zero, 6)

            def body1(at):
                if has(at, 0):
                    b, q = at, at.par
                    after(sp, u_x2, b - 2)
                    sp.sem_inc(go_sp)
                    after(sp, u_gnn, b - 2)
                    after(sp, u_agg, b - 2)
                    sp.sem_inc(go_sp)
                    sp.dma_start(xb[q][:, :], t_x1[bass.ds(b.times(P), P), :]).then_inc(u_in[q], 16)
                    sp.sem_inc(go_sp)
                    sp.dma_start(hT[q][:, :], t_ht[bass.ds(b.times(P), P), :]).then_inc(u_in[q], 16)
                    load_rest(sp, flag, 1, b)
                if has(at, 1):
                    b, q = at - 1, (at - 1).par
                    after(sp, u_base, b)
                    sp.sem_inc(go_sp)
                    sp.dma_start(t_base[bass.ds(b.times(P), P), :], acc[q][:, :]).then_inc(u_bst[q], 16)
            drive(sp, body1, S1)

            def rows_of(table, n):
                return table[n * CH * P:(n + 1) * CH * P, :].rearrange("(t p) d -> p t d", p=P)

            for q in range(2):
                sp.wait_ge(u_bst[q], 16 * (NB // 2))
            sp.wait_ge(u_agg, NB)
            sp.wait_ge(u_y, NB)
            sp.wait_ge(u_idx, NB)
            sp.wait_ge(u_oh, GRP * NB)
            for n in range(NCH + NBUF):
                k = n % NBUF
                if n >= NBUF:
                    sp.wait_ge(f_out, (n - NBUF + 1) * CH)
                    sp.dma_start(rows_of(out, n - NBUF), fbuf[k]).then_inc(f_io[k], 16)
                    if n < NCH:
                        sp.wait_ge(f_io[k], 32 * (n // NBUF))
                if n < NCH:
                    sp.dma_start(fbuf[k], rows_of(t_base, n)).then_inc(f_io[k], 16)
            for k in range(NBUF):
                sp.wait_ge(f_io[k], 32 * (NCH // NBUF))

        @block.gpsimd
        def _(gp):
            gp.iota(iota_i[:, :], [[1, P]], base=0, channel_multiplier=0).then_inc(s_iota, 1)
            gp.iota(part_i[:, :], [[0, 1]], base=0, channel_multiplier=1).then_inc(s_iota, 1)
            gp.iota(thr_i[:, :], [[P, NB + 1]], base=0, channel_multiplier=0).then_inc(s_iota, 1)
            gp.iota(tri_i[:, :, :], [[-1, NE], [1, NE]], base=0, channel_multiplier=0).then_inc(s_iota, 1)
            gp.wait_ge(s_row, 3)
            for j in range(WROWS):
                gp.indirect_dma_start(win[:, j, :], None, edges, bass.IndirectOffsetOnAxis(ap=rowi[:, j:j + 1], axis=0)).then_inc(s_win, 16)
            with gp.Fori(0, (NCH - LOW_V) // 2) as i:
                for q in range(2):
                    n = At(i, LOW_V + q)
                    after(gp, p_hi, n)
                    gp.sem_inc(go_gp)
                    gp.tensor_tensor(xno[n.par][:, :, D:2 * D], fch[n.par], xno[n.par][:, :, 0:D], ALU.subtract).then_inc(p_lo, 1)
            tables_done(gp)
            for q in range(2):
                gp.wait_ge(p_st[q], 16 * (NCH // 2))
            flag = flagged(gp)

            def general(layer):
                table = (t_xn, t_hp)[layer]
                width = (D, PJ)[layer]
                with gp.If(flag == 1):
                    gp.wait_ge(k_zeroed, 16 * (NB + 1) * (layer + 1))
                    with gp.Fori(0, ER) as r:
                        gp.wait_ge(k_in, r * 64 + 64 * (ER * layer + 1))
                        gp.sem_inc(go_gp)
                        gp.indirect_dma_start((k_got16, k_got[:, 0:width])[layer], None, table, bass.IndirectOffsetOnAxis(ap=k_cols[:, 0:1], axis=0)).then_inc(k_gather, 16)
                        gp.wait_ge(k_v, r * KV + KV * (ER * layer + 1))
                        gp.sem_inc(go_gp)
                        gp.indirect_dma_start(t_rest[layer], bass.IndirectOffsetOnAxis(ap=k_ix[:, 0:1], axis=0), k_out[:, 0:width], None,
                                              compute_op=ALU.add).then_inc(k_scatter, 16)
                        gp.wait_ge(k_scatter, r * 16 + 16 * (ER * layer + 1))
                        gp.sem_inc(go_gp)
                gp.sem_inc(go_gp)

            general(0)
            gp.tensor_copy(idx[:, 0, :], src_t[:, 0, :]).then_inc(s_idx, 1)

            def body(at):
                if not has(at, 0):
                    return
                b, q = at, at.par
                after(gp, s_idx, b)
                for j in range(WROWS):
                    if j == WROWS // 2 and (at.i is not None or at.c + 1 < NB):
                        after(gp, s_sum, b - 1, WROWS)
                        gp.tensor_copy(idx[:, 1 - q, :], src_t[:, bass.ds((b + 1).times(1), 1), :].rearrange("p a j -> p (a j)")).then_inc(s_idx, 1)
                    after(gp, s_sum, b - 1, WROWS, j + 1 - WROWS)
                    gp.sem_inc(go_gp)
                    gp.indirect_dma_start(gb16[:, j, :], None, t_xn, bass.IndirectOffsetOnAxis(ap=idx[:, q, j:j + 1], axis=0)).then_inc(g_in[j], 16)
            drive(gp, body, S0)

            gp.wait_ge(s_idx, NB + 1)
            for q in range(2):
                gp.wait_ge(s_hpst[q], 16 * (NB // 2))
            general(1)
            gp.tensor_copy(idx[:, 0, :], src_t[:, 0, :]).then_inc(u_idx, 1)

            def has_earlier(b):
                return b.i is not None or b.c > 0

            gp.wait_ge(s_row, 10)

            def body1(at):
                if not has(at, 0):
                    return
                b, q = at, at.par
                after(gp, u_idx, b)
                for j in range(WROWS):
                    if j == WROWS // 2 + 2 and has_earlier(b):
                        gp.sem_inc(go_gp)
                        extra = gp.value_load(extra_i[0:1, 0, bass.ds(b.times(1), 1)], min_val=0, max_val=WROWS - FIXED)
                    if j == WROWS // 2 and (at.i is not None or at.c + 1 < NB):
                        after(gp, u_sum, b - 1, WROWS)
                        gp.tensor_copy(idx[:, 1 - q, :], src_t[:, bass.ds((b + 1).times(1), 1), :].rearrange("p a j -> p (a j)")).then_inc(u_idx, 1)
                    after(gp, u_sum, b - 1, WROWS, j + 1 - WROWS)
                    gp.sem_inc(go_gp)

                    def gather():
                        gp.indirect_dma_start(gbuf[:, j, 0:PJ], None, t_hp, bass.IndirectOffsetOnAxis(ap=idx[:, q, j:j + 1], axis=0)).then_inc(g_in[j], 16)

                    if j < FIXED or not has_earlier(b):
                        gather()
                    else:
                        with gp.If(extra > j - FIXED):
                            gather()
            drive(gp, body1, S1)

        @block.vector
        def _(v):
            v.wait_ge(s_iota, 4)
            v.memset(ones[:, :], 1.0).then_inc(s_const, 1)
            v.memset(src_t[:, NB, :], 0).then_inc(s_const, 1)
            v.memset(dst_t[:, NB, :], -1.0).then_inc(s_const, 1)
            v.memset(wgt_t[:, NB, :], 0.0).then_inc(s_const, 1)
            v.tensor_copy(iota_f[:, :], iota_i[:, :]).then_inc(s_const, 1)
            v.tensor_copy(part_f[:, :], part_i[:, :]).then_inc(s_const, 1)
            v.tensor_copy(thr_f[:, :], thr_i[:, :]).then_inc(s_const, 1)
            v.tensor_scalar(tri[:, :, :], tri_i[:, :, :], 0.0, None, ALU.is_lt).then_inc(s_const, 1)
            v.wait_ge(s_const, 8)
            v.tensor_scalar(ident[:, :], iota_f[:, :], part_f[:, 0:1], None, ALU.is_equal).then_inc(s_const, 1)
            v.tensor_scalar(ident16[:, :], iota_f[:, :], part_f[:, 0:1], None, ALU.is_equal).then_inc(s_const, 1)
            v.tensor_copy(iota_b[:, :], iota_f[:, :]).then_inc(s_const, 1)
            v.wait_ge(s_first, 16)
            v.tensor_copy(first_f[:, :], first_i[:, :]).then_inc(s_cnt, 1)
            v.wait_ge(s_cnt, 1)
            cmp = oh[0][:, 0:11, :].rearrange("p j n -> p (j n)")[:, 0:(NB + 1) * CC].rearrange("p (b c) -> p b c", c=CC)
            v.tensor_tensor(cmp, first_f[:, :].unsqueeze(1).broadcast_to([P, NB + 1, CC]),
                            thr_f[:, :].unsqueeze(2).broadcast_to([P, NB + 1, CC]), ALU.is_lt).then_inc(s_cnt, 1)
            v.wait_ge(s_cnt, 2)
            v.tensor_reduce(cnt[:, :], cmp, AX.X, ALU.add).then_inc(s_cnt, 1)
            v.wait_ge(s_cntp, 1)
            v.tensor_scalar(r0[:, :], ps[0][0:NB, 0:1], -1.0, 0.0, ALU.add, ALU.max).then_inc(s_row, 1)
            v.wait_ge(s_row, 1)
            v.tensor_scalar(r1[:, :], r0[:, :], float(ER - WROWS), None, ALU.min).then_inc(s_row, 1)
            v.wait_ge(s_row, 2)
            v.tensor_scalar(rowi[:, :], iota_f[0:NB, 0:WROWS], r1[:, 0:1], None, ALU.add).then_inc(s_row, 1)

            v.tensor_scalar(unused[:, :], r1[:, :], float(FIXED), ps[0][0:NB, 1:2], ALU.add, ALU.subtract).then_inc(s_row, 1)
            v.tensor_scalar(r0[:, :], part_f[0:NB, :], 0.0, None, ALU.is_equal).then_inc(s_row, 1)
            v.tensor_scalar(to_here, iota_f[0:NB, 0:NB], part_f[0:NB, 0:1], None, ALU.is_ge).then_inc(s_row, 1)
            v.wait_ge(s_row, 6)
            for k in range(WROWS - FIXED):
                v.tensor_scalar(edged[:, k:k + 1], unused[:, :], float(-k), r0[:, 0:1], ALU.is_lt, ALU.max).then_inc(s_row, 1)
            v.wait_ge(s_cntp, 2)
            rows_ps = ps[1][0:1, 0:3 * P].rearrange("a (r b) -> a r b", b=P)[:, :, 0:NB]
            v.tensor_copy(extra_i[:, 0:1, :], rows_ps[:, 0:1, :]).then_inc(s_row, 1)
            v.tensor_scalar(extra_i[:, 1:3, :], rows_ps[:, 1:3, :], 16.0, float(16 * NB), ALU.mult, ALU.add).then_inc(s_row, 1)

            v.memset(bad[:, :], 0.0).then_inc(s_flag, 1)
            v.wait_ge(s_flag, 1)
            v.tensor_scalar(bad[0:NB, 0:1], r1[:, :], float(WROWS), ps[0][0:NB, 1:2], ALU.add, ALU.is_lt).then_inc(s_flag, 1)
            v.memset(zero[:, :], 0.0).then_inc(s_zero, 1)

            def chunk_stats(n):
                q = n.par
                landed(v, p_ld, n)
                for t in range(CH):
                    v.bn_stats(st[:, t, :], xin[q][:, t, :]).then_inc(p_stat, 1)
                after(v, p_stat, n, 2 * CH + 1, -CH - 1)
                v.sem_inc(go_v)
                for t in range(CH):
                    v.bn_aggr(mvc[q][:, t, :], st[:, t, :]).then_inc(p_stat, 1)
                after(v, p_stat, n, 2 * CH + 1, -1)
                v.tensor_scalar(rs[:, q, :], mvc[q][:, :, 1], EPS, None, ALU.add).then_inc(p_stat, 1)
                after(v, p_stat, n, 2 * CH + 1)
                after(v, p_rs, n - 2)
                v.reciprocal(inv[:, q, :], rs[:, q, :]).then_inc(p_iv, 1)

            def chunk_norm(n):
                q = n.par
                after(v, p_rs, n)
                after(v, p_lo, n - 2)
                for t in range(CH):
                    v.tensor_scalar(fch[q][:, t, :], xin[q][:, t, :], mvc[q][:, t, 0:1], rs[:, q, t:t + 1], ALU.subtract, ALU.mult).then_inc(p_xn, 1)

            def chunk_step(n):
                chunk_stats(n + 1)
                if n.i is None and n.c < LOW_V:
                    after(v, p_hi, n)
                    v.tensor_tensor(xno[n.par][:, :, D:2 * D], fch[n.par], xno[n.par][:, :, 0:D], ALU.subtract).then_inc(p_lo, 1)
                chunk_norm(n + 1)

            chunk_stats(At(None, 0))
            chunk_norm(At(None, 0))
            for n in range(5):
                chunk_step(At(None, n))
            with v.Fori(0, (MIDDLE - 5) // 2) as i:
                for q in range(2):
                    chunk_step(At(i, 5 + q))

            v.wait_ge(s_dst, 16)
            v.tensor_tensor(order, dsts[:, 0:ER], dsts[:, 1:ER + 1], ALU.is_gt).then_inc(s_flag, 1)
            v.wait_ge(s_flag, 3)
            v.tensor_reduce(bad[:, 1:2], order, AX.X, ALU.add).then_inc(s_flag, 1)
            v.wait_ge(s_flag, 4)
            v.tensor_tensor(bad[:, 2:3], bad[:, 0:1], bad[:, 1:2], ALU.add).then_inc(s_flag, 1)
            v.wait_ge(s_flagp, 1)
            v.tensor_scalar(flag_i[:, :], ps[0][:, 2:3], 0.0, None, ALU.is_gt).then_inc(s_flag, 1)
            v.tensor_scalar(away[:, :], ps[0][:, 2:3], 0.0, float(1 << 20), ALU.is_gt, ALU.mult).then_inc(s_flag, 1)

            v.wait_ge(s_win, 16 * WROWS)
            blk0 = sm[0:NB, 0:1]
            v.tensor_scalar(blk0, part_f[0:NB, 0:1], float(P), None, ALU.mult).then_inc(s_winf, 1)
            v.wait_ge(s_winf, 1)
            v.tensor_scalar(winf[0], win[:, :, P:2 * P], blk0, None, ALU.subtract).then_inc(s_winf, 1)
            for g, (k, js) in enumerate(BANKS[:DST_BANKS]):
                v.wait_ge(s_tp, g + 1)
                to, of = table_bank(g)
                v.tensor_scalar(to, of, away[:, 0:1], None, ALU.subtract).then_inc(s_tab, 1)

            with v.Fori(0, (NCH - 1 - MIDDLE) // 2) as i:
                for q in range(2):
                    chunk_step(At(i, MIDDLE + q))

            v.wait_ge(s_par, 16 * 8)

            def onehot(b, g):
                q = b.par
                if g == 0:
                    after(v, s_sum, b - 2, WROWS)
                j0, size = GROUP[g][0], len(GROUP[g])
                d = dst_t[:, bass.ds(b.times(1), 1), j0:j0 + size].rearrange("p a j -> p (a j)")
                v.tensor_tensor(oh16[q][:, j0:j0 + size, :], iota_b[:, :].unsqueeze(1).broadcast_to([P, size, P]),
                                d.unsqueeze(2).broadcast_to([P, size, P]), ALU.is_equal).then_inc(s_oh, 1)

            tables_done(v)
            v.wait_ge(s_tp, len(BANKS))
            for q in range(2):
                v.wait_ge(p_st[q], 16 * (NCH // 2))
            for q in range(2):
                v.memset(rest[0][q], 0.0).then_inc(s_zero, 1)
            v.memset(var2[:, :], 1.0).then_inc(s_zero, 1)
            flag = flagged(v)

            def general(layer):
                width = (D, PJ)[layer]
                dst_f, before, ok, here, off, to, dump = (k_f[:, k:k + 1] for k in range(7))
                with v.If(flag == 1):
                    v.tensor_scalar(k_low, iota_f[:, :], part_f[:, 0:1], None, ALU.is_lt).then_inc(k_low_ready, 1)
                    v.tensor_scalar(dump, part_f[:, 0:1], float(NB * P), None, ALU.add).then_inc(k_low_ready, 1)
                    v.wait_ge(k_low_ready, 2 * layer + 2)
                    with v.Fori(0, ER) as r:
                        v.wait_ge(k_in, r * 64 + 64 * (ER * layer + 1))
                        n = [0]

                        def link(ins):
                            n[0] += 1
                            ins.then_inc(k_v, 1)
                            v.wait_ge(k_v, r * KV + (KV * ER * layer + n[0]))

                        link(v.tensor_copy(dst_f, k_cols[:, 1:2]))
                        link(v.tensor_scalar(k_same, k_row, dst_f, None, ALU.is_equal))
                        link(v.tensor_tensor(k_wgt, k_same, k_low, ALU.mult))
                        link(v.tensor_reduce(before, k_wgt, AX.X, ALU.add))
                        link(v.tensor_scalar(ok, before, 0.0, None, ALU.is_equal))
                        link(v.tensor_scalar(here, dst_f, float(N), ok, ALU.is_lt, ALU.mult))
                        link(v.tensor_scalar(off, dst_f, dump, None, ALU.subtract))
                        link(v.tensor_scalar(to, off, here, dump, ALU.mult, ALU.add))
                        link(v.tensor_copy(k_ix[:, :], to))
                        if layer:
                            link(v.tensor_scalar(k_wgt, k_same, k_cols[:, 2:3].bitcast(f32), None, ALU.mult))
                        else:
                            link(v.tensor_copy(k_wgt16, k_same))
                        v.wait_ge(k_sum, r + (ER * layer + 1))
                        link(v.tensor_copy(k_out[:, 0:width], ps[0][:, 0:width]))
                v.sem_inc(go_v)

            general(0)
            for g in range(GRP):
                onehot(At(None, 0), g)

            v.wait_ge(s_nrm, 1)
            v.tensor_copy(bnd[:, 0:2], nrm[:, 0:2]).then_inc(s_scl, 1)
            v.tensor_scalar(bnd[:, 2:3], nrm[:, 3:4], float(D) ** 0.5, nrm[:, 4:5], ALU.mult, ALU.add).then_inc(s_scl, 1)
            v.wait_ge(s_scl, 2)
            v.tensor_scalar(bnd[:, 3:4], bnd[:, 2:3], nrm[:, 0:1], nrm[:, 2:3], ALU.mult, ALU.add).then_inc(s_scl, 1)
            v.wait_ge(s_scl, 3)
            v.tensor_scalar(bnd[:, :], bnd[:, :], 2.0 ** -40, None, ALU.max).then_inc(s_scl, 1)
            v.wait_ge(s_scl, 4)
            v.tensor_scalar(bnd_i[:, :], bnd[:, :].bitcast(i32), 0x7f800000, None, ALU.bitwise_and).then_inc(s_scl, 1)
            v.wait_ge(s_scl, 5)
            v.tensor_scalar(scl_i[:, :], bnd_i[:, :], -1.0, float((127 + 127 + 14) << 23), ALU.mult, ALU.add).then_inc(s_scl, 1)
            v.wait_ge(s_scl, 6)
            v.tensor_tensor(prod[:, :], scl[:, 0:2], scl[:, 2:4], ALU.mult).then_inc(s_scl, 1)
            v.wait_ge(s_scl, 7)
            v.reciprocal(unscl[:, :], prod[:, :]).then_inc(s_scl, 1)
            v.wait_ge(s_scl, 8)
            for n, c in enumerate(reversed(range(WCH))):
                w = 2 * c // WCH
                v.wait_ge(s_whi, n + 1)
                v.scalar_tensor_tensor(part(c, 1), raw(c), scl[:, w:w + 1], part(c, 0), ALU.mult, ALU.subtract).then_inc(s_wlo, 1)

            def body(at):
                A, B, C, Dd = has(at, 0), has(at, 1), has(at, 2), has(at, 3)
                nxt = at + 1
                N1 = at.i is not None or at.c + 1 < NB
                b, c, d = at - 1, at - 2, at - 3
                def low(e):
                    k = e % 2
                    after(v, s_hh, c, NE, e + 1 - NE)
                    v.scalar_tensor_tensor(hp16[k][1], hs[k][:, :, :], scl[:, 3:4], hp16[k][0], ALU.mult, ALU.subtract).then_inc(s_hl, 1)

                def accumulate(e):
                    yp = ps[(3, 7)[(e + 1) % 2]][:, 0:D]
                    after(v, s_y, c, NE + 1, e + 1 - NE)
                    if e < 0:
                        landed(v, s_x1st, c - 2)
                        v.tensor_tensor(acc[c.par][:, :], yp, x0[c.par][:, :], ALU.add).then_inc(s_acc, 1)
                    else:
                        after(v, s_acc, c, NE + 1, e - NE)
                        v.scalar_tensor_tensor(acc[c.par][:, :], yp, wfs[c.par][:, e:e + 1], acc[c.par][:, :], ALU.mult, ALU.add).then_inc(s_acc, 1)

                if Dd:
                    after(v, s_acc, d, NE + 1)
                    v.bn_stats(std[:, :], acc[d.par][:, :]).then_inc(s_dst3, 1)
                    after(v, s_dst3, d, 2, -1)
                    v.sem_inc(go_v)
                    v.bn_aggr(mvd[:, :], std[:, :]).then_inc(s_dst3, 1)
                    after(v, s_dst3, d, 2, 0)
                    v.tensor_scalar(var2[:, 1:2], mvd[:, 1:2], EPS, None, ALU.add).then_inc(s_var, 1)
                if B:
                    after(v, s_gnn, b)
                    landed(v, s_xb, b, 32)
                    after(v, s_acc, b - 2, NE + 1, -NE)
                    v.scalar_tensor_tensor(x0[b.par][:, :], ps[4][:, 0:D], 0.0, xb[b.par][:, :], ALU.max, ALU.add).then_inc(s_x0, 1)
                    after(v, s_x0, b)
                    v.bn_stats(st[:, 0, :], x0[b.par][:, :]).then_inc(s_bst, 1)
                    after(v, s_bst, b, NORM_STEPS, -5)
                    v.sem_inc(go_v)
                    v.bn_aggr(mv[:, 0, :], st[:, 0, :]).then_inc(s_bst, 1)
                if C:
                    low(0)
                if B:
                    after(v, s_bst, b, NORM_STEPS, -4)
                    v.tensor_scalar(sm[:, 0:1], mv[:, 0, 1:2], EPS, None, ALU.add).then_inc(s_bst, 1)
                    after(v, s_bst, b, NORM_STEPS, -3)
                    v.reciprocal(sm[:, 1:2], sm[:, 0:1]).then_inc(s_bst, 1)
                    after(v, s_bst, b, NORM_STEPS, -2)
                    v.tensor_scalar(sm[:, 2:3], mv[:, 0, 1:2], sm[:, 1:2], EPS, ALU.mult, ALU.add).then_inc(s_bst, 1)
                    after(v, s_bst, b, NORM_STEPS, -1)
                    v.tensor_tensor(var2[:, 0:1], sm[:, 0:1], sm[:, 2:3], ALU.mult).then_inc(s_bst, 1)
                if C:
                    accumulate(-1)
                    low(1)
                if B or Dd:
                    if at.i is None and at.c == 1:
                        v.wait_ge(s_zero, 4)
                    if B:
                        after(v, s_bst, b, NORM_STEPS, 0)
                    if Dd:
                        after(v, s_var, d)
                    v.tensor_scalar(var2_i[:, :], var2[:, :].bitcast(i32), 1, None, ALU.arith_shift_right).then_inc(s_rsq, 1)
                    after(v, s_rsq, b, NEWTON, 1 - NEWTON)
                    if C:
                        after(v, s_xn, b - 1)
                    after(v, s_dn, d - 1)
                    v.tensor_scalar(rsq_i[:, :], var2_i[:, :], -1.0, float(0x5f3759df), ALU.mult, ALU.add).then_inc(s_rsq, 1)
                    for n in range(3):
                        after(v, s_rsq, b, NEWTON, 3 * n + 2 - NEWTON)
                        v.tensor_tensor(nwt[:, :], var2[:, :], rsq, ALU.mult).then_inc(s_rsq, 1)
                        after(v, s_rsq, b, NEWTON, 3 * n + 3 - NEWTON)
                        v.scalar_tensor_tensor(nwt[:, :], nwt[:, :], -0.5, rsq, ALU.mult, ALU.mult).then_inc(s_rsq, 1)
                        after(v, s_rsq, b, NEWTON, 3 * n + 4 - NEWTON)
                        v.scalar_tensor_tensor(rsq, nwt[:, :], 1.5, rsq, ALU.add, ALU.mult).then_inc(s_rsq, 1)
                    after(v, s_rsq, b, NEWTON, 0)
                if B:
                    after(v, s_xnTp, b - 1)
                    v.tensor_scalar(xn[:, :], x0[b.par][:, :], mv[:, 0, 0:1], rsq[:, 0:1], ALU.subtract, ALU.mult).then_inc(s_xn, 1)
                if Dd:
                    after(v, s_dTp, d - 1)
                    v.tensor_scalar(xnd, acc[d.par][:, :], mvd[:, 0:1], rsq[:, 1:2], ALU.subtract, ALU.mult).then_inc(s_dn, 1)

                if C:
                    low(2)
                    accumulate(0)
                if N1:
                    onehot(nxt, 0)
                if C:
                    low(3)
                    accumulate(1)
                if B:
                    after(v, s_xh, b)
                    v.scalar_tensor_tensor(xs[b.par][1], xnT[b.par][:, :, :], scl[:, 2:3], xs[b.par][0], ALU.mult, ALU.subtract).then_inc(s_xl, 1)
                    after(v, s_lgp, b)
                    v.tensor_tensor(lg[:, :], ps[4][:, D:D + NE], row[:, R_BR0:R_BR0 + NE], ALU.add).then_inc(s_rt, 1)
                    after(v, s_rt, b, ROUTE_STEPS, -7)
                    lj = lg[:, :].unsqueeze(1).broadcast_to([P, NE, NE])
                    le = lg[:, :].unsqueeze(2).broadcast_to([P, NE, NE])
                    v.tensor_tensor(gt[:, :, :], lj, le, ALU.is_gt).then_inc(s_rt, 1)
                    v.tensor_tensor(eq[:, :, :], lj, le, ALU.is_equal).then_inc(s_rt, 1)
                    after(v, s_rt, b, ROUTE_STEPS, -5)
                    v.tensor_tensor(eq[:, :, :], eq[:, :, :], tri[:, :, :], ALU.mult).then_inc(s_rt, 1)
                    after(v, s_rt, b, ROUTE_STEPS, -4)
                    v.tensor_tensor(gt[:, :, :], gt[:, :, :], eq[:, :, :], ALU.add).then_inc(s_rt, 1)
                    after(v, s_rt, b, ROUTE_STEPS, -3)
                    v.tensor_reduce(rank[:, :], gt[:, :, :], AX.X, ALU.add).then_inc(s_rt, 1)
                    after(v, s_rt, b, ROUTE_STEPS, -2)
                    v.scalar_tensor_tensor(gt[:, 0, :], rank[:, :], 2.0, lg[:, :], ALU.is_lt, ALU.mult).then_inc(s_rt, 1)
                    after(v, s_rt, b, ROUTE_STEPS, -1)
                    v.tensor_reduce(sm[:, 5:6], gt[:, 0, :], AX.X, ALU.add).then_inc(s_rt, 1)
                    after(v, s_rt, b, ROUTE_STEPS, 0)
                    after(v, s_ex, b - 1)
                    v.scalar_tensor_tensor(dif[:, :], sm[:, 5:6].broadcast_to([P, NE]), -0.5, lg[:, :], ALU.mult, ALU.add).then_inc(s_dl, 1)
                if C:
                    low(4)
                    accumulate(2)
                if Dd:
                    after(v, s_hT, d)
                    after(v, s_hpT, d - 1)
                    v.tensor_tensor(hq, hT[d.par][:, :], hT[d.par][:, :], ALU.mult).then_inc(s_hq, 1)
                if B:
                    after(v, s_ex, b)
                    v.tensor_scalar(exs[:, :], ex[:, :], 0.5, 0.5, ALU.mult, ALU.add).then_inc(s_exs, 1)
                    after(v, s_exs, b)
                    after(v, s_acc, b - 2, NE + 1)
                    v.scalar_tensor_tensor(wf[b.par][:, :], rank[:, :], 2.0, exs[:, :], ALU.is_lt, ALU.mult).then_inc(s_wf, 1)
                    after(v, s_wf, b, 2, -1)
                    v.tensor_scalar(wfs[b.par][:, :], wf[b.par][:, :], unscl[:, 1:2], None, ALU.mult).then_inc(s_wf, 1)
                if C:
                    low(5)
                    accumulate(3)
                if N1:
                    onehot(nxt, 1)
                if C:
                    low(6)
                    accumulate(4)
                    low(7)
                    accumulate(5)
                    accumulate(6)
                if A:
                    after(v, s_sum, at, WROWS)
                    after(v, s_T, at - 1)
                    landed(v, s_rest[0], at)
                    v.tensor_tensor(agg_s[:, :], ps[at.par][:, 0:D], rest[0][at.par], ALU.add).then_inc(s_agg, 1)
                if C:
                    accumulate(7)
            drive(v, body, S0)

            v.tensor_tensor(brow[:, :], row[0:1, R_GB1:R_GB1 + D], row[0:1, R_GB2:R_GB2 + D], ALU.add).then_inc(s_brow, 1)

            def onehot1(b, g):
                q = b.par
                if g == 0:
                    after(v, u_sum, b - 2, WROWS)
                j0, size = GROUP[g][0], len(GROUP[g])
                d = dst_t[:, bass.ds(b.times(1), 1), j0:j0 + size].rearrange("p a j -> p (a j)")
                w = wgt_t[:, bass.ds(b.times(1), 1), j0:j0 + size].rearrange("p a j -> p (a j)")
                o = oh[q][:, j0:j0 + size, :]
                v.tensor_tensor(o, iota_f[:, :].unsqueeze(1).broadcast_to([P, size, P]), d.unsqueeze(2).broadcast_to([P, size, P]), ALU.is_equal).then_inc(u_eq, 1)
                after(v, u_eq, b, GRP, g + 1 - GRP)
                v.tensor_tensor(o, o, w.unsqueeze(2).broadcast_to([P, size, P]), ALU.mult).then_inc(u_oh, 1)

            v.wait_ge(s_sum, NB * WROWS)
            v.wait_ge(s_oh, GRP * (NB + 1))
            v.wait_ge(s_hp, NB)
            general(1)
            for q in range(2):
                v.memset(rest[1][q], 0.0).then_inc(s_zero, 1)
            v.wait_ge(s_zero, 6)
            for g in range(GRP):
                onehot1(At(None, 0), g)

            def body1(at):
                B, C = has(at, 1), has(at, 2)
                N1 = at.i is not None or at.c + 1 < NB
                b, c = at - 1, at - 2
                if B:
                    after(v, u_sum, b, WROWS)
                    after(v, u_sqTp, b - 1)
                    landed(v, s_rest[1], b)
                    v.tensor_tensor(agg_s[:, 0:PJ], ps[b.par][:, 0:PJ], rest[1][b.par], ALU.add).then_inc(u_agg, 1)
                if N1:
                    onehot1(at + 1, 0)
                if B:
                    after(v, u_gnn, b)
                    landed(v, u_in, b, 32)
                    v.tensor_tensor(x0[b.par][:, :], ps[4][:, 0:D], xb[b.par][:, :], ALU.add).then_inc(u_x2, 1)
                    after(v, u_x2, b)
                    v.bn_stats(st[:, 0, :], x0[b.par][:, :]).then_inc(u_bst3, 1)
                    after(v, u_bst3, b, 3, -2)
                    v.sem_inc(go_v)
                    v.bn_aggr(mv[:, 0, :], st[:, 0, :]).then_inc(u_bst3, 1)
                    after(v, u_bst3, b, 3, -1)
                    v.tensor_scalar(sm[:, 0:1], mv[:, 0, 1:2], EPS, None, ALU.add).then_inc(u_bst3, 1)
                    after(v, u_bst3, b, 3, 0)
                    v.reciprocal(sm[:, 1:2], sm[:, 0:1]).then_inc(u_iv, 1)
                    after(v, u_r, b)
                    after(v, u_xnTp, b - 1)
                    v.tensor_scalar(xn[:, :], x0[b.par][:, :], mv[:, 0, 0:1], rb[:, 0:1], ALU.subtract, ALU.mult).then_inc(u_xn, 1)
                    after(v, u_xn, b)
                    landed(v, u_bst, b - 2)
                    v.tensor_tensor(acc[b.par][:, :], x0[b.par][:, :], xn[:, :], ALU.add).then_inc(u_base, 1)
                if N1:
                    onehot1(at + 1, 1)
                if C:
                    after(v, u_y, c)
                    after(v, u_wc, c)
                    v.tensor_scalar(yw[:, bass.ds(c.times(D), D)], ps[(3, 7)[c.par]][:, 0:D], wc[:, c.par:c.par + 1], None, ALU.mult).then_inc(u_yw, 1)
                if B:
                    after(v, u_wp, b)
                    after(v, u_yw, b - 2)
                    after(v, u_wts, b - 2)
                    v.tensor_tensor(wc[:, b.par:b.par + 1], ps[4][:, D:D + 1], row[:, R_BR1:R_BR1 + 1], ALU.add).then_inc(u_wc, 1)
                    after(v, u_wc, b)
                    v.tensor_copy(wts[:, bass.ds(b.times(1), 1)], wc[:, b.par:b.par + 1]).then_inc(u_wts, 1)
            drive(v, body1, S1 - 1)

            nf = [0]

            def link(ins):
                nf[0] += 1
                ins.then_inc(f_key, 1)
                v.wait_ge(f_key, nf[0])

            v.wait_ge(u_wts, NB)
            v.wait_ge(s_const, 11)
            link(v.tensor_scalar(equal, thr_f[:, 0:NB], part_f[:, 0:1], None, ALU.add))
            link(v.tensor_scalar(valid, equal, float(N), None, ALU.is_lt))
            link(v.tensor_scalar(cmpf, wts[:, 0:NB], 0.0, None, ALU.add))
            bits = cmpf.bitcast(i32)
            link(v.tensor_scalar(ki, bits, 31, 0x7fffffff, ALU.arith_shift_right, ALU.bitwise_and))
            link(v.tensor_tensor(kj, ki, bits, ALU.bitwise_xor))
            link(v.tensor_scalar(ki, kj, 16, None, ALU.arith_shift_right))
            link(v.tensor_copy(hi, ki))
            link(v.tensor_scalar(ki, kj, 0xffff, None, ALU.bitwise_and))
            link(v.tensor_copy(lo, ki))
            LOW = 65536.0
            link(v.scalar_tensor_tensor(hi, hi, LOW, valid, ALU.add, ALU.mult))
            link(v.tensor_scalar(hi, hi, LOW, None, ALU.subtract))
            digit, base, step, want, hstar, lstar = (fc[:, k:k + 1] for k in range(6))
            link(v.memset(want, float(KEEP)))
            link(v.memset(count[:, :], 0.0))
            totals = ps[0][:, 0:RADIX - 1]

            def search(key, least, done, star):
                link(v.memset(base, least))
                link(v.memset(step, float(RADIX) ** (DIGITS - 1)))
                with v.Fori(0, DIGITS) as i:
                    def step_done(k):
                        v.wait_ge(f_step, i * 6 + (6 * DIGITS * (done > 0) + k))

                    v.tensor_scalar(thr[:, :], iota_f[:, 1:RADIX], step, base, ALU.mult, ALU.add).then_inc(f_step, 1)
                    step_done(1)
                    v.tensor_tensor(ge, key.unsqueeze(1).broadcast_to([P, RADIX - 1, NB]), thr[:, :].unsqueeze(2).broadcast_to([P, RADIX - 1, NB]), ALU.is_ge).then_inc(f_step, 1)
                    step_done(2)
                    v.tensor_reduce(count[:, :], ge, AX.X, ALU.add).then_inc(f_cnt, 1)
                    v.wait_ge(f_tot, i + (done + 1))
                    v.tensor_scalar(thr[:, :], totals, want, 0.0, ALU.is_ge, ALU.add, accum_out=digit).then_inc(f_step, 1)
                    step_done(3)
                    v.tensor_scalar(digit, digit, step, None, ALU.mult).then_inc(f_step, 1)
                    step_done(4)
                    v.tensor_tensor(base, base, digit, ALU.add).then_inc(f_step, 1)
                    v.tensor_scalar(step, step, 1.0 / RADIX, None, ALU.mult).then_inc(f_step, 1)
                    step_done(6)
                link(v.tensor_copy(star, base))

            def wanted_less_above(key, star, done):
                v.tensor_scalar(cmpf, key, star, 0.0, ALU.is_gt, ALU.add, accum_out=count[:, 0:1]).then_inc(f_cnt, 1)
                v.wait_ge(f_tot, done + 1)
                link(v.tensor_tensor(want, want, ps[0][:, 0:1], ALU.subtract))

            search(hi, -32768.0, 0, hstar)
            body1(At(None, S1 - 1))
            wanted_less_above(hi, hstar, DIGITS)
            link(v.tensor_scalar(cmpf, hi, hstar, None, ALU.is_equal))
            link(v.scalar_tensor_tensor(lo, lo, 1.0, cmpf, ALU.add, ALU.mult))
            link(v.tensor_scalar(lo, lo, 1.0, None, ALU.subtract))
            search(lo, 0.0, DIGITS + 1, lstar)
            wanted_less_above(lo, lstar, 2 * DIGITS + 1)
            link(v.memset(scan[0], 0.0))
            link(v.memset(scan[1], 0.0))
            link(v.tensor_scalar(low_tri, iota_f[:, :], part_f[:, 0:1], None, ALU.is_gt))
            v.tensor_scalar(equal, lo, lstar, None, ALU.is_equal).then_inc(f_cnt, 1)
            v.wait_ge(f_tot, 2 * DIGITS + 3)
            link(v.tensor_copy(scan[0][:, P:P + NB], ps[0][:, P:P + NB]))
            link(v.tensor_tensor(before[:, 0:NB], ps[0][:, 0:NB], scan[0][:, P:P + NB], ALU.subtract))
            shift, k = 1, 0
            while shift < NB:
                link(v.tensor_tensor(scan[1 - k][:, P:P + NB], scan[k][:, P:P + NB], scan[k][:, P - shift:P - shift + NB], ALU.add))
                shift, k = 2 * shift, 1 - k
            link(v.tensor_tensor(before[:, 0:NB], before[:, 0:NB], scan[k][:, P:P + NB], ALU.add))
            link(v.scalar_tensor_tensor(equal, before[:, 0:NB], want, equal, ALU.is_lt, ALU.mult))
            link(v.scalar_tensor_tensor(msk, hi, hstar, equal, ALU.is_gt, ALU.add))
            link(v.scalar_tensor_tensor(msk, lo, lstar, msk, ALU.is_gt, ALU.add))

            v.wait_ge(u_yw, NB)
            with v.Fori(0, NCH // NBUF) as i:
                for q in range(NBUF):
                    v.wait_ge(f_io[q], i * 32 + 16)
                    for k in range(CH):
                        v.scalar_tensor_tensor(fbuf[q][:, k, :], yw[:, bass.ds(i * (NBUF * CH * D) + (q * CH + k) * D, D)],
                                               oh[0][:, 7, bass.ds(i * (NBUF * CH) + (q * CH + k), 1)],
                                               fbuf[q][:, k, :], ALU.mult, ALU.add).then_inc(f_out, 1)

        @block.scalar
        def _(a):
            def chunk_scale(n):
                after(a, p_iv, n)
                after(a, p_xn, n - 2, CH)
                a.activation(rs[:, n.par, :], inv[:, n.par, :], ACT.Sqrt).then_inc(p_rs, 1)
            def chunk_high(n):
                after(a, p_xn, n, CH)
                landed(a, p_st, n - 2)
                a.copy(xno[n.par][:, :, 0:D], fch[n.par]).then_inc(p_hi, 1)

            def chunk_step(n):
                chunk_high(n)
                chunk_scale(n + 1)

            chunk_scale(At(None, 0))
            for n in range(5):
                chunk_step(At(None, n))
            with a.Fori(0, (MIDDLE - 5) // 2) as i:
                for q in range(2):
                    chunk_step(At(i, 5 + q))
            a.wait_ge(s_win, 16 * WROWS)
            a.copy(winf[1], win[:, :, 0:P]).then_inc(s_srcf, 1)
            for g in range(DST_BANKS, len(BANKS)):
                a.wait_ge(s_tp, g + 1)
                to, of = table_bank(g)
                a.copy(to, of).then_inc(s_tab_a, 1)
            tables_done(a)

            def load_expert(e):
                one = bass.ds(e.times(1), 1)
                a.dma_start(w1e[:, one, :, :], wmoe1[one, :, :].rearrange("e (k p) h -> p e k h", p=P)).then_inc(s_w2, 16)
                a.dma_start(w2e[:, one, :, :], wmoe2[one, :, :].rearrange("e (t p) d -> p e t d", p=P)).then_inc(s_w2, 16)

            load_expert(At(None, 0))
            with a.Fori(0, (NCH - 1 - MIDDLE) // 2) as i:
                for q in range(2):
                    chunk_step(At(i, MIDDLE + q))
                    load_expert(At(i, 1 + q))
            chunk_high(At(None, NCH - 1))
            load_expert(At(None, NCH - MIDDLE))
            a.wait_ge(s_par, 16 * 8)

            a.wait_ge(s_w2, 2 * NE * 16)
            a.wait_ge(p_lo, NCH)
            waste = arena[:, WCH * WSZ:WCH * WSZ + gap].bitcast(f16)
            for k, of in enumerate((arena[:, 0:2 * gap], arena[:, 2 * gap:4 * gap], col[:, C_B1:C_B1 + NE * HT0],
                                    col[:, C_GAMMA:C_GAMMA + KD], col[:, C_BETA:C_BETA + KD])):
                if k:
                    a.wait_ge(s_sq, k)
                a.activation(waste[:, 0:of.shape[1]], of, ACT.Square, accum_out=sq[:, k:k + 1]).then_inc(s_sq, 1)
            a.wait_ge(s_sqp, 1)
            a.activation(nrm[:, :], ps[7][:, 0:5], ACT.Sqrt).then_inc(s_nrm, 1)
            a.wait_ge(s_scl, 8)
            for n, c in enumerate(reversed(range(WCH))):
                w = 2 * c // WCH
                if n >= 2:
                    a.wait_ge(s_wlo, n - 1)
                a.activation(part(c, 0), raw(c), ACT.Identity, scale=scl[:, w:w + 1]).then_inc(s_whi, 1)
            a.wait_ge(s_wlo, WCH)

            def body(at):
                B, C, Dd = has(at, 1), has(at, 2), has(at, 3)
                b, c, d = at - 1, at - 2, at - 3

                def gelu(e):
                    k = e % 2
                    for t in range(HT0):
                        if t == 0:
                            after(a, s_hps, c, NE, e + 1 - NE)
                            after(a, s_hl, c, NE, e - 1 - NE)
                        a.activation(hs[k][:, t, :], ps[5 + k][:, t * P:(t + 1) * P], ACT.Gelu,
                                     bias=col[:, C_B1 + e * HT0 + t:C_B1 + e * HT0 + t + 1], scale=unscl[:, 0:1]).then_inc(s_h, 1)
                    after(a, s_h, c, NE * HT0, (e + 1 - NE) * HT0)
                    after(a, s_y, c, NE + 1, e - NE - 1)
                    a.activation(hp16[k][0], hs[k][:, :, :], ACT.Identity, scale=scl[:, 3:4]).then_inc(s_hh, 1)

                if B:
                    after(a, s_T, b)
                    after(a, s_gnn, b - 1)
                    a.copy(xaT[:, :, :], ps[2][:, :].rearrange("p (k n) -> p k n", k=2 * KD)).then_inc(s_aggT, 1)
                if C:
                    gelu(0)
                    gelu(1)
                    gelu(2)
                    gelu(3)
                if B:
                    after(a, s_xnTp, b)
                    if Dd:
                        after(a, s_dTp, d)
                    after(a, s_lgp, b - 2)
                    after(a, s_xl, b - 2)
                    for k in range(KD):
                        a.activation(xnT[b.par][:, k, :], ps[2][:, k * P:(k + 1) * P], ACT.Identity,
                                     bias=col[:, C_BETA + k:C_BETA + k + 1], scale=col[:, C_GAMMA + k:C_GAMMA + k + 1]).then_inc(s_xnT, 1)
                    after(a, s_xnT, b, KD)
                    after(a, s_hps, b - 2, NE)
                    a.activation(xs[b.par][0], xnT[b.par][:, :, :], ACT.Identity, scale=scl[:, 2:3]).then_inc(s_xh, 1)
                if Dd:
                    after(a, s_dTp, d)
                    after(a, s_hj, d - 1)
                    a.copy(xndT, ps[2][:, D:2 * D].rearrange("p (k n) -> p k n", k=KD)).then_inc(s_dT, 1)
                if C:
                    gelu(4)
                if Dd:
                    after(a, s_hj, d)
                    landed(a, s_htst, d - 2)
                    after(a, s_hq, d - 2)
                    a.activation(hT[d.par][:, :], ps[1 - at.par][:, D:D + P], ACT.Relu, bias=col[:, C_BP:C_BP + 1]).then_inc(s_hT, 1)
                if B:
                    after(a, s_dl, b)
                    after(a, s_exs, b - 1)
                    a.activation(ex[:, :], dif[:, :], ACT.Tanh).then_inc(s_ex, 1)
                if C:
                    gelu(5)
                    gelu(6)
                if B:
                    after(a, s_wfTp, b)
                    after(a, s_y, b - 1, NE + 1, -NE)
                    a.copy(wfT[:, :], ps[4][0:NE, D + NE:D + NE + P]).then_inc(s_wfT, 1)
                if Dd:
                    after(a, s_hpT, d)
                    landed(a, s_hpst, d - 2)
                    a.copy(hp_s[d.par][:, :], ps[1 - at.par][:, D + P:D + 2 * P]).then_inc(s_hp, 1)
                if C:
                    gelu(7)
            drive(a, body, S0)

            def body1(at):
                B, C = has(at, 1), has(at, 2)
                b, c = at - 1, at - 2
                if B:
                    after(a, u_agg, b)
                    a.activation(agg_s[:, PJ:2 * PJ], agg_s[:, 0:PJ], ACT.Sqrt).then_inc(u_sq, 1)
                    after(a, u_sqTp, b)
                    after(a, u_gnn, b - 1)
                    a.copy(xaT[:, 0, :], ps[2][:, 0:P]).then_inc(u_sqT, 1)
                    after(a, u_iv, b)
                    after(a, u_xn, b - 1)
                    a.activation(rb[:, :], sm[:, 1:2], ACT.Sqrt).then_inc(u_r, 1)
                if C:
                    for t in range(HT1):
                        after(a, u_hps, c, 2, t // HT0 - 1)
                        after(a, u_y, c - 1)
                        a.activation(hs[t // HT0][:, t % HT0, :], ps[5 + t // HT0][:, t % HT0 * P:(t % HT0 + 1) * P], ACT.Gelu_apprx_tanh,
                                     bias=col[:, C_FB1 + t:C_FB1 + t + 1]).then_inc(u_h, 1)
                if B:
                    after(a, u_xnTp, b)
                    after(a, u_hps, b - 2, 2)
                    a.copy(xnT[b.par][:, :, :], ps[2][:, 0:D].rearrange("p (k n) -> p k n", k=KD)).then_inc(u_xnT, 1)
            drive(a, body1, S1)

        @block.tensor
        def _(t):
            t.wait_ge(s_const, 11)
            t.wait_ge(s_cnt, 3)
            t.matmul(ps[0][0:NB, 0:1], cnt[:, 0:NB], ones[:, 0:1], start=True, stop=True)
            t.matmul(ps[0][0:NB, 1:2], cnt[:, 1:NB + 1], ones[:, 0:1], start=True, stop=True).then_inc(s_cntp, 1)
            t.wait_ge(s_row, 8)
            for k in range(WROWS - FIXED):
                t.matmul(ps[1][0:1, 0:NB], edged[:, k:k + 1], ident[0:NB, 0:NB], start=(k == 0), stop=(k == 1))
            for k in range(WROWS - FIXED):
                last = t.matmul(ps[1][0:1, (k + 1) * P:(k + 1) * P + NB], edged[:, k:k + 1], to_here, start=True, stop=True)
            last.then_inc(s_cntp, 1)
            t.wait_ge(s_flag, 5)
            t.matmul(ps[0][:, 2:3], ones[:, :], bad[:, 2:3], start=True, stop=True).then_inc(s_flagp, 1)
            t.wait_ge(s_flag, 7)
            t.wait_ge(s_winf, 2)
            for g, (k, js) in enumerate(BANKS):
                if g == DST_BANKS:
                    t.wait_ge(s_srcf, 1)
                if g >= 8:
                    t.wait_ge(s_tab, g - 7)
                w = (winf[0], winf[1], win[:, :, 2 * P:3 * P].bitcast(f32))[k]
                for n, j in enumerate(js):
                    last = t.transpose(ps[g % 8][:, n * NB:(n + 1) * NB], w[:, j, :], ident[0:NB, 0:NB])
                last.then_inc(s_tp, 1)
            tables_done(t)
            t.wait_ge(s_par, 16 * 8)
            t.wait_ge(s_sq, 5)
            t.matmul(ps[7][:, 0:5], ones[:, :], sq[:, :], start=True, stop=True).then_inc(s_sqp, 1)
            flag = flagged(t)

            def general(layer):
                width = (D, PJ)[layer]
                with t.If(flag == 1):
                    with t.Fori(0, ER) as r:
                        t.wait_ge(k_v, r * KV + KV * (ER * layer + 1) - 1)
                        t.wait_ge(k_gather, r * 16 + 16 * (ER * layer + 1))
                        if layer:
                            t.matmul(ps[0][:, 0:width], k_wgt, k_got[:, 0:width], start=True, stop=True).then_inc(k_sum, 1)
                        else:
                            t.matmul(ps[0][:, 0:D], k_wgt16, k_got16[:, 0:D], start=True, stop=False)
                            t.matmul(ps[0][:, 0:D], k_wgt16, k_got16[:, D:2 * D], start=False, stop=True).then_inc(k_sum, 1)
                t.sem_inc(go_t)

            general(0)

            def body(at):
                A, B, C, Dd = has(at, 0), has(at, 1), has(at, 2), has(at, 3)
                b, c, d = at - 1, at - 2, at - 3

                def sums(g):
                    if g == 0:
                        after(t, s_agg, at - 2)
                        after(t, s_hp, at - 4)
                    after(t, s_oh, at, GRP, g + 1 - GRP)
                    for j in GROUP[g]:
                        t.wait_ge(g_in[j], at.times(16, 16))
                        t.matmul(ps[at.par][:, 0:D], oh16[at.par][:, j, :], gb16[:, j, 0:D], start=(j == 0), stop=False)
                        t.matmul(ps[at.par][:, 0:D], oh16[at.par][:, j, :], gb16[:, j, D:2 * D], start=False, stop=(j == WROWS - 1)).then_inc(s_sum, 1)

                PARTS = ((0, 0), (0, 1), (1, 0))

                def hidden(e):
                    k = e % 2
                    after(t, s_h, c, NE * HT0, (e - 1 - NE) * HT0)
                    if e == 0:
                        after(t, s_xl, c)
                        after(t, s_wlo, At(None, 0), WCH)
                    for h in range(HT0):
                        for kk in range(KD):
                            for n, (wl, xl) in enumerate(PARTS):
                                last = t.matmul(ps[5 + k][:, h * P:(h + 1) * P], w1s[e][wl][:, kk, h * P:(h + 1) * P], xs[c.par][xl][:, kk, :],
                                                start=(kk == 0 and n == 0), stop=(kk == KD - 1 and n == 2))
                    last.then_inc(s_hps, 1)

                def y(e):
                    yp = ps[(3, 7)[(e + 1) % 2]][:, 0:D]
                    after(t, s_acc, c, NE + 1, max(e, 0) - 1 - NE)
                    if e < 0:
                        after(t, s_wfT, c)
                        t.matmul(yp, wfT[:, :], b2e_s[:, :], start=True, stop=True).then_inc(s_y, 1)
                        return
                    after(t, s_hl, c, NE, e + 1 - NE)
                    for h in range(HT0):
                        for n, (wl, hl) in enumerate(PARTS):
                            last = t.matmul(yp, hp16[e % 2][hl][:, h, :], w2s[e][wl][:, h, :], start=(h == 0 and n == 0), stop=(h == HT0 - 1 and n == 2))
                    last.then_inc(s_y, 1)

                if B:
                    after(t, s_xnT, b - 1, KD)
                    after(t, s_dT, d - 1)
                    landed(t, s_xb, b, 32)
                    for k in range(KD):
                        for low in range(2):
                            t.matmul(ps[2][:, k * P:(k + 1) * P], xnb[b.par][:, low * D + k * P:low * D + (k + 1) * P], ident16[:, :],
                                     start=(low == 0), stop=(low == 1))
                    after(t, s_agg, b)
                    for k in range(KD):
                        last = t.transpose(ps[2][:, D + k * P:D + (k + 1) * P], agg_s[:, k * P:(k + 1) * P], ident[:, :])
                    last.then_inc(s_T, 1)
                if C:
                    hidden(0)
                    y(-1)
                if B:
                    after(t, s_aggT, b)
                    after(t, s_wfT, b - 1)
                    for k in range(2 * KD):
                        last = t.matmul(ps[4][:, 0:D], xaT[:, k, :], gw0_s[:, k % KD, k // KD * D:k // KD * D + D],
                                        start=(k == 0), stop=(k == 2 * KD - 1))
                    last.then_inc(s_gnn, 1)
                if C:
                    hidden(1)
                    hidden(2)
                    y(0)
                    hidden(3)
                    y(1)
                    hidden(4)
                if B:
                    after(t, s_xn, b)
                    for k in range(KD):
                        last = t.transpose(ps[2][:, k * P:(k + 1) * P], xn[:, k * P:(k + 1) * P], ident[:, :])
                    last.then_inc(s_xnTp, 1)
                if Dd:
                    after(t, s_dn, d)
                    if not B:
                        after(t, s_dT, d - 1)
                    for k in range(KD):
                        last = t.transpose(ps[2][:, D + k * P:D + (k + 1) * P], xnd[:, k * P:(k + 1) * P], ident[:, :])
                    last.then_inc(s_dTp, 1)
                if C:
                    y(2)
                    hidden(5)
                if B:
                    after(t, s_xnT, b, KD)
                    after(t, s_x0, b)
                    for k in range(KD):
                        last = t.matmul(ps[4][:, D:D + NE], xnT[b.par][:, k, :], col[:, C_WR0 + k * NE:C_WR0 + (k + 1) * NE],
                                        start=(k == 0), stop=(k == KD - 1))
                    last.then_inc(s_lgp, 1)
                if Dd:
                    after(t, s_dT, d)
                    if B:
                        after(t, s_agg, b)
                    after(t, s_hp, d - 1)
                    for k in range(KD):
                        last = t.matmul(ps[1 - at.par][:, D:D + P], wp_s[:, k, :], xndT[:, k, :], start=(k == 0), stop=(k == KD - 1))
                    last.then_inc(s_hj, 1)
                if C:
                    y(3)
                if A:
                    sums(0)
                if C:
                    hidden(6)
                    y(4)
                if B:
                    after(t, s_wf, b, 2, -1)
                    t.transpose(ps[4][0:NE, D + NE:D + NE + P], wf[b.par][:, :], ident[:, :]).then_inc(s_wfTp, 1)
                if Dd:
                    after(t, s_hq, d)
                    t.transpose(ps[1 - at.par][:, D + P:D + 2 * P], hq, ident[:, :]).then_inc(s_hpT, 1)
                if C:
                    hidden(7)
                    y(5)
                    y(6)
                if A:
                    sums(1)
                if C:
                    y(7)
            drive(t, body, S0)

            t.wait_ge(s_brow, 1)
            t.wait_ge(s_row, 10)
            general(1)

            def body1(at):
                A, B, C = has(at, 0), has(at, 1), has(at, 2)
                b, c = at - 1, at - 2

                def sums(g):
                    if g == 0:
                        after(t, u_agg, at - 2)
                    after(t, u_oh, at, GRP, g + 1 - GRP)
                    for j in GROUP[g]:
                        if j < FIXED:
                            t.wait_ge(g_in[j], at.times(16, 16 * (NB + 1)))
                        else:
                            so_far = t.value_load(extra_i[0:1, 1 + j - FIXED, bass.ds(at.times(1), 1)], min_val=16 * (NB + 1), max_val=32 * NB)
                            t.wait_ge(g_in[j], so_far)
                        t.matmul(ps[at.par][:, 0:PJ], oh[at.par][:, j, :], gbuf[:, j, 0:PJ], start=(j == 0), stop=(j == WROWS - 1)).then_inc(u_sum, 1)

                if A:
                    sums(0)
                if B:
                    after(t, u_sq, b)
                    after(t, u_xnT, b - 1)
                    t.transpose(ps[2][:, 0:P], agg_s[:, PJ:2 * PJ], ident[:, :]).then_inc(u_sqTp, 1)
                if A:
                    sums(1)
                if B:
                    after(t, u_sqT, b)
                    landed(t, u_in, b, 32)
                    after(t, u_wc, b - 1)
                    t.matmul(ps[4][:, 0:D], hT[b.par][:, :], gw1_s[:, 0, :], start=True, stop=False)
                    t.matmul(ps[4][:, 0:D], xaT[:, 0, :], gw1_s[:, 1, :], start=False, stop=False)
                    t.matmul(ps[4][:, 0:D], ones[0:1, :], brow[:, :], start=False, stop=True).then_inc(u_gnn, 1)
                if C:
                    for h in range(HT1):
                        if h % HT0 == 0:
                            after(t, u_h, c - 1, HT1, h + HT0 - HT1)
                        if h == 0:
                            after(t, u_xnT, c)
                        for k in range(KD):
                            last = t.matmul(ps[5 + h // HT0][:, h % HT0 * P:(h % HT0 + 1) * P], wf1_s[:, k, h * P:(h + 1) * P], xnT[c.par][:, k, :],
                                            start=(k == 0), stop=(k == KD - 1))
                        if h % HT0 == HT0 - 1:
                            last.then_inc(u_hps, 1)
                if B:
                    after(t, u_xn, b)
                    for k in range(KD):
                        last = t.transpose(ps[2][:, k * P:(k + 1) * P], xn[:, k * P:(k + 1) * P], ident[:, :])
                    last.then_inc(u_xnTp, 1)
                if C:
                    yp = ps[(3, 7)[c.par]][:, 0:D]
                    after(t, u_yw, c - 2)
                    t.matmul(yp, ones[0:1, :], fb2row, start=True, stop=False)
                    for h in range(HT1):
                        after(t, u_h, c, HT1, h + 1 - HT1)
                        last = t.matmul(yp, hs[h // HT0][:, h % HT0, :], wf2_s[:, h, :], start=False, stop=(h == HT1 - 1))
                    last.then_inc(u_y, 1)
                if B:
                    after(t, u_xnT, b)
                    after(t, u_x2, b)
                    for k in range(KD):
                        last = t.matmul(ps[4][:, D:D + 1], xnT[b.par][:, k, :], col[:, C_WR1 + k:C_WR1 + k + 1], start=(k == 0), stop=(k == KD - 1))
                    last.then_inc(u_wp, 1)
            drive(t, body1, S1)

            t.wait_ge(u_agg, NB)
            with t.Fori(0, 2 * (DIGITS + 1)) as i:
                t.wait_ge(f_cnt, i + 1)
                t.matmul(ps[0][:, 0:RADIX - 1], ones[:, :], count[:, :], start=True, stop=True).then_inc(f_tot, 1)
            t.wait_ge(f_cnt, 2 * (DIGITS + 1) + 1)
            t.matmul(ps[0][:, 0:NB], low_tri, equal, start=True, stop=True)
            t.matmul(ps[0][:, P:P + NB], ones[:, :], equal, start=True, stop=True).then_inc(f_tot, 1)


def kernel(x, src, dst, edge_weight, L0_gnn_W1, L0_gnn_W2, L0_ffn_gamma, L0_ffn_beta, L0_ffn_Wr, L0_ffn_br, L0_ffn_W1,
           L0_ffn_b1, L0_ffn_W2, L0_ffn_b2, L1_gnn_Wp, L1_gnn_bp, L1_gnn_W1, L1_gnn_b1, L1_gnn_W2, L1_gnn_b2,
           L1_ffn_attention_mask, L1_ffn_wr, L1_ffn_br, L1_ffn_w1, L1_ffn_b1, L1_ffn_w2, L1_ffn_b2):
    import concourse.bacc as bacc
    from concourse.bass_utils import run_bass_kernel_spmd

    a = np.asarray
    xpad = np.concatenate([a(x), np.zeros((NB * P - N, D), np.float32)])
    pad = ER * P - E

    def edge_rows(v, fill):
        return np.concatenate([a(v), np.full(pad, fill, a(v).dtype)]).reshape(ER, P)

    dst_r = edge_rows(dst, 1 << 20)
    flat = dst_r.reshape(P, ER)
    dstrun = np.concatenate([flat, np.append(flat[1:, 0], flat[-1, -1])[:, None].astype(flat.dtype)], 1)
    edges = np.concatenate([edge_rows(src, 0), dst_r, edge_rows(edge_weight, 0).view(np.int32)], 1)
    cols = np.concatenate([
        a(L0_ffn_b1).reshape(NE * HT0, P).T, a(L0_ffn_gamma).reshape(KD, P).T, a(L0_ffn_beta).reshape(KD, P).T,
        a(L1_gnn_bp).reshape(1, P).T, a(L1_ffn_b1).reshape(HT1, P).T,
        a(L0_ffn_Wr).reshape(KD, P, NE).transpose(1, 0, 2).reshape(P, KD * NE), a(L1_ffn_wr).reshape(KD, P).T], 1)
    rows = np.concatenate([a(L0_ffn_br), a(L1_ffn_br), a(L1_gnn_b1), a(L1_gnn_b2), a(L1_ffn_b2)])[None]
    ins = dict(
        xpad=xpad, edges=edges, firsts=dst_r[:, 0].reshape(P, CC), dstrun=dstrun, wmoe1=a(L0_ffn_W1), wmoe2=a(L0_ffn_W2),
        gw0=np.concatenate([a(L0_gnn_W1).T, a(L0_gnn_W2).T], 1), wp=a(L1_gnn_Wp).T,
        gw1=np.concatenate([a(L1_gnn_W1).T, a(L1_gnn_W2).T], 0), wf1=a(L1_ffn_w1), wf2=a(L1_ffn_w2), b2e=a(L0_ffn_b2),
        cols=cols, rows=rows)
    ins = {k: np.ascontiguousarray(v) for k, v in ins.items()}
    nc = bacc.Bacc("TRN2", target_bir_lowering=False, num_devices=1)
    aps = {k: nc.dram_tensor("in_" + k, v.shape, mybir.dt.from_np(v.dtype), kind="ExternalInput").ap() for k, v in ins.items()}
    out = nc.dram_tensor("out_0", (NB * P, D), f32, kind="ExternalOutput").ap()
    gnn_kernel(nc, **aps, out=out)
    r = run_bass_kernel_spmd(nc, [{"in_" + k: v for k, v in ins.items()}], core_ids=[0])
    return r.results[0]["out_0"][:N]
```
